# Optimizing a Trainium2 kernel written in Bass

```python
import numpy as np
import jax
import jax.numpy as jnp

def _softmax(x, axis=-1):
    return jax.nn.softmax(x, axis=axis)

def _gelu(x):
    return jax.nn.gelu(x, approximate=True)

def _silu(x):
    return jax.nn.silu(x)

def _sigmoid(x):
    return jax.nn.sigmoid(x)

def _layernorm(x, axis=-1, eps=1e-05):
    m = jnp.mean(x, axis=axis, keepdims=True)
    v = jnp.var(x, axis=axis, keepdims=True)
    return (x - m) / jnp.sqrt(v + eps)

def _scatter_add(tgt, idx, src, axis=0):
    return tgt.at[idx].add(src)

def _segment_sum(src, seg, n):
    return jax.ops.segment_sum(src, seg, n)
kernel_name = 'mk_gnn_ffn_d2_gnn_r16_5cc8e7'

def setup_inputs(seed: int=0):
    np.random.seed(seed)
    _w = jnp.asarray

    def _rec_inputs():
        import jax
        import jax.numpy as jnp
        _gk = jax.random.key(seed)
        x = -0.0002117 + 1 * jax.random.normal(jax.random.fold_in(_gk, 1), (6250, 256), jnp.float32)
        src = jax.random.randint(jax.random.fold_in(_gk, 2), (100000,), 0, 6250, jnp.int32)
        dst = jax.random.randint(jax.random.fold_in(_gk, 3), (100000,), 0, 6250, jnp.int32)
        _o = jnp.argsort(dst, stable=True)
        src = src[_o]
        dst = dst[_o]
        edge_type_8 = jax.random.randint(jax.random.fold_in(_gk, 12), (100000,), 0, 8, jnp.int32)
        edge_weight = jax.random.uniform(jax.random.fold_in(_gk, 13), (100000,), jnp.float32, 0.0, 0.999999)
        return (x, src, dst, edge_type_8, edge_weight)
    x, src, dst, edge_type_8, edge_weight = _rec_inputs()

    def _L0_gnn_setup():
        import jax, jax.numpy as jnp
        import numpy as np
        N_NODES = 6250
        N_EDGES = 100000
        D = 256
        key = jax.random.key(seed)
        ks = jax.random.split(key, 8)
        h6_all = jax.random.normal(ks[0], (N_NODES, D), dtype=jnp.float32)
        edge_index = jax.random.randint(ks[1], (2, N_EDGES), 0, N_NODES, dtype=jnp.int64)
        edge_weight = jax.random.uniform(ks[2], (N_EDGES,), dtype=jnp.float32)
        s = 1.0 / np.sqrt(D)
        W = jax.random.normal(ks[3], (D, D), dtype=jnp.float32) * s
        b = jnp.zeros((D,), dtype=jnp.float32)
        W1 = jax.random.normal(ks[4], (D, D), dtype=jnp.float32) * s
        b1 = jnp.zeros((D,), dtype=jnp.float32)
        W2 = jax.random.normal(ks[5], (D, D), dtype=jnp.float32) * s
        b2 = jnp.zeros((D,), dtype=jnp.float32)
        return {'h6_all': h6_all, 'edge_index': edge_index, 'edge_weight': edge_weight, 'W': W, 'b': b, 'W1': W1, 'b1': b1, 'W2': W2, 'b2': b2}
    _L0_gnn_all = _L0_gnn_setup()
    _L0_gnn_in = {k: v for k, v in _L0_gnn_all.items() if k in ('W', 'b', 'W1', 'b1', 'W2', 'b2')}
    del _L0_gnn_all

    def _L0_ffn_setup():
        import jax, jax.numpy as jnp
        import numpy as np
        NUM_EXPERTS = 8
        TOP_K = 2
        B, S, D = (8, 512, 256)

        def _moe(tokens, router_w, w1, b1, w2, b2):
            N = tokens.shape[0]
            E = router_w.shape[0]
            logits = tokens.astype(jnp.float32) @ router_w.astype(jnp.float32).T
            probs = jax.nn.softmax(logits, axis=-1)
            rw, re = jax.lax.top_k(probs, TOP_K)
            if TOP_K > 1:
                rw = rw / jnp.maximum(rw.sum(-1, keepdims=True), 1e-12)
            rw = rw.astype(tokens.dtype)
            combine = jnp.zeros((N, E), tokens.dtype).at[jnp.arange(N)[:, None], re].set(rw)
            out = tokens
            for e in range(E):
                h = jax.nn.gelu(tokens @ w1[e] + b1[e], approximate=False)
                y = h @ w2[e] + b2[e]
                out = out + combine[:, e:e + 1] * y
            return out
        key = jax.random.key(seed)
        ks = jax.random.split(key, 4)
        scale = 1.0 / np.sqrt(D).astype(np.float32)
        return {'input_embeddings': jax.random.normal(ks[0], (B, S, D), jnp.float32), 'router_w': jax.random.normal(ks[1], (NUM_EXPERTS, D), jnp.float32) * scale, 'w1': jax.random.normal(ks[2], (NUM_EXPERTS, D, D), jnp.float32) * scale, 'b1': jnp.zeros((NUM_EXPERTS, D), jnp.float32), 'w2': jax.random.normal(ks[3], (NUM_EXPERTS, D, D), jnp.float32) * scale, 'b2': jnp.zeros((NUM_EXPERTS, D), jnp.float32)}
    _L0_ffn_all = _L0_ffn_setup()
    _L0_ffn_in = {k: v for k, v in _L0_ffn_all.items() if k in ('router_w', 'w1', 'b1', 'w2', 'b2')}
    del _L0_ffn_all

    def _L1_gnn_setup():
        import jax, jax.numpy as jnp
        import numpy as np
        N_NODES = 3125
        N_EDGES = 50000
        IN_FEAT = 256
        OUT_FEAT = 256
        NUM_RELS = 8
        ALPHA = 0.5
        key = jax.random.key(seed)
        k1, k2, k3, k4, k5, k6 = jax.random.split(key, 6)
        x = jax.random.normal(k1, (N_NODES, IN_FEAT), dtype=jnp.float32)
        edge_index = jax.random.randint(k2, (2, N_EDGES), 0, N_NODES, dtype=jnp.int64)
        edge_type = jax.random.randint(k3, (N_EDGES,), 0, NUM_RELS, dtype=jnp.int64)
        gain = float(np.sqrt(2.0))
        lim_w = gain * float(np.sqrt(6.0 / (IN_FEAT + OUT_FEAT)))
        weight = jax.random.uniform(k4, (NUM_RELS, IN_FEAT, OUT_FEAT), dtype=jnp.float32, minval=-lim_w, maxval=lim_w)
        loop_weight = jax.random.uniform(k5, (IN_FEAT, OUT_FEAT), dtype=jnp.float32, minval=-lim_w, maxval=lim_w)
        h_bias = jnp.zeros((OUT_FEAT,), dtype=jnp.float32)
        return {'edge_index': edge_index, 'x': x, 'edge_type': edge_type, 'weight': weight, 'h_bias': h_bias, 'loop_weight': loop_weight}
    _L1_gnn_all = _L1_gnn_setup()
    _L1_gnn_in = {k: v for k, v in _L1_gnn_all.items() if k in ('weight', 'h_bias', 'loop_weight')}
    del _L1_gnn_all

    def _L1_ffn_setup():
        import jax, jax.numpy as jnp
        import numpy as np
        E, D, H, TOP_K = (6, 256, 256, 2)
        ROUTER_H = D // 2
        key = jax.random.key(seed)
        ks = jax.random.split(key, 12)
        s = 1.0 / np.sqrt(D)
        sh = 1.0 / np.sqrt(H)
        sr = 1.0 / np.sqrt(ROUTER_H)
        return {'features': jax.random.normal(ks[0], (8, 256, D), dtype=jnp.float32), 'router_w1': jax.random.uniform(ks[1], (D, ROUTER_H), jnp.float32, -s, s), 'router_b1': jnp.zeros((ROUTER_H,), jnp.float32), 'router_w2': jax.random.uniform(ks[2], (ROUTER_H, E), jnp.float32, -sr, sr), 'router_b2': jnp.zeros((E,), jnp.float32), 'expert_w1': jax.random.uniform(ks[3], (E, D, H), jnp.float32, -s, s), 'expert_b1': jnp.zeros((E, H), jnp.float32), 'expert_w2': jax.random.uniform(ks[4], (E, H, H), jnp.float32, -sh, sh), 'expert_b2': jnp.zeros((E, H), jnp.float32), 'expert_w3': jax.random.uniform(ks[5], (E, H, D), jnp.float32, -sh, sh), 'expert_b3': jnp.zeros((E, D), jnp.float32)}
    _L1_ffn_all = _L1_ffn_setup()
    _L1_ffn_in = {k: v for k, v in _L1_ffn_all.items() if k in ('router_w1', 'router_b1', 'router_w2', 'router_b2', 'expert_w1', 'expert_b1', 'expert_w2', 'expert_b2', 'expert_w3', 'expert_b3')}
    del _L1_ffn_all
    return {'x': x, 'src': src, 'dst': dst, 'edge_type_8': edge_type_8, 'edge_weight': edge_weight, 'L0_gnn_W': _L0_gnn_in['W'], 'L0_gnn_b': _L0_gnn_in['b'], 'L0_gnn_W1': _L0_gnn_in['W1'], 'L0_gnn_b1': _L0_gnn_in['b1'], 'L0_gnn_W2': _L0_gnn_in['W2'], 'L0_gnn_b2': _L0_gnn_in['b2'], 'L0_ffn_router_w': _L0_ffn_in['router_w'], 'L0_ffn_w1': _L0_ffn_in['w1'], 'L0_ffn_b1': _L0_ffn_in['b1'], 'L0_ffn_w2': _L0_ffn_in['w2'], 'L0_ffn_b2': _L0_ffn_in['b2'], 'L1_gnn_weight': _L1_gnn_in['weight'], 'L1_gnn_h_bias': _L1_gnn_in['h_bias'], 'L1_gnn_loop_weight': _L1_gnn_in['loop_weight'], 'L1_ffn_router_w1': _L1_ffn_in['router_w1'], 'L1_ffn_router_b1': _L1_ffn_in['router_b1'], 'L1_ffn_router_w2': _L1_ffn_in['router_w2'], 'L1_ffn_router_b2': _L1_ffn_in['router_b2'], 'L1_ffn_expert_w1': _L1_ffn_in['expert_w1'], 'L1_ffn_expert_b1': _L1_ffn_in['expert_b1'], 'L1_ffn_expert_w2': _L1_ffn_in['expert_w2'], 'L1_ffn_expert_b2': _L1_ffn_in['expert_b2'], 'L1_ffn_expert_w3': _L1_ffn_in['expert_w3'], 'L1_ffn_expert_b3': _L1_ffn_in['expert_b3']}

def reference(x, src, dst, edge_type_8, edge_weight, L0_gnn_W, L0_gnn_b, L0_gnn_W1, L0_gnn_b1, L0_gnn_W2, L0_gnn_b2, L0_ffn_router_w, L0_ffn_w1, L0_ffn_b1, L0_ffn_w2, L0_ffn_b2, L1_gnn_weight, L1_gnn_h_bias, L1_gnn_loop_weight, L1_ffn_router_w1, L1_ffn_router_b1, L1_ffn_router_w2, L1_ffn_router_b2, L1_ffn_expert_w1, L1_ffn_expert_b1, L1_ffn_expert_w2, L1_ffn_expert_b2, L1_ffn_expert_w3, L1_ffn_expert_b3):
    import jax
    import jax.numpy as jnp

    def _L0_gnn_ref(h6_all, edge_index, edge_weight, W, b, W1, b1, W2, b2):
        import jax, jax.numpy as jnp
        import numpy as np
        N_NODES = 6250
        N_EDGES = 100000
        D = 256
        'GCNConv(256->256, weighted, self-loops, symmetric norm) + 2-layer MLP head.'
        N = h6_all.shape[0]
        row, col = (edge_index[0], edge_index[1])
        sl = jnp.arange(N, dtype=edge_index.dtype)
        row_sl = jnp.concatenate([row, sl])
        col_sl = jnp.concatenate([col, sl])
        ew_sl = jnp.concatenate([edge_weight, jnp.ones((N,), dtype=edge_weight.dtype)])
        deg = jax.ops.segment_sum(ew_sl, row_sl, num_segments=N)
        dinv = jnp.where(deg > 0, jax.lax.rsqrt(deg), 0.0)
        norm = dinv[row_sl] * ew_sl * dinv[col_sl]
        xw = h6_all @ W
        msgs = xw[col_sl] * norm[:, None]
        h7 = jax.ops.segment_sum(msgs, row_sl, num_segments=N) + b
        h = jax.nn.relu(h7 @ W1 + b1)
        out = h @ W2 + b2
        return out

    def _L0_ffn_ref(input_embeddings, router_w, w1, b1, w2, b2):
        import jax, jax.numpy as jnp
        import numpy as np
        NUM_EXPERTS = 8
        TOP_K = 2
        B, S, D = (8, 512, 256)

        def _moe(tokens, router_w, w1, b1, w2, b2):
            N = tokens.shape[0]
            E = router_w.shape[0]
            logits = tokens.astype(jnp.float32) @ router_w.astype(jnp.float32).T
            probs = jax.nn.softmax(logits, axis=-1)
            rw, re = jax.lax.top_k(probs, TOP_K)
            if TOP_K > 1:
                rw = rw / jnp.maximum(rw.sum(-1, keepdims=True), 1e-12)
            rw = rw.astype(tokens.dtype)
            combine = jnp.zeros((N, E), tokens.dtype).at[jnp.arange(N)[:, None], re].set(rw)
            out = tokens
            for e in range(E):
                h = jax.nn.gelu(tokens @ w1[e] + b1[e], approximate=False)
                y = h @ w2[e] + b2[e]
                out = out + combine[:, e:e + 1] * y
            return out
        b, s, d = input_embeddings.shape
        tokens = input_embeddings.reshape(b * s, d)
        return _moe(tokens, router_w, w1, b1, w2, b2).reshape(b, s, d)

    def _L1_gnn_ref(edge_index, x, edge_type, weight, h_bias, loop_weight):
        import jax, jax.numpy as jnp
        import numpy as np
        N_NODES = 3125
        N_EDGES = 50000
        IN_FEAT = 256
        OUT_FEAT = 256
        NUM_RELS = 8
        ALPHA = 0.5
        num_nodes = x.shape[0]
        src, dst = (edge_index[0], edge_index[1])
        hx = jnp.einsum('ni,rio->rno', x, weight)
        msg = hx[edge_type, src]
        agg = jax.ops.segment_sum(msg, dst, num_segments=num_nodes)
        node_repr = agg * jnp.asarray(ALPHA, x.dtype) ** 0.5
        node_repr = node_repr + h_bias
        loop_message = x @ loop_weight
        node_repr = node_repr + loop_message * jnp.asarray(1.0 - ALPHA, x.dtype) ** 0.5
        return node_repr

    def _L1_ffn_ref(features, router_w1, router_b1, router_w2, router_b2, expert_w1, expert_b1, expert_w2, expert_b2, expert_w3, expert_b3):
        import jax, jax.numpy as jnp
        import numpy as np
        E, D, H, TOP_K = (6, 256, 256, 2)
        ROUTER_H = D // 2
        rh = jax.nn.relu(features @ router_w1 + router_b1)
        expert_logits = jax.nn.softmax(rh @ router_w2 + router_b2, axis=-1)
        top_w, top_i = jax.lax.top_k(expert_logits, TOP_K)
        routing_weights = jax.nn.softmax(top_w, axis=-1)
        h1 = jax.nn.relu(jnp.einsum('bsd,edh->bseh', features, expert_w1) + expert_b1)
        h2 = jax.nn.relu(jnp.einsum('bseh,ehf->bsef', h1, expert_w2) + expert_b2)
        expert_out = jnp.einsum('bsef,efo->bseo', h2, expert_w3) + expert_b3
        sel = jnp.take_along_axis(expert_out, top_i[:, :, :, None], axis=2)
        combined = jnp.sum(sel * routing_weights[..., None], axis=2)
        return combined
    edge_index = jnp.stack([src, dst])
    x = x + _L0_gnn_ref(_layernorm(x, axis=-1), edge_index, edge_weight, L0_gnn_W, L0_gnn_b, L0_gnn_W1, L0_gnn_b1, L0_gnn_W2, L0_gnn_b2)
    x = x + _L0_ffn_ref(_layernorm(x, axis=-1)[None], L0_ffn_router_w, L0_ffn_w1, L0_ffn_b1, L0_ffn_w2, L0_ffn_b2)[0]
    x = x + _L1_gnn_ref(edge_index, _layernorm(x, axis=-1), edge_type_8, L1_gnn_weight, L1_gnn_h_bias, L1_gnn_loop_weight)
    x = x + _L1_ffn_ref(_layernorm(x, axis=-1)[None], L1_ffn_router_w1, L1_ffn_router_b1, L1_ffn_router_w2, L1_ffn_router_b2, L1_ffn_expert_w1, L1_ffn_expert_b1, L1_ffn_expert_w2, L1_ffn_expert_b2, L1_ffn_expert_w3, L1_ffn_expert_b3)[0]
    return x

_drawn_inputs = setup_inputs


def setup_inputs(seed=0):
    import zlib

    import numpy as np

    out = dict(_drawn_inputs(seed))
    spreads = {'L0_gnn_b': (0.0, 0.1),
     'L0_gnn_b1': (0.0, 0.1),
     'L0_gnn_b2': (0.0, 0.1),
     'L0_ffn_b1': (0.0, 0.308),
     'L0_ffn_b2': (0.0, 0.1),
     'L1_gnn_h_bias': (0.0, 0.362),
     'L1_ffn_router_b1': (0.0, 0.762),
     'L1_ffn_router_b2': (0.0, 0.8),
     'L1_ffn_expert_b1': (0.0, 0.8),
     'L1_ffn_expert_b2': (0.0, 0.8),
     'L1_ffn_expert_b3': (0.0, 0.549)}
    factors = {'L1_ffn_router_w1': 3.128,
     'L1_ffn_router_w2': 2.987,
     'L1_ffn_expert_w1': 5.264,
     'L1_ffn_expert_w2': 4.514,
     'L1_ffn_expert_w3': 3.427}
    for name, (base, spread) in spreads.items():
        noise = np.random.default_rng([zlib.crc32(name.encode()), seed]).standard_normal(out[name].shape)
        drawn = base * np.exp(spread * noise) if base else spread * noise
        out[name] = jnp.asarray(drawn.astype(out[name].dtype))
    for name, factor in factors.items():
        out[name] = (out[name] * factor).astype(out[name].dtype)
    return out
```

```python
import concourse.bass as bass
from concourse import mybir
from contextlib import ExitStack

f32 = mybir.dt.float32
i32 = mybir.dt.int32
u32 = mybir.dt.uint32
u8 = mybir.dt.uint8
ALU = mybir.AluOpType
ACT = mybir.ActivationFunctionType
AX = mybir.AxisListType.X
ds = bass.ds

N, D, E, P = 6250, 256, 100000, 128
B = -(-N // P)
NP = B * P
U = 4
T = 792
TG = 7
ROW = 264
BK = B + 1
R0, REL = 8, 8
E1 = 6
CB = 7
CN = CB * P
HN = CN // 2
NC = B // CB
BIG = 1024
EPS = 1e-5
DST, SRC = 0, 1
C_IOTA, C_ID, C_TRI, C_ONE, C_ZERO = 0, 128, 256, 384, 512
C_NODE, C_NEG, C_BLK, C_I8, C_REV, C_NEXT, C_N = 768, 817, 867, 917, 925, 932, 939
K_B, K_B1, K_F0, K_R1, K_X1, K_X2, K_N = 0, 2, 4, 20, 21, 33, 45
SQH = 0.5 ** 0.5


def build(nc, x, src_t, dst_t, type_t, weight_t, dst_rows, consts, shifted, bias_cols,
          gnn_w, gnn_w1, gnn_w2, gnn_b2, f0_router, f0_w1, f0_w2, f0_b2,
          rel_w, loop_w, h_bias, f1_rw1, f1_rw2, f1_rb2, f1_w1, f1_w2, f1_w3, f1_b3, out):
    ctx = ExitStack()
    with ctx:
        def sb(name, shape, dt=f32):
            return ctx.enter_context(nc.sbuf_tensor(name, shape, dt))

        def sem(name):
            return ctx.enter_context(nc.semaphore(name))

        def sems(name, n):
            return [sem(f"{name}{i}") for i in range(n)]

        msgs = nc.dram_tensor("msgs_sorted", [T * P, ROW], f32, kind="Internal").ap()
        hx = nc.dram_tensor("hx_rows", [NP * REL, D], f32, kind="Internal").ap()

        X = sb("X", [P, B, D])
        R1 = sb("R1", [P, B * D])
        R2 = sb("R2", [P, B * D])
        R3 = sb("R3", [P, 7168])
        C = sb("C", [P, C_N])
        GW = sb("GW", [P, 4 * 512])
        KC = sb("KC", [P, K_N])
        blk_shift = sb("blk_shift", [P, BK], i32)
        dstf = sb("dstf", [P, T])
        gidx = sb("gidx", [P, T], u32)
        blkD = sb("blkD", [P, T], i32)
        tab = sb("tab", [1, 6 * BK + 4], i32)
        stat6 = sb("stat6", [P, B, 6])
        mv = sb("mv", [P, B, 2])
        rstd = sb("rstd", [P, B])
        nmr = sb("nmr", [P, B])
        dinv = sb("dinv", [P, B])
        sc1 = sb("sc1", [P, B])
        sc2 = sb("sc2", [P, B])
        idx = sb("idx", [P, 8], u32)
        iota, ident, tri = C[:, C_IOTA:C_IOTA + P], C[:, C_ID:C_ID + P], C[:, C_TRI:C_TRI + P]
        ones, zeros = C[:, C_ONE:C_ONE + P], C[:, C_ZERO:C_ZERO + D]

        XS = R1[:, :].rearrange("p (b d) -> p b d", d=D)
        AG = R2[:, :].rearrange("p (b d) -> p b d", d=D)
        XT = R2[:, :].rearrange("p (k n) -> p k n", k=2)
        src_i = R1[:, 0:T].bitcast(i32)
        dst_i = R1[:, T:2 * T].bitcast(i32)
        typ_i = R1[:, 2 * T:3 * T].bitcast(i32)
        tmp_i = R1[:, 3 * T:4 * T].bitcast(i32)
        blkS = R1[:, 4 * T:5 * T]
        loS = R1[:, 5 * T:6 * T]
        pos1 = R1[:, 6 * T:7 * T]
        tmp_f = R1[:, 7 * T:8 * T]
        drow_i = R1[:, 8 * T:8 * T + TG * P].bitcast(i32)
        OHB = R2[:, 0:BK * T // 4].bitcast(u8).rearrange("p (b t) -> p b t", b=BK)
        o = BK * T // 4
        wts, srcf, pos_i = R2[:, o:o + T], R2[:, o + T:o + 2 * T], R2[:, o + 2 * T:o + 3 * T].bitcast(i32)
        WOH = R3[:, 0:8 * P].rearrange("p (s n) -> p s n", s=8)
        OHHI = R3[:, 1024:1024 + 2 * U * B].rearrange("p (h s n) -> p h s n", h=2, s=U)
        junk = R3[:, 1500:1500 + T]
        tot = R3[:, 2400:2400 + BK]
        cum = R3[:, 2450:2450 + BK]
        exc = R3[:, 2500:2500 + BK]
        base = R3[:, 2550:2550 + BK]
        tmn = R3[:, 2600:2600 + TG]
        tmx = R3[:, 2607:2607 + TG]
        tmn_i = R3[:, 2614:2614 + TG].bitcast(i32)
        tmx_i = R3[:, 2621:2621 + TG].bitcast(i32)
        ge = R3[:, 2640:2640 + B * TG].rearrange("p (b g) -> p b g", g=TG)
        le = R3[:, 3000:3000 + B * TG].rearrange("p (b g) -> p b g", g=TG)
        inb = R3[:, 3400:3400 + B * TG].rearrange("p (b g) -> p b g", g=TG)
        two = R3[:, 3800:3800 + 2 * B].rearrange("p (a b) -> p a b", a=2)
        ext = R3[0:B, 3900:3902]
        rowf = R3[0:1, 4000:4000 + 8 * BK].rearrange("p (a b) -> p a b", a=8)
        rowi = R3[0:1, 4500:4500 + 8 * BK].bitcast(i32).rearrange("p (a b) -> p a b", a=8)
        dst_bc = R3[:, 0:U * P].bitcast(i32).rearrange("p (s n) -> p s n", s=U)
        oneh = R3[:, 512:512 + U * P].rearrange("p (s n) -> p s n", s=U)
        msg = R3[:, 1024:1024 + U * ROW].rearrange("p (s n) -> p s n", s=U)
        TC = [R3[:, 1792 * i:1792 * (i + 1)].rearrange("p (k n) -> p k n", k=2) for i in range(3)]
        head_in = R3[:, 5376:5376 + CB * D].rearrange("p (s d) -> p s d", s=CB)
        xn = R3[:, 0:4 * D].rearrange("p (s d) -> p s d", s=4)
        xts = R3[:, 1024:1024 + CB * D].rearrange("p (s k n) -> p s k n", s=CB, k=2)
        hxs = R3[:, 2816:2816 + 2 * REL * D].rearrange("p (s n) -> p s n", s=2)
        rows_in = R3[:, 1024:1024 + U * D].rearrange("p (s d) -> p s d", s=U)
        def route(i):
            return R3[:, 2900 + 400 * i:2900 + 400 * i + B * 8].rearrange("p (b e) -> p b e", e=8)

        lg, pr, eq1, eq2, top = (route(i) for i in range(5))
        top_i = route(5).bitcast(u32)
        top_f = route(6)
        rmax, rsum = R3[:, 5800:5800 + B], R3[:, 5850:5850 + B]
        g12 = R3[:, 5900:5900 + 2 * B].rearrange("p (a b) -> p a b", a=2)
        comb_s = R3[0:8, 6100:6100 + CB * P].rearrange("p (s n) -> p s n", s=CB)
        HT = [R3[:, 2 * CN * i:2 * CN * (i + 1)].rearrange("p (k n) -> p k n", k=2) for i in range(4)]
        W0 = R1[:, 0:R0 * 1024].rearrange("p (e m k o) -> p e m k o", e=R0, m=2, k=2)
        WR = R1[:, R0 * 1024:R0 * 1024 + 2 * REL * D].rearrange("p (k n) -> p k n", k=2)
        W1 = R1[:, 0:E1 * 1536].rearrange("p (e m k o) -> p e m k o", e=E1, m=3, k=2)
        comb = sb("comb", [P, B, 8])
        HB = sb("HB", [P, D])
        RW = sb("RW", [P, 2, 8])
        RW1 = sb("RW1", [P, 2, P])
        RW2 = sb("RW2", [P, E1])
        brow = sb("brow", [8, 2 * D])
        srow = sb("srow", [1, D + 8])
        PS = ctx.enter_context(nc.psum_tensor("PS", [P, 8, 512], f32))
        PB = [PS[:, i, :] for i in range(8)]
        scanp = [PS[:, i:i + 2, :].rearrange("p a n -> p (a n)")[:, 0:T] for i in (3, 6)]
        aggp = PS[:, 6:8, :]
        zero_rows = R3[0:43, 4800:4800 + 8 * ROW]

        phase_done = sem("phase_done")
        phases = {}

        def phase_end(e):
            k = phases[id(e)] = phases.get(id(e), 0) + 1
            e.drain().then_inc(phase_done, 1)
            e.wait_ge(phase_done, 5 * k)

        class Chain:

            def __init__(self, e, s):
                self.e, self.s, self.base, self.n = e, s, 0, 0

            def link(self, ins):
                ins.then_inc(self.s, 1)
                self.n += 1
                self.e.wait_ge(self.s, self.base + self.n)

            def loop(self, i, per):
                self.start, self.per = self.base + self.n, per
                self.base, self.n = self.start + i * per, 0

            def loop_end(self, count):
                assert self.n == self.per, (self.n, self.per)
                self.base, self.n = self.start + count * self.per, 0

        dve_step, act_step, pool_step = sem("dve_step"), sem("act_step"), sem("pool_step")

        def block_row(e, which, b):
            o = 3 * BK * which
            return (e.value_load(tab[0:1, ds(b + o, 1)], min_val=0, max_val=T),
                    e.value_load(tab[0:1, ds(b + (o + BK), 1)], min_val=1, max_val=T),
                    e.value_load(tab[0:1, ds(b + (o + 2 * BK), 1)], min_val=0, max_val=B * T))

        def this_round(e, lo, before, j):
            why = "rounds are cut so that a block's last one begins at its last tile or before"
            return (nc.s_assert_within(e.snap(lo + j * U), 0, T - U, skip_runtime_bounds_check_because=why),
                    e.snap(before + j))

        def all_rounds(e, which):
            o = 3 * BK * which + 2 * BK + B
            return e.value_load(tab[0:1, o:o + 1], min_val=B, max_val=B * T)

        in_const, in_edge, in_dst, in_rows = sem("in_const"), sem("in_edge"), sem("in_dst"), sem("in_rows")
        in_x, in_gw, brow_clear = sem("in_x"), sem("in_gw"), sem("brow_clear")
        low_made, low_used = sems("low_made", 8), sems("low_used", 8)
        high_made = sems("high_made", 2)
        keys_ready, bucket_rows, bucket_tot, totals_ready, bases_ready = (
            sem("keys_ready"), sem("bucket_rows"), sem("bucket_tot"), sem("totals_ready"), sem("bases_ready"))
        deg_ready, ext_ready, ext_t, ext2_ready, ext2_t = (
            sem("deg_ready"), sem("ext_ready"), sem("ext_t"), sem("ext2_ready"), sem("ext2_t"))
        root_in, root_out, scales_ready = sem("root_in"), sem("root_out"), sem("scales_ready")
        dst_in, oht_made, exp_done = sems("dst_in", U), sems("oht_made", U), sems("exp_done", U)
        msg_made, idx_made, scattered = sems("msg_made", U), sems("idx_made", U), sems("scattered", U)
        row_in, oh_made, row_used = sems("row_in", U), sems("oh_made", U), sems("row_used", U)
        rows_written, sends_begun, gathers_begun = sem("rows_written"), sem("sends_begun"), sem("gathers_begun")
        in_w0, in_w1, in_small = sem("in_w0"), sem("in_w1"), sem("in_small")
        agg_made, head_mm, head_moved, head_y, head_added = (
            sem("agg_made"), sem("head_mm"), sem("head_moved"), sem("head_y"), sem("head_added"))
        norm_made, slot_read, turned, turn_moved, slot_moved = (
            sem("norm_made"), sem("slot_read"), sem("turned"), sem("turn_moved"), sem("slot_moved"))
        logits1, exp_in, exp_out, comb_ready = sem("logits1"), sem("exp_in"), sem("exp_out"), sem("comb_ready")
        comb_t, comb_moved, bias_mm, bias_added = sem("comb_t"), sem("comb_moved"), sem("bias_mm"), sem("bias_added")
        hid_mm, hid_moved, y_mm, y_added = sem("hid_mm"), sem("hid_moved"), sem("y_mm"), sem("y_added")
        hid1_mm, hid1_moved, y1_mm, y1_added = sem("hid1_mm"), sem("hid1_moved"), sem("y1_mm"), sem("y1_added")
        pair_mm, pair_act, pair_dve, loop_mm, loop_added = (
            sem("pair_mm"), sem("pair_act"), sem("pair_dve"), sem("loop_mm"), sem("loop_added"))
        hx_out, hx_freed = sem("hx_out"), sem("hx_freed")
        gidx_made, got, oh2_made, row2_used = sems("gidx_made", U), sems("got", U), sems("oh2_made", U), sems("row2_used", U)
        agg2_done, agg2_saved = sem("agg2_done"), sem("agg2_saved")
        rh_mm, rh_moved = sem("rh_mm"), sem("rh_moved")
        x_final, out_done = sem("x_final"), sem("out_done")
        agg_done, agg_saved = sem("agg_done"), sem("agg_saved")

        def turn_bank(s):
            return PB[s % 2][:, 0:D].rearrange("p (k n) -> p k n", k=2)

        RH = R3[:, 0:CN]
        RH_CUTS = ((0, 4 * P), (4 * P, 3 * P))
        HIDDEN1 = [(0, 0)] + [x for e in range(E1) for x in ([(0, e + 1)] if e + 1 < E1 else []) + [(1, e)]]

        block = ctx.enter_context(nc.Block())

        @block.sync
        def _(sp):
            for to, of in ((C[:, :], consts), (blk_shift[:, :], shifted), (KC[:, :], bias_cols)):
                sp.dma_start(to, of).then_inc(in_const, 16)
            sp.dma_start(src_i, src_t).then_inc(in_edge, 16)
            sp.dma_start(wts, weight_t).then_inc(in_edge, 16)
            sp.dma_start(drow_i.rearrange("p (g e) -> p g e", g=TG),
                         dst_rows.rearrange("(g p) e -> p g e", p=P)).then_inc(in_rows, 16)
            sp.dma_start(dst_i, dst_t).then_inc(in_dst, 16)
            sp.dma_start(typ_i, type_t).then_inc(in_dst, 16)
            for c in range(NC):
                sp.dma_start(X[:, c * CB:(c + 1) * CB, :],
                             x[c * CN:(c + 1) * CN, :].rearrange("(b p) d -> p b d", p=P)).then_inc(in_x, 16)
            sp.dma_start(RW[:, :, :], f0_router.rearrange("(k p) e -> p k e", p=P)).then_inc(in_small, 16)
            sp.dma_start(RW1[:, :, :], f1_rw1.rearrange("(k p) e -> p k e", p=P)).then_inc(in_small, 16)
            sp.dma_start(RW2[:, :], f1_rw2).then_inc(in_small, 16)
            sp.dma_start(brow[:, 0:D], f0_b2).then_inc(in_small, 16)
            sp.wait_ge(brow_clear, 1)
            sp.dma_start(brow[0:E1, D:2 * D], f1_b3).then_inc(in_small, 16)
            sp.dma_start(srow[:, 0:D], gnn_b2).then_inc(in_small, 16)
            sp.dma_start(srow[:, D:D + E1], f1_rb2).then_inc(in_small, 16)
            sp.dma_start(HB[:, :], h_bias.broadcast_to([P, D])).then_inc(in_small, 16)
            for i, w in enumerate((gnn_w, gnn_w1, gnn_w2, loop_w)):
                sp.dma_start(GW[:, 512 * i:512 * (i + 1)].rearrange("p (k o) -> p k o", k=2),
                             w.rearrange("(k p) o -> p k o", p=P)).then_inc(in_gw, 16)
            phase_end(sp)
            with sp.Fori(0, B) as b:
                lo, rounds, before = block_row(sp, DST, b)
                with sp.Fori(0, rounds) as j:
                    t0, g = this_round(sp, lo, before, j)
                    for u in range(U):
                        sp.wait_ge(oht_made[u], g + 1)
                        sp.dma_start(dst_bc[:, u, :],
                                     dst_rows[ds(t0 + u, 1), :].broadcast_to([P, P])).then_inc(dst_in[u], 16)
            phase_end(sp)
            sp.wait_ge(rows_written, 1)
            with sp.Fori(0, B) as b:
                lo, rounds, before = block_row(sp, SRC, b)
                with sp.Fori(0, rounds) as j:
                    t0, g = this_round(sp, lo, before, j)
                    for u in range(U):
                        sp.wait_ge(row_used[u], g + 1)
                        sp.dma_start(msg[:, u, :],
                                     msgs[ds((t0 + u) * P, P), :]).then_inc(row_in[u], 16)
            phase_end(sp)
            phase_end(sp)
            for e in range(R0):
                for m, w in enumerate((f0_w1, f0_w2)):
                    sp.dma_start(W0[:, e, m, :, :], w[e, :, :].rearrange("(k p) o -> p k o", p=P)).then_inc(in_w0, 16)
            for rel in range(REL):
                sp.dma_start(WR[:, :, rel * D:(rel + 1) * D],
                             rel_w[rel, :, :].rearrange("(k p) o -> p k o", p=P)).then_inc(in_w0, 16)
            phase_end(sp)
            phase_end(sp)
            with sp.Fori(0, NC) as c:
                for s in range(CB):
                    sp.wait_ge(pair_act, c * (2 * CB) + 2 * s + 4)
                    sp.wait_ge(pair_dve, c * (2 * CB) + 2 * s + 4)
                    sp.dma_start(hx[ds((c * CB + s) * (P * REL), P * REL), :].rearrange("(p r) d -> p (r d)", r=REL),
                                 hxs[:, s % 2, :]).then_inc(hx_out, 16)
                    sp.wait_ge(hx_out, c * (16 * CB) + 16 * s + 16)
                    sp.sem_inc(hx_freed, 1)
            phase_end(sp)
            for e in range(E1):
                for m, w in enumerate((f1_w1, f1_w2, f1_w3)):
                    sp.dma_start(W1[:, e, m, :, :], w[e, :, :].rearrange("(k p) o -> p k o", p=P)).then_inc(in_w1, 16)
            phase_end(sp)
            phase_end(sp)
            sp.wait_ge(x_final, 1)
            full = N // P
            sp.dma_start(out[0:full * P, :].rearrange("(b p) d -> p b d", p=P), X[:, 0:full, :]).then_inc(out_done, 16)
            sp.dma_start(out[full * P:N, :], X[0:N - full * P, full, :]).then_inc(out_done, 16)
            sp.wait_ge(out_done, 32)

        @block.gpsimd
        def _(pool):
            nc.gpsimd.memset(brow[:, D:2 * D], 0.0).then_inc(brow_clear, 1)
            nc.gpsimd.memset(zero_rows, 0.0).then_inc(pool_step, 1)
            pool.wait_ge(pool_step, 1)
            tail = (T * P - E) // U
            for u in range(U):
                pool.dma_start(msgs[E + tail * u:E + tail * (u + 1), :].rearrange("(p r) c -> p (r c)", p=43),
                               zero_rows).then_inc(scattered[u], 16)
            phase_end(pool)
            last_row = pool.to_reg(T * P - 1)
            with pool.Fori(0, B) as b:
                lo, rounds, before = block_row(pool, DST, b)
                with pool.Fori(0, rounds) as j:
                    t0, g = this_round(pool, lo, before, j)
                    for u in range(U):
                        pool.wait_ge(msg_made[u], g + 2)
                        pool.wait_ge(idx_made[u], g + 1)
                        pool.sem_inc(sends_begun, 1)
                        pool.indirect_dma_start(
                            msgs, bass.IndirectOffsetOnAxis(ap=idx[:, u:u + 1], axis=0), msg[:, u, :], None,
                            bounds_check=last_row, oob_is_err=False).then_inc(scattered[u], 16)
            n = all_rounds(pool, DST)
            for u in range(U):
                pool.wait_ge(scattered[u], n * 16 + 16)
            pool.sem_inc(rows_written, 1)
            phase_end(pool)
            phase_end(pool)
            phase_end(pool)
            phase_end(pool)
            phase_end(pool)
            phase_end(pool)
            with pool.Fori(0, B) as b:
                lo, rounds, before = block_row(pool, DST, b)
                with pool.Fori(0, rounds) as j:
                    g = pool.snap(before + j)
                    for u in range(U):
                        pool.wait_ge(gidx_made[u], g + 1)
                        pool.sem_inc(gathers_begun, 1)
                        pool.indirect_dma_start(
                            rows_in[:, u, :], None, hx, bass.IndirectOffsetOnAxis(ap=idx[:, u:u + 1], axis=0),
                        ).then_inc(got[u], 16)
            phase_end(pool)
            phase_end(pool)

        @block.scalar
        def _(act):
            for b in range(BK):
                act.wait_ge(bucket_rows, b + 1)
                if b:
                    act.wait_ge(bucket_tot, b)
                nc.scalar.activation(junk, OHB[:, b, :], ACT.Identity,
                                     accum_out=tot[:, b:b + 1]).then_inc(bucket_tot, 1)
            act.wait_ge(root_in, 1)
            nc.scalar.activation(sc1[:, :], sc1[:, :], ACT.Sqrt)
            nc.scalar.activation(rstd[:, :], rstd[:, :], ACT.Sqrt).then_inc(root_out, 1)
            act.wait_ge(scales_ready, 1)
            phase_end(act)
            with act.Fori(0, B) as b:
                lo, rounds, before = block_row(act, DST, b)
                with act.Fori(0, rounds) as j:
                    t0, g = this_round(act, lo, before, j)
                    for u in range(U):
                        act.wait_ge(scattered[u], g * 16 + 16)
                        nc.scalar.activation(msg[:, u, D:D + 1], srcf[:, ds(t0 + u, 1)], ACT.Copy)
                        act.wait_ge(exp_done[u], g + 2)
                        nc.scalar.activation(msg[:, u, 0:D], PB[u][:, 0:D], ACT.Copy,
                                             scale=wts[:, ds(t0 + u, 1)]).then_inc(msg_made[u], 1)
            phase_end(act)
            with act.Fori(0, B) as b:
                act.wait_ge(agg_done, b + 1)
                nc.scalar.activation(AG[:, ds(b, 1), :], aggp[:, ds(b % 2, 1), 0:D], ACT.Copy,
                                     scale=dinv[:, ds(b, 1)]).then_inc(agg_saved, 1)
            phase_end(act)
            with act.Fori(0, NC) as c:
                for i in range(CB):
                    act.wait_ge(head_mm, c * 15 + i + 1)
                    nc.scalar.activation(TC[0][:, :, i * P:(i + 1) * P],
                                         PB[i % 4][:, 0:D].rearrange("p (k n) -> p k n", k=2),
                                         ACT.Copy).then_inc(head_moved, 1)
                for layer, (func, k0) in enumerate(((ACT.Identity, K_B), (ACT.Relu, K_B1))):
                    for q in range(4):
                        half, m = divmod(q, 2)
                        act.wait_ge(head_mm, c * 15 + CB + 4 * layer + q + 1)
                        nc.scalar.activation(TC[layer + 1][:, m, half * HN:(half + 1) * HN],
                                             PB[4 - 4 * layer + q][:, 0:HN], func,
                                             bias=KC[:, k0 + m:k0 + m + 1]).then_inc(head_moved, 1)
            phase_end(act)

            def roots(k):
                act.wait_ge(root_in, k + 1)
                nc.scalar.activation(rstd[:, :], rstd[:, :], ACT.Sqrt).then_inc(root_out, 1)

            def normalise(k, xt):
                act.wait_ge(scales_ready, k + 1)

                def to_xt(c, s):
                    act.wait_ge(slot_moved, c * CB + (k - 1) * B + s + 4)
                    nc.scalar.activation(XT[:, :, ds((c * CB + s) * P, P)], xts[:, s, :, :],
                                         ACT.Copy).then_inc(turn_moved, 1)

                with act.Fori(0, NC) as c:
                    for s in range(CB):
                        act.wait_ge(slot_moved, c * CB + (k - 1) * B + s + 1)
                        nc.scalar.activation(xn[:, s % 4, :], X[:, ds(c * CB + s, 1), :], ACT.Identity,
                                             bias=nmr[:, ds(c * CB + s, 1)],
                                             scale=rstd[:, ds(c * CB + s, 1)]).then_inc(norm_made, 1)
                        if xt and s:
                            to_xt(c, s - 1)
                        if k == 2:
                            if s:
                                pairs(c, s - 1)
                    if xt:
                        to_xt(c, CB - 1)
                    if k == 2:
                        pairs(c, CB - 1)

            def pairs(c, s):
                act.wait_ge(hx_freed, c * CB + s + (2 if s == 0 else 1))
                for q in (0, 2):
                    act.wait_ge(pair_mm, c * (4 * CB) + 4 * s + q + 1)
                    nc.scalar.activation(hxs[:, s % 2, q * 512:(q + 1) * 512], PB[2 + q][:, :],
                                         ACT.Copy).then_inc(pair_act, 1)

            roots(1)
            normalise(1, True)
            act.wait_ge(exp_in, 1)
            nc.scalar.activation(pr, pr, ACT.Exp).then_inc(exp_out, 1)
            phase_end(act)
            with act.Fori(0, NC) as c:
                for e in range(R0):
                    for q in range(4):
                        half, m = divmod(q, 2)
                        act.wait_ge(hid_mm, c * (4 * R0) + 4 * e + q + 1)
                        nc.scalar.activation(HT[e % 2][:, m, half * HN:(half + 1) * HN], PB[q][:, 0:HN], ACT.Gelu,
                                             bias=KC[:, K_F0 + 2 * e + m:K_F0 + 2 * e + m + 1]).then_inc(hid_moved, 1)
            phase_end(act)
            roots(2)
            normalise(2, False)
            phase_end(act)
            with act.Fori(0, B) as b:
                act.wait_ge(agg2_done, b + 1)
                nc.scalar.activation(AG[:, ds(b, 1), :], aggp[:, ds(b % 2, 1), 0:D], ACT.Copy,
                                     scale=SQH).then_inc(agg2_saved, 1)
            phase_end(act)
            roots(3)
            normalise(3, True)
            with act.Fori(0, NC) as c:
                for h, (at, n) in enumerate(RH_CUTS):
                    act.wait_ge(rh_mm, c * 2 + h + 1)
                    nc.scalar.activation(RH[:, at:at + n], PB[h][:, 0:n], ACT.Relu,
                                         bias=KC[:, K_R1:K_R1 + 1]).then_inc(rh_moved, 1)
            act.wait_ge(exp_in, 2)
            nc.scalar.activation(pr[:, :, 0:E1], pr[:, :, 0:E1], ACT.Exp).then_inc(exp_out, 1)
            act.wait_ge(exp_in, 3)
            nc.scalar.activation(g12, g12, ACT.Exp).then_inc(exp_out, 1)
            phase_end(act)
            with act.Fori(0, NC) as c:
                for at, (layer, e) in enumerate(HIDDEN1):
                    for q in range(4):
                        half, m = divmod(q, 2)
                        k0 = (K_X1, K_X2)[layer] + 2 * e + m
                        act.wait_ge(hid1_mm, c * (8 * E1) + 4 * at + q + 1)
                        nc.scalar.activation(HT[2 * layer + e % 2][:, m, half * HN:(half + 1) * HN], PB[q][:, 0:HN],
                                             ACT.Relu, bias=KC[:, k0:k0 + 1]).then_inc(hid1_moved, 1)

        @block.vector
        def _(dve):
            ch = Chain(dve, dve_step)
            for s in low_used + oht_made + exp_done + msg_made + row_used:
                dve.sem_inc(s, 1)
            for s in row2_used:
                dve.sem_inc(s, 1)
            for s, n in ((agg_saved, 2), (agg2_saved, 2), (head_added, 1), (slot_moved, 3), (hid_moved, 4),
                         (hid1_moved, 4), (y_added, 4), (y1_added, 4), (hx_freed, 2), (loop_added, 1),
                         (comb_moved, 2), (bias_added, 2), (turn_moved, CB), (slot_read, CB),
                         (pair_act, 2), (pair_dve, 2)):
                dve.sem_inc(s, n)
            dve.wait_ge(in_edge, 32)
            nc.vector.tensor_copy(srcf, src_i)
            ch.link(nc.vector.tensor_scalar(tmp_i, src_i, 7, None, ALU.arith_shift_right))
            ch.link(nc.vector.tensor_copy(blkS, tmp_i))
            ch.link(nc.vector.tensor_scalar(tmp_i, src_i, 127, None, ALU.bitwise_and))
            nc.vector.tensor_copy(loS, tmp_i).then_inc(keys_ready, 1)
            dve.wait_ge(keys_ready, 1)
            for b in range(BK):
                nc.vector.tensor_scalar(OHB[:, b, :], blkS, float(b), None, ALU.is_equal).then_inc(bucket_rows, 1)
            dve.wait_ge(in_const, 48)
            with dve.Fori(0, T // 8) as i:
                for s in range(8):
                    dve.wait_ge(low_used[s], i + 1)
                    if s % U == 0:
                        dve.wait_ge(low_used[s + U - 1], i + 1)
                        nc.vector.tensor_tensor(
                            OHHI[:, s // U, :, :],
                            blkS[:, ds(i * 8 + s, U)].unsqueeze(2).broadcast_to([P, U, B]),
                            C[:, C_BLK:C_BLK + B].unsqueeze(1).broadcast_to([P, U, B]),
                            ALU.is_equal).then_inc(high_made[s // U], 1)
                    nc.vector.tensor_scalar(WOH[:, s, :], iota, loS[:, ds(i * 8 + s, 1)], wts[:, ds(i * 8 + s, 1)],
                                            ALU.is_equal, ALU.mult).then_inc(low_made[s], 1)
            dve.wait_ge(bucket_tot, BK)
            ch.link(nc.vector.tensor_tensor_scan(cum, tot, tot, 0.0, ALU.add, ALU.max))
            nc.vector.tensor_tensor(exc, cum, tot, ALU.subtract).then_inc(totals_ready, 1)
            for c in range(NC):
                dve.wait_ge(in_x, 16 * NC)
                for b in range(c * CB, (c + 1) * CB):
                    nc.vector.bn_stats(stat6[:, b, :], X[:, b, :]).then_inc(dve_step, 1)
                    ch.n += 1
            dve.wait_ge(dve_step, ch.base + ch.n)
            for b in range(B):
                nc.vector.bn_aggr(mv[:, b, :], stat6[:, b, :]).then_inc(dve_step, 1)
                ch.n += 1
            dve.wait_ge(bases_ready, 1)
            ch.link(nc.vector.tensor_copy(base, PB[1][:, 0:BK]))
            for b in range(BK + 1):
                if b < BK:
                    nc.vector.tensor_tensor_scan(scanp[b % 2], OHB[:, b, :], OHB[:, b, :], base[:, b:b + 1],
                                                 ALU.add, ALU.max).then_inc(dve_step, 1)
                    ch.n += 1
                if b:
                    dve.wait_ge(dve_step, ch.base + ch.n - (1 if b < BK else 0))
                    ch.link(nc.vector.copy_predicated(pos1, OHB[:, b - 1, :], scanp[(b - 1) % 2]))
            nc.vector.tensor_scalar(pos_i, pos1, -1.0, None, ALU.add)
            dve.wait_ge(in_dst, 32)
            nc.vector.tensor_copy(dstf[:, :], dst_i)
            nc.vector.tensor_scalar(blkD[:, :], dst_i, 7, 20, ALU.arith_shift_right, ALU.arith_shift_left)
            ch.link(nc.vector.tensor_scalar(tmp_f, src_i, float(NP - 1), float(REL), ALU.min, ALU.mult))
            nc.vector.tensor_tensor(gidx[:, :], tmp_f, typ_i, ALU.add)
            dve.wait_ge(in_rows, 16)
            rows3 = drow_i.rearrange("p (g e) -> p g e", g=TG)
            ch.link(nc.vector.tensor_reduce(tmn, rows3, AX, ALU.min))
            ch.link(nc.vector.tensor_reduce(tmx, rows3, AX, ALU.max))
            ch.link(nc.vector.tensor_copy(tmn_i, tmn))
            ch.link(nc.vector.tensor_copy(tmx_i, tmx))
            ch.link(nc.vector.tensor_scalar(tmn_i, tmn_i, 7, None, ALU.arith_shift_right))
            ch.link(nc.vector.tensor_scalar(tmx_i, tmx_i, 7, None, ALU.arith_shift_right))
            ch.link(nc.vector.tensor_copy(tmn, tmn_i))
            ch.link(nc.vector.tensor_copy(tmx, tmx_i))
            blks = C[:, C_BLK:C_BLK + B].unsqueeze(2).broadcast_to([P, B, TG])
            ch.link(nc.vector.tensor_tensor(ge, blks, tmn.unsqueeze(1).broadcast_to([P, B, TG]), ALU.is_ge))
            ch.link(nc.vector.tensor_tensor(le, blks, tmx.unsqueeze(1).broadcast_to([P, B, TG]), ALU.is_le))
            ch.link(nc.vector.tensor_tensor(inb, ge, le, ALU.mult))
            ch.link(nc.vector.tensor_tensor(ge, inb, C[:, C_REV:C_REV + TG].unsqueeze(1).broadcast_to([P, B, TG]), ALU.mult))
            ch.link(nc.vector.tensor_tensor(le, inb, C[:, C_NEXT:C_NEXT + TG].unsqueeze(1).broadcast_to([P, B, TG]), ALU.mult))
            ch.link(nc.vector.tensor_reduce(two[:, 0, :], ge, AX, ALU.max))
            nc.vector.tensor_reduce(two[:, 1, :], le, AX, ALU.max).then_inc(ext_ready, 1)
            dve.wait_ge(ext_t, 1)
            ch.link(nc.vector.tensor_reduce(ext[:, 0:1], PB[5][0:B, 0:P], AX, ALU.max))
            nc.vector.tensor_reduce(ext[:, 1:2], PB[5][0:B, P:2 * P], AX, ALU.max).then_inc(ext2_ready, 1)
            dve.wait_ge(ext2_t, 1)
            ch.link(nc.vector.tensor_scalar(rowf[:, 0, 0:B], PB[5][0:1, 256:256 + B], -1.0, float(BIG), ALU.mult, ALU.add))
            ch.link(nc.vector.tensor_scalar(rowf[:, 0, 0:B], rowf[:, 0, 0:B], float(E // P), None, ALU.min))
            ch.link(nc.vector.tensor_tensor(rowf[:, 1, 0:B], PB[5][0:1, 384:384 + B], rowf[:, 0, 0:B], ALU.subtract))
            ch.link(nc.vector.tensor_copy(rowi[:, 0, :], PB[2][0:1, 0:BK]))
            ch.link(nc.vector.tensor_scalar(rowf[:, 4, 0:B], PB[2][0:1, 1:BK], -1.0, 0.0, ALU.add, ALU.max))
            ch.link(nc.vector.tensor_copy(rowi[:, 1, 0:B], rowf[:, 4, 0:B]))
            ch.link(nc.vector.tensor_scalar(rowi[:, 2, 0:B], rowi[:, 0, 0:B], 7, None, ALU.arith_shift_right))
            ch.link(nc.vector.tensor_scalar(rowi[:, 3, 0:B], rowi[:, 1, 0:B], 7, None, ALU.arith_shift_right))
            ch.link(nc.vector.tensor_copy(rowf[:, 2, 0:B], rowi[:, 2, 0:B]))
            ch.link(nc.vector.tensor_tensor(rowf[:, 3, 0:B], rowi[:, 3, 0:B], rowi[:, 2, 0:B], ALU.subtract))
            ch.link(nc.vector.tensor_scalar(rowf[:, 3, 0:B], rowf[:, 3, 0:B], 1.0, None, ALU.add))
            for which in (DST, SRC):
                first, tiles = rowf[:, 2 * which, 0:B], rowf[:, 2 * which + 1, 0:B]
                o = 3 * BK * which
                ch.link(nc.vector.tensor_copy(tab[0:1, o:o + B], first))
                ch.link(nc.vector.tensor_scalar(tiles, tiles, 1.0, float(U - 1), ALU.max, ALU.add))
                ch.link(nc.vector.tensor_copy(rowi[:, 4, 0:B], tiles))
                ch.link(nc.vector.tensor_scalar(tab[0:1, o + BK:o + BK + B], rowi[:, 4, 0:B], 2, None,
                                                ALU.arith_shift_right))
                ch.link(nc.vector.tensor_copy(rowf[:, 5, 0:B], tab[0:1, o + BK:o + BK + B]))
                ch.link(nc.vector.tensor_tensor_scan(rowf[:, 6, 0:B], rowf[:, 5, 0:B], rowf[:, 5, 0:B], 0.0,
                                                     ALU.add, ALU.max))
                ch.link(nc.vector.memset(tab[0:1, o + 2 * BK:o + 2 * BK + 1], 0))
                ch.link(nc.vector.tensor_copy(tab[0:1, o + 2 * BK + 1:o + 3 * BK], rowf[:, 6, 0:B]))
            dve.wait_ge(deg_ready, 1)
            ch.link(nc.vector.tensor_scalar(sc2[:, :], PB[0][:, 0:B], 1.0, None, ALU.add))
            ch.link(nc.vector.tensor_scalar(sc1[:, :], sc2[:, :], 1e-30, None, ALU.max))
            nc.vector.tensor_scalar(rstd[:, :], mv[:, :, 1], EPS, None, ALU.add).then_inc(root_in, 1)
            ch.link(nc.vector.tensor_scalar(sc2[:, :], sc2[:, :], 0.0, None, ALU.is_gt))
            dve.wait_ge(root_out, 1)
            ch.link(nc.vector.reciprocal(sc1[:, :], sc1[:, :]))
            ch.link(nc.vector.tensor_tensor(dinv[:, :], sc1[:, :], sc2[:, :], ALU.mult))
            ch.link(nc.vector.reciprocal(rstd[:, :], rstd[:, :]))
            ch.link(nc.vector.tensor_tensor(sc1[:, :], rstd[:, :], dinv[:, :], ALU.mult))
            ch.link(nc.vector.scalar_tensor_tensor(sc2[:, :], mv[:, :, 0], -1.0, sc1[:, :], ALU.mult, ALU.mult))
            for b in range(B):
                nc.vector.tensor_scalar(XS[:, b, :], X[:, b, :], sc1[:, b:b + 1], sc2[:, b:b + 1], ALU.mult, ALU.add)
            nc.vector.memset(junk[:, 0:1], 0.0).then_inc(scales_ready, 1)
            phase_end(dve)
            nc.vector.memset(msg[:, :, D + 1:ROW], 0.0)
            with dve.Fori(0, B) as b:
                lo, rounds, before = block_row(dve, DST, b)
                with dve.Fori(0, rounds) as j:
                    t0, g = this_round(dve, lo, before, j)
                    for u in range(U):
                        dve.wait_ge(dst_in[u], g * 16 + 16)
                        dve.wait_ge(exp_done[u], g + 1)
                        nc.vector.tensor_scalar(oneh[:, u, :], dst_bc[:, u, :], C[:, ds(b + C_NODE, 1)], None,
                                                ALU.is_equal).then_inc(oht_made[u], 1)
                        dve.wait_ge(scattered[u], g * 16 + 16)
                        nc.vector.scalar_tensor_tensor(
                            idx[:, u:u + 1].bitcast(i32), blkD[:, ds(t0 + u, 1)], blk_shift[:, ds(b, 1)],
                            pos_i[:, ds(t0 + u, 1)], ALU.bitwise_xor, ALU.bitwise_or).then_inc(idx_made[u], 1)
            phase_end(dve)
            with dve.Fori(0, B) as b:
                lo, rounds, before = block_row(dve, SRC, b)
                with dve.Fori(0, rounds) as j:
                    t0, g = this_round(dve, lo, before, j)
                    for u in range(U):
                        dve.wait_ge(row_in[u], g * 16 + 16)
                        dve.wait_ge(row_used[u], g + 1)
                        nc.vector.tensor_scalar(oneh[:, u, :], iota, msg[:, u, D:D + 1], C[:, ds(b + C_NEG, 1)],
                                                ALU.subtract, ALU.is_equal).then_inc(oh_made[u], 1)
            phase_end(dve)
            with dve.Fori(0, NC) as c:
                for i in range(CB):
                    nc.vector.scalar_tensor_tensor(
                        head_in[:, i, :], XS[:, ds(c * CB + i, 1), :], dinv[:, ds(c * CB + i, 1)],
                        AG[:, ds(c * CB + i, 1), :], ALU.mult, ALU.add).then_inc(agg_made, 1)
                for i in range(CB):
                    dve.wait_ge(head_y, c * CB + i + 1)
                    nc.vector.tensor_tensor(X[:, ds(c * CB + i, 1), :], X[:, ds(c * CB + i, 1), :],
                                            PB[4 + i % 4][:, 0:D], ALU.add).then_inc(head_added, 1)
            phase_end(dve)

            def statistics(k):
                for b in range(B):
                    nc.vector.bn_stats(stat6[:, b, :], X[:, b, :]).then_inc(dve_step, 1)
                    ch.n += 1
                dve.wait_ge(dve_step, ch.base + ch.n)
                for b in range(B):
                    nc.vector.bn_aggr(mv[:, b, :], stat6[:, b, :]).then_inc(dve_step, 1)
                    ch.n += 1
                dve.wait_ge(dve_step, ch.base + ch.n)
                nc.vector.tensor_scalar(rstd[:, :], mv[:, :, 1], EPS, None, ALU.add).then_inc(root_in, 1)
                dve.wait_ge(root_out, k + 1)
                ch.link(nc.vector.reciprocal(rstd[:, :], rstd[:, :]))
                nc.vector.scalar_tensor_tensor(nmr[:, :], mv[:, :, 0], -1.0, rstd[:, :], ALU.mult,
                                               ALU.mult).then_inc(scales_ready, 1)

            def move_blocks(k, add):
                with dve.Fori(0, NC) as c:
                    for s in range(CB):
                        n = c * CB + (k - 1) * B + s
                        if add:
                            dve.wait_ge(norm_made, n + 1)
                            nc.vector.tensor_tensor(X[:, ds(c * CB + s, 1), :], X[:, ds(c * CB + s, 1), :],
                                                    xn[:, s % 4, :], ALU.add)
                        dve.wait_ge(turned, n + 1)
                        if k == 1:
                            dve.wait_ge(slot_read, n + 1)
                        if k != 2:
                            dve.wait_ge(turn_moved, c * CB + (B if k == 3 else 0) + s + 1)
                        nc.vector.tensor_copy(xts[:, s, :, :], turn_bank(s)).then_inc(slot_moved, 1)
                        if k == 2 and s:
                            pairs(c, s - 1)
                    if k == 2:
                        pairs(c, CB - 1)

            def pairs(c, s):
                dve.wait_ge(hx_freed, c * CB + s + (2 if s == 0 else 1))
                for q in (1, 3):
                    dve.wait_ge(pair_mm, c * (4 * CB) + 4 * s + q + 1)
                    nc.vector.tensor_copy(hxs[:, s % 2, q * 512:(q + 1) * 512], PB[2 + q][:, :]).then_inc(pair_dve, 1)
                dve.wait_ge(loop_mm, c * CB + s + 1)
                nc.vector.scalar_tensor_tensor(X[:, ds(c * CB + s, 1), :], PB[6 + s % 2][:, 0:D], SQH,
                                               X[:, ds(c * CB + s, 1), :], ALU.mult, ALU.add).then_inc(loop_added, 1)

            def softmax_top2(layer, n):
                dve.wait_ge((slot_read, logits1)[layer], (CB, 0)[layer] + B)
                ch.link(nc.vector.tensor_copy(
                    lg[:, :, 0:n], PB[7][:, 0:B * 8].rearrange("p (b e) -> p b e", e=8)[:, :, 0:n]))
                ch.link(nc.vector.tensor_reduce(rmax, lg[:, :, 0:n], AX, ALU.max))
                nc.vector.tensor_tensor(pr[:, :, 0:n], lg[:, :, 0:n], rmax.unsqueeze(2).broadcast_to([P, B, n]),
                                        ALU.subtract).then_inc(exp_in, 1)
                dve.wait_ge(exp_out, layer + 1)
                ch.link(nc.vector.tensor_reduce(rsum, pr[:, :, 0:n], AX, ALU.add))
                ch.link(nc.vector.reciprocal(rsum, rsum))
                ch.link(nc.vector.tensor_tensor(pr[:, :, 0:n], pr[:, :, 0:n],
                                                rsum.unsqueeze(2).broadcast_to([P, B, n]), ALU.mult))
                if n < 8:
                    ch.link(nc.vector.memset(pr[:, :, n:8], -1.0))
                for b in range(B):
                    nc.vector.max(top[:, b, :], pr[:, b, :]).then_inc(dve_step, 1)
                    ch.n += 1
                dve.wait_ge(dve_step, ch.base + ch.n)
                for b in range(B):
                    nc.vector.max_index(top_i[:, b, :], top[:, b, :], pr[:, b, :]).then_inc(dve_step, 1)
                    ch.n += 1
                dve.wait_ge(dve_step, ch.base + ch.n)
                ch.link(nc.vector.tensor_copy(top_f, top_i))

            def combine():
                eights = C[:, C_I8:C_I8 + 8].unsqueeze(1).broadcast_to([P, B, 8])
                for i, eq in enumerate((eq1, eq2)):
                    ch.link(nc.vector.tensor_tensor(eq, eights, top_f[:, :, i:i + 1].broadcast_to([P, B, 8]),
                                                    ALU.is_equal))
                    ch.link(nc.vector.tensor_tensor(eq, eq, g12[:, i, :].unsqueeze(2).broadcast_to([P, B, 8]),
                                                    ALU.mult))
                nc.vector.tensor_tensor(comb[:, :, :], eq1, eq2, ALU.add).then_inc(comb_ready, 1)

            def output_bias(layer):
                def add(b):
                    dve.wait_ge(bias_mm, layer * B + b + 1)
                    nc.vector.tensor_tensor(X[:, b, :], X[:, b, :], PB[2 + b % 2][:, 0:D],
                                            ALU.add).then_inc(bias_added, 1)

                for b in range(B):
                    dve.wait_ge(comb_t, layer * B + b + 1)
                    nc.vector.tensor_copy(comb_s[:, b % 4, :], PB[b % 2][0:8, 0:P]).then_inc(comb_moved, 1)
                    if b:
                        add(b - 1)
                add(B - 1)

            def add_experts(n, made, added):
                with dve.Fori(0, NC) as c:
                    for e in range(n):
                        for i in range(CB):
                            m = c * (n * CB) + e * CB + i
                            dve.wait_ge(made, m + 1)
                            if e:
                                dve.wait_ge(added, m - CB + 1 + 4)
                            nc.vector.scalar_tensor_tensor(
                                X[:, ds(c * CB + i, 1), :], PB[4 + (e * CB + i) % 4][:, 0:D],
                                comb[:, ds(c * CB + i, 1), e:e + 1], X[:, ds(c * CB + i, 1), :],
                                ALU.mult, ALU.add).then_inc(added, 1)

            statistics(1)
            move_blocks(1, True)
            softmax_top2(0, R0)
            ch.link(nc.vector.tensor_tensor(rsum, top[:, :, 0], top[:, :, 1], ALU.add))
            ch.link(nc.vector.tensor_scalar(rsum, rsum, 1e-12, None, ALU.max))
            ch.link(nc.vector.reciprocal(rsum, rsum))
            for i in range(2):
                ch.link(nc.vector.tensor_tensor(g12[:, i, :], top[:, :, i], rsum, ALU.mult))
            combine()
            output_bias(0)
            phase_end(dve)
            add_experts(R0, y_mm, y_added)
            phase_end(dve)
            statistics(2)
            move_blocks(2, False)
            dve.wait_ge(in_small, 128)
            dve.wait_ge(loop_added, B + 1)
            nc.vector.tensor_tensor(X[:, :, :], X[:, :, :], HB[:, :].unsqueeze(1).broadcast_to([P, B, D]), ALU.add)
            phase_end(dve)
            with dve.Fori(0, B) as b:
                lo, rounds, before = block_row(dve, DST, b)
                with dve.Fori(0, rounds) as j:
                    t0, g = this_round(dve, lo, before, j)
                    for u in range(U):
                        dve.wait_ge(row2_used[u], g + 1)
                        nc.vector.tensor_copy(idx[:, u:u + 1], gidx[:, ds(t0 + u, 1)]).then_inc(gidx_made[u], 1)
                        nc.vector.tensor_scalar(oneh[:, u, :], iota, dstf[:, ds(t0 + u, 1)], C[:, ds(b + C_NEG, 1)],
                                                ALU.subtract, ALU.is_equal).then_inc(oh2_made[u], 1)
            dve.wait_ge(agg2_saved, B + 2)
            nc.vector.tensor_tensor(X[:, :, :], X[:, :, :], AG, ALU.add)
            phase_end(dve)
            statistics(3)
            move_blocks(3, False)
            softmax_top2(1, E1)
            for i in (1, 0):
                ch.link(nc.vector.tensor_tensor(g12[:, i, :], top[:, :, i], top[:, :, 0], ALU.subtract))
            nc.vector.memset(rmax, 0.0).then_inc(exp_in, 1)
            dve.wait_ge(exp_out, 3)
            ch.link(nc.vector.tensor_tensor(rsum, g12[:, 0, :], g12[:, 1, :], ALU.add))
            ch.link(nc.vector.reciprocal(rsum, rsum))
            for i in range(2):
                ch.link(nc.vector.tensor_tensor(g12[:, i, :], g12[:, i, :], rsum, ALU.mult))
            combine()
            output_bias(1)
            phase_end(dve)
            add_experts(E1, y1_mm, y1_added)
            dve.wait_ge(y1_added, B * E1 + 4)
            nc.vector.memset(rmax, 0.0).then_inc(x_final, 1)

        @block.tensor
        def _(pe):
            pe.wait_ge(in_const, 48)
            pe.matmul(PB[0][:, 0:B], zeros[:, 0:P], zeros[:, 0:B], start=True, stop=False, skip_group_check=True)
            with pe.Fori(0, T // 8) as i:
                for s in range(8):
                    if s % U == 0:
                        pe.wait_ge(high_made[s // U], i + 1)
                    pe.wait_ge(low_made[s], i + 1)
                    pe.matmul(PB[0][:, 0:B], WOH[:, s, :], OHHI[:, s // U, s % U, :], start=False, stop=False,
                              skip_group_check=True).then_inc(low_used[s], 1)
            pe.matmul(PB[0][:, 0:B], zeros[:, 0:P], zeros[:, 0:B], start=False, stop=True,
                      skip_group_check=True).then_inc(deg_ready, 1)
            pe.wait_ge(totals_ready, 1)
            pe.matmul(PB[2][:, 0:BK], ones, exc, start=True, stop=True)
            pe.matmul(PB[1][:, 0:BK], ones, exc, start=True, stop=False)
            pe.matmul(PB[1][:, 0:BK], tri, tot, start=False, stop=True).then_inc(bases_ready, 1)
            pe.wait_ge(ext_ready, 1)
            pe.transpose(PB[5][0:B, 0:P], two[:, 0, :], ident)
            pe.transpose(PB[5][0:B, P:2 * P], two[:, 1, :], ident).then_inc(ext_t, 1)
            pe.wait_ge(ext2_ready, 1)
            pe.transpose(PB[5][0:1, 256:256 + B], ext[:, 0:1], ident[0:B, 0:B])
            pe.transpose(PB[5][0:1, 384:384 + B], ext[:, 1:2], ident[0:B, 0:B]).then_inc(ext2_t, 1)
            phase_end(pe)
            with pe.Fori(0, B) as b:
                lo, rounds, before = block_row(pe, DST, b)
                with pe.Fori(0, rounds) as j:
                    t0, g = this_round(pe, lo, before, j)
                    for u in range(U):
                        pe.wait_ge(oht_made[u], g + 2)
                        pe.wait_ge(msg_made[u], g + 1)
                        pe.matmul(PB[u][:, 0:D], oneh[:, u, :], XS[:, ds(b, 1), :], start=True,
                                  stop=True).then_inc(exp_done[u], 1)
            phase_end(pe)
            with pe.Fori(0, B) as b:
                lo, rounds, before = block_row(pe, SRC, b)
                pe.wait_ge(agg_saved, b + 1)
                pe.matmul(aggp[:, ds(b % 2, 1), 0:D], zeros[:, 0:P], zeros[:, 0:D], start=True, stop=False,
                          skip_group_check=True)
                with pe.Fori(0, rounds) as j:
                    t0, g = this_round(pe, lo, before, j)
                    for u in range(U):
                        pe.wait_ge(oh_made[u], g + 1)
                        pe.matmul(aggp[:, ds(b % 2, 1), 0:D], oneh[:, u, :], msg[:, u, 0:D], start=False, stop=False,
                                  skip_group_check=True).then_inc(row_used[u], 1)
                pe.matmul(aggp[:, ds(b % 2, 1), 0:D], zeros[:, 0:P], zeros[:, 0:D], start=False, stop=True,
                          skip_group_check=True).then_inc(agg_done, 1)
            phase_end(pe)

            def layer(weight, m, of, at, n, to, signal):
                for k in range(2):
                    moving = of[:, k, at:at + n] if isinstance(at, int) else of[:, k, ds(at, n)]
                    mm = pe.matmul(to[:, 0:n], weight[:, k, m * P:(m + 1) * P], moving,
                                   start=(k == 0), stop=(k == 1))
                mm.then_inc(signal, 1)

            pe.wait_ge(in_gw, 64)
            pe.wait_ge(in_small, 128)
            gw = [GW[:, 512 * i:512 * (i + 1)].rearrange("p (k o) -> p k o", k=2) for i in range(4)]
            with pe.Fori(0, NC) as c:
                for i in range(CB):
                    pe.wait_ge(agg_made, c * CB + i + 1)
                    if i >= 4:
                        pe.wait_ge(head_moved, c * 15 + i - 3)
                    for k in range(2):
                        mm = pe.transpose(PB[i % 4][:, k * P:(k + 1) * P],
                                          head_in[:, i, k * P:(k + 1) * P], ident)
                    mm.then_inc(head_mm, 1)
                pe.wait_ge(head_added, c * CB + 1)
                pe.wait_ge(head_moved, c * 15 + 7)
                for q in range(4):
                    layer(gw[0], q % 2, TC[0], q // 2 * HN, HN, PB[4 + q], head_mm)
                pe.wait_ge(head_moved, c * 15 + 11)
                for q in range(4):
                    layer(gw[1], q % 2, TC[1], q // 2 * HN, HN, PB[q], head_mm)
                pe.wait_ge(head_moved, c * 15 + 15)
                for i in range(CB):
                    if i >= 4:
                        pe.wait_ge(head_added, c * CB + i - 2)
                    for k in range(2):
                        pe.matmul(PB[4 + i % 4][:, 0:D], TC[2][:, k, i * P:(i + 1) * P], gw[2][:, k, :],
                                  start=(k == 0), stop=False)
                    pe.matmul(PB[4 + i % 4][:, 0:D], ones[0:1, :], srow[:, 0:D], start=False,
                              stop=True).then_inc(head_y, 1)
            phase_end(pe)

            def turn(k, after=None):
                with pe.Fori(0, NC) as c:
                    for s in range(CB):
                        n = c * CB + (k - 1) * B + s
                        pe.wait_ge(norm_made, n + 1)
                        last = 3 if s == 0 else 2
                        pe.wait_ge(slot_moved, n + last)
                        for h in range(2):
                            mm = pe.transpose(turn_bank(s)[:, h, :], xn[:, s % 4, h * P:(h + 1) * P], ident)
                        mm.then_inc(turned, 1)
                        if after and s:
                            after(c, s - 1)
                    if after:
                        after(c, CB - 1)

            def logits0(c, s):
                pe.wait_ge(slot_moved, c * CB + s + 4)
                for k in range(2):
                    mm = pe.matmul(PB[7][:, ds((c * CB + s) * 8, 8)], xts[:, s, k, :], RW[:, k, :],
                                   start=(k == 0), stop=(k == 1))
                mm.then_inc(slot_read, 1)

            def relations(c, s):
                pe.wait_ge(slot_moved, c * CB + B + s + 4)
                for q in range(4):
                    pe.wait_ge((pair_act, pair_dve)[q % 2], c * (2 * CB) + 2 * s + q // 2 + 1)
                    for k in range(2):
                        mm = pe.matmul(PB[2 + q][:, :], xts[:, s, k, :], WR[:, k, 512 * q:512 * (q + 1)],
                                       start=(k == 0), stop=(k == 1))
                    mm.then_inc(pair_mm, 1)
                pe.wait_ge(loop_added, c * CB + s + 1)
                for k in range(2):
                    mm = pe.matmul(PB[6 + s % 2][:, 0:D], xts[:, s, k, :], gw[3][:, k, :],
                                   start=(k == 0), stop=(k == 1))
                mm.then_inc(loop_mm, 1)

            def bias_products(layer_no):
                pe.wait_ge(comb_ready, layer_no + 1)

                def product(b):
                    n = layer_no * B + b
                    pe.wait_ge(comb_moved, n + 3)
                    pe.wait_ge(bias_added, n + 1)
                    pe.matmul(PB[2 + b % 2][:, 0:D], comb_s[:, b % 4, :], brow[:, layer_no * D:(layer_no + 1) * D],
                              start=True, stop=True).then_inc(bias_mm, 1)

                for b in range(B):
                    pe.wait_ge(comb_moved, layer_no * B + b + 1)
                    pe.transpose(PB[b % 2][0:8, 0:P], comb[:, b, :], ident).then_inc(comb_t, 1)
                    if b:
                        product(b - 1)
                product(B - 1)

            turn(1, logits0)
            bias_products(0)
            phase_end(pe)
            pe.wait_ge(in_w0, 16 * (2 * R0 + REL))
            with pe.Fori(0, NC) as c:
                def hidden(e):
                    for q in range(4):
                        pe.wait_ge(hid_moved, c * (4 * R0) + 4 * e + q + 1)
                        layer(W0[:, e, 0, :, :], q % 2, XT, c * CN + q // 2 * HN, HN, PB[q], hid_mm)

                hidden(0)
                for e in range(R0):
                    if e + 1 < R0:
                        hidden(e + 1)
                    pe.wait_ge(hid_moved, c * (4 * R0) + 4 * e + 8)
                    for i in range(CB):
                        pe.wait_ge(y_added, c * (R0 * CB) + e * CB + i + 1)
                        for k in range(2):
                            mm = pe.matmul(PB[4 + (e * CB + i) % 4][:, 0:D], HT[e % 2][:, k, i * P:(i + 1) * P],
                                           W0[:, e, 1, k, :], start=(k == 0), stop=(k == 1))
                        mm.then_inc(y_mm, 1)
            phase_end(pe)
            turn(2, relations)
            phase_end(pe)
            with pe.Fori(0, B) as b:
                lo, rounds, before = block_row(pe, DST, b)
                pe.wait_ge(agg2_saved, b + 1)
                pe.matmul(aggp[:, ds(b % 2, 1), 0:D], zeros[:, 0:P], zeros[:, 0:D], start=True, stop=False,
                          skip_group_check=True)
                with pe.Fori(0, rounds) as j:
                    g = pe.snap(before + j)
                    for u in range(U):
                        pe.wait_ge(oh2_made[u], g + 1)
                        pe.wait_ge(got[u], g * 16 + 16)
                        pe.matmul(aggp[:, ds(b % 2, 1), 0:D], oneh[:, u, :], rows_in[:, u, :], start=False,
                                  stop=False, skip_group_check=True).then_inc(row2_used[u], 1)
                pe.matmul(aggp[:, ds(b % 2, 1), 0:D], zeros[:, 0:P], zeros[:, 0:D], start=False, stop=True,
                          skip_group_check=True).then_inc(agg2_done, 1)
            phase_end(pe)
            turn(3)
            pe.wait_ge(turn_moved, 2 * B + CB)
            with pe.Fori(0, NC) as c:
                for h, (at, n) in enumerate(RH_CUTS):
                    for k in range(2):
                        mm = pe.matmul(PB[h][:, 0:n], RW1[:, k, :], XT[:, k, ds(c * CN + at, n)],
                                       start=(k == 0), stop=(k == 1))
                    mm.then_inc(rh_mm, 1)
                pe.wait_ge(rh_moved, c * 2 + 2)
                for i in range(CB):
                    to = PB[7][:, ds((c * CB + i) * 8, E1)]
                    pe.matmul(to, RH[:, i * P:(i + 1) * P], RW2[:, :], start=True, stop=False)
                    pe.matmul(to, ones[0:1, :], srow[:, D:D + E1], start=False, stop=True).then_inc(logits1, 1)
            bias_products(1)
            phase_end(pe)
            pe.wait_ge(in_w1, 16 * 3 * E1)
            with pe.Fori(0, NC) as c:
                def outputs(e):
                    pe.wait_ge(hid1_moved, c * (8 * E1) + 4 * HIDDEN1.index((1, e)) + 8)
                    for i in range(CB):
                        m = c * (E1 * CB) + e * CB + i
                        pe.wait_ge(y1_added, m + (3 if e == 0 and i < 2 else 1))
                        for k in range(2):
                            mm = pe.matmul(PB[4 + (e * CB + i) % 4][:, 0:D], HT[2 + e % 2][:, k, i * P:(i + 1) * P],
                                           W1[:, e, 2, k, :], start=(k == 0), stop=(k == 1))
                        mm.then_inc(y1_mm, 1)

                for at, (part, e) in enumerate(HIDDEN1):
                    if part == 1:
                        pe.wait_ge(hid1_moved, c * (8 * E1) + 4 * HIDDEN1.index((0, e)) + 8)
                    for q in range(4):
                        pe.wait_ge(hid1_moved, c * (8 * E1) + 4 * at + q + 1)
                        if part == 0:
                            layer(W1[:, e, 0, :, :], q % 2, XT, c * CN + q // 2 * HN, HN, PB[q], hid1_mm)
                        else:
                            layer(W1[:, e, 1, :, :], q % 2, HT[e % 2], q // 2 * HN, HN, PB[q], hid1_mm)
                    if part == 1 and e:
                        outputs(e - 1)
                outputs(E1 - 1)


_OUT = (N, D)


def _lay_out(a):
    import numpy as np

    def tiles(v, pad):
        v = np.concatenate([v, np.full(T * P - E, pad, v.dtype)])
        return np.ascontiguousarray(v.reshape(T, P).T)

    def cols(*vs):
        return np.concatenate([v.reshape(-1, P).T for v in vs], axis=1)

    a = {k: np.asarray(v) for k, v in a.items()}
    consts = np.zeros((P, C_N), np.float32)
    p = np.arange(P)
    consts[:, C_IOTA:C_IOTA + P] = p[None]
    consts[:, C_ID:C_ID + P] = np.eye(P)
    consts[:, C_TRI:C_TRI + P] = p[:, None] < p[None]
    consts[:, C_ONE:C_ONE + P] = 1
    consts[:, C_NODE:C_NODE + B] = p[:, None] + P * np.arange(B)[None]
    consts[:, C_NEG:C_NEG + BK] = -P * np.arange(BK)[None]
    consts[:, C_BLK:C_BLK + BK] = np.arange(BK)[None]
    consts[:, C_I8:C_I8 + 8] = np.arange(8)[None]
    tile = p[:, None] + P * np.arange(TG)[None]
    consts[:, C_REV:C_REV + TG] = BIG - tile
    consts[:, C_NEXT:C_NEXT + TG] = tile + 1
    dst, src = a["dst"].astype(np.int32, copy=False), a["src"].astype(np.int32, copy=False)
    return {
        "x": np.concatenate([a["x"], np.zeros((NP - N, D), np.float32)]),
        "src_t": tiles(src, NP),
        "dst_t": tiles(dst, NP),
        "type_t": tiles(a["edge_type_8"], 0),
        "weight_t": tiles(a["edge_weight"], 0),
        "dst_rows": np.concatenate([dst, np.full(TG * P * P - E, NP, dst.dtype)]).reshape(TG * P, P),
        "consts": consts,
        "shifted": np.broadcast_to(np.arange(BK, dtype=np.int32) << 20, (P, BK)).copy(),
        "bias_cols": np.ascontiguousarray(cols(
            a["L0_gnn_b"], a["L0_gnn_b1"], a["L0_ffn_b1"], a["L1_ffn_router_b1"], a["L1_ffn_expert_b1"],
            a["L1_ffn_expert_b2"])),
        "gnn_w": a["L0_gnn_W"], "gnn_w1": a["L0_gnn_W1"], "gnn_w2": a["L0_gnn_W2"],
        "gnn_b2": a["L0_gnn_b2"].reshape(1, D),
        "f0_router": np.ascontiguousarray(a["L0_ffn_router_w"].T), "f0_w1": a["L0_ffn_w1"],
        "f0_w2": a["L0_ffn_w2"], "f0_b2": a["L0_ffn_b2"],
        "rel_w": a["L1_gnn_weight"], "loop_w": a["L1_gnn_loop_weight"],
        "h_bias": a["L1_gnn_h_bias"].reshape(1, D),
        "f1_rw1": a["L1_ffn_router_w1"], "f1_rw2": a["L1_ffn_router_w2"],
        "f1_rb2": a["L1_ffn_router_b2"].reshape(1, E1), "f1_w1": a["L1_ffn_expert_w1"],
        "f1_w2": a["L1_ffn_expert_w2"], "f1_w3": a["L1_ffn_expert_w3"], "f1_b3": a["L1_ffn_expert_b3"],
    }


def kernel(**inputs):
    import concourse.bacc as bacc
    from concourse.bass_utils import run_bass_kernel_spmd

    nc = bacc.Bacc("TRN2", target_bir_lowering=False, num_devices=1)
    arrays = {f"in_{k}": v for k, v in _lay_out(inputs).items()}
    args = {k[3:]: nc.dram_tensor(k, v.shape, mybir.dt.from_np(v.dtype), kind="ExternalInput").ap()
            for k, v in arrays.items()}
    out = nc.dram_tensor("out", _OUT, f32, kind="ExternalOutput").ap()
    build(nc, out=out, **args)
    r = run_bass_kernel_spmd(nc, [arrays], core_ids=[0])
    return r.results[0]["out"]
```

```python
import concourse.bass as bass
from concourse import mybir
from contextlib import ExitStack

f32 = mybir.dt.float32
i32 = mybir.dt.int32
u32 = mybir.dt.uint32
u8 = mybir.dt.uint8
ALU = mybir.AluOpType
ACT = mybir.ActivationFunctionType
AX = mybir.AxisListType.X
ds = bass.ds

N, D, E, P = 6250, 256, 100000, 128
B = -(-N // P)
NP = B * P
U = 6
UH = U // 2
UW = 18
UG = 6
UD = 4
T = 800
TG = 7
ROW = 264
BK = B + 1
R0, REL = 8, 8
E1 = 6
CB = 7
CN = CB * P
HN = CN // 2
NC = B // CB
BIG = 1024
EPS = 1e-5
DST, SRC, DST_W = 0, 1, 2
PER_ROUND = (U, UW, UW)
ROUNDS_AT, BEFORE_AT = 10, 18
C_IOTA, C_ID, C_TRI, C_ONE, C_ZERO = 0, 128, 256, 384, 512
C_NODE, C_NEG, C_BLK, C_I8, C_REV, C_NEXT, C_N = 768, 817, 867, 917, 925, 932, 939
K_B, K_B1, K_F0, K_R1, K_X1, K_X2, K_N = 0, 2, 4, 20, 21, 33, 45
SQH = 0.5 ** 0.5


def build(nc, x, src_t, dst_t, type_t, weight_t, dst_rows, consts, shifted, bias_cols,
          gnn_w, gnn_w1, gnn_w2, gnn_b2, f0_router, f0_w1, f0_w2, f0_b2,
          rel_w, loop_w, h_bias, f1_rw1, f1_rw2, f1_rb2, f1_w1, f1_w2, f1_w3, f1_b3, out):
    ctx = ExitStack()
    with ctx:
        def sb(name, shape, dt=f32):
            return ctx.enter_context(nc.sbuf_tensor(name, shape, dt))

        def sem(name):
            return ctx.enter_context(nc.semaphore(name))

        def sems(name, n):
            return [sem(f"{name}{i}") for i in range(n)]

        msgs = nc.dram_tensor("msgs_sorted", [T * P, ROW], f32, kind="Internal").ap()
        hx = nc.dram_tensor("hx_rows", [NP * REL, D], f32, kind="Internal").ap()

        X = sb("X", [P, B, D])
        R1 = sb("R1", [P, B * D])
        R2 = sb("R2", [P, B * D])
        R3 = sb("R3", [P, 7168])
        C = sb("C", [P, C_N])
        GW = sb("GW", [P, 4 * 512])
        KC = sb("KC", [P, K_N])
        blk_shift = sb("blk_shift", [P, BK], i32)
        dstf = sb("dstf", [P, T])
        gidx = sb("gidx", [P, T], u32)
        blkD = sb("blkD", [P, T], i32)
        tab = sb("tab", [1, 3 * BK], i32)
        stat6 = sb("stat6", [P, B, 6])
        mv = sb("mv", [P, B, 2])
        rstd = sb("rstd", [P, B])
        nmr = sb("nmr", [P, B])
        dinv = sb("dinv", [P, B])
        sc1 = sb("sc1", [P, B])
        sc2 = sb("sc2", [P, B])
        idx = sb("idx", [P, UW], u32)
        iota, ident, tri = C[:, C_IOTA:C_IOTA + P], C[:, C_ID:C_ID + P], C[:, C_TRI:C_TRI + P]
        ones, zeros = C[:, C_ONE:C_ONE + P], C[:, C_ZERO:C_ZERO + D]

        XS = R1[:, :].rearrange("p (b d) -> p b d", d=D)
        AG = R2[:, :].rearrange("p (b d) -> p b d", d=D)
        XT = R2[:, :].rearrange("p (k n) -> p k n", k=2)
        src_i = R1[:, 0:T].bitcast(i32)
        dst_i = R1[:, T:2 * T].bitcast(i32)
        typ_i = R1[:, 2 * T:3 * T].bitcast(i32)
        tmp_i = R1[:, 3 * T:4 * T].bitcast(i32)
        blkS = R1[:, 4 * T:5 * T]
        loS = R1[:, 5 * T:6 * T]
        pos1 = R1[:, 6 * T:7 * T]
        tmp_f = R1[:, 7 * T:8 * T]
        drow_i = R1[:, 8 * T:8 * T + TG * P].bitcast(i32)
        OHB = R2[:, 0:BK * T // 4].bitcast(u8).rearrange("p (b t) -> p b t", b=BK)
        o = BK * T // 4
        wts, srcf, pos_i = R2[:, o:o + T], R2[:, o + T:o + 2 * T], R2[:, o + 2 * T:o + 3 * T].bitcast(i32)
        WOH = R3[:, 0:8 * P].rearrange("p (s n) -> p s n", s=8)
        OHHI = R3[:, 1024:1024 + 2 * UD * B].rearrange("p (h s n) -> p h s n", h=2, s=UD)
        junk = R3[:, 1500:1500 + T]
        tot = R3[:, 2400:2400 + BK]
        cum = R3[:, 2450:2450 + BK]
        exc = R3[:, 2500:2500 + BK]
        base = R3[:, 2550:2550 + BK]
        tmn = R3[:, 2600:2600 + TG]
        tmx = R3[:, 2607:2607 + TG]
        tmn_i = R3[:, 2614:2614 + TG].bitcast(i32)
        tmx_i = R3[:, 2621:2621 + TG].bitcast(i32)
        ge = R3[:, 2640:2640 + B * TG].rearrange("p (b g) -> p b g", g=TG)
        le = R3[:, 3000:3000 + B * TG].rearrange("p (b g) -> p b g", g=TG)
        inb = R3[:, 3400:3400 + B * TG].rearrange("p (b g) -> p b g", g=TG)
        two = R3[:, 3800:3800 + 2 * B].rearrange("p (a b) -> p a b", a=2)
        ext = R3[0:B, 3900:3902]
        rowf = R3[0:1, 4000:4000 + 8 * BK].rearrange("p (a b) -> p a b", a=8)
        rowi = R3[0:1, 4500:4500 + 8 * BK].bitcast(i32).rearrange("p (a b) -> p a b", a=8)
        dst_bc = R3[:, 0:U * P].bitcast(i32).rearrange("p (s n) -> p s n", s=U)
        oneh = R3[:, 1024:1024 + U * P].rearrange("p (s n) -> p s n", s=U)
        msg = R3[:, 2304:2304 + U * ROW].rearrange("p (s n) -> p s n", s=U)
        oneh_w = R3[:, 0:UW * P].rearrange("p (s n) -> p s n", s=UW)
        back = R3[:, UW * P:UW * (P + ROW)].rearrange("p (s n) -> p s n", s=UW)
        TC = [R3[:, 1792 * i:1792 * (i + 1)].rearrange("p (k n) -> p k n", k=2) for i in range(3)]
        head_in = R3[:, 5376:5376 + CB * D].rearrange("p (s d) -> p s d", s=CB)
        xn = R3[:, 0:4 * D].rearrange("p (s d) -> p s d", s=4)
        xts = R3[:, 1024:1024 + CB * D].rearrange("p (s k n) -> p s k n", s=CB, k=2)
        hxs = R3[:, 2816:2816 + 2 * REL * D].rearrange("p (s n) -> p s n", s=2)
        def route(i):
            return R3[:, 2900 + 400 * i:2900 + 400 * i + B * 8].rearrange("p (b e) -> p b e", e=8)

        lg, pr, eq1, eq2, top = (route(i) for i in range(5))
        top_i = route(5).bitcast(u32)
        top_f = route(6)
        rmax, rsum = R3[:, 5800:5800 + B], R3[:, 5850:5850 + B]
        g12 = R3[:, 5900:5900 + 2 * B].rearrange("p (a b) -> p a b", a=2)
        comb_s = R3[0:8, 6100:6100 + CB * P].rearrange("p (s n) -> p s n", s=CB)
        HT = [R3[:, 2 * CN * i:2 * CN * (i + 1)].rearrange("p (k n) -> p k n", k=2) for i in range(4)]
        W0 = R1[:, 0:R0 * 1024].rearrange("p (e m k o) -> p e m k o", e=R0, m=2, k=2)
        WR = R1[:, R0 * 1024:R0 * 1024 + 2 * REL * D].rearrange("p (k n) -> p k n", k=2)
        W1 = R1[:, 0:E1 * 1536].rearrange("p (e m k o) -> p e m k o", e=E1, m=3, k=2)
        rows_in = R2[:, 0:UW * D].rearrange("p (s d) -> p s d", s=UW)
        oneh_l = R2[:, 4608:4608 + UW * P].rearrange("p (s n) -> p s n", s=UW)
        x_norm = R2[:, 6912:6912 + D]
        x_turned = R2[:, 7168:7168 + 2 * D]
        H1 = R2[:, 7680:7680 + 2 * D].rearrange("p (s k n) -> p s k n", s=2, k=2)
        H2 = R2[:, 8192:8192 + 2 * D].rearrange("p (s k n) -> p s k n", s=2, k=2)
        router_h = R2[:, 8704:8704 + P]
        stat1, mv1 = R2[:, 8832:8838], R2[:, 8840:8842]
        rstd1, nmr1 = R2[:, 8844:8845], R2[:, 8845:8846]
        neg_max, prob_sum, neg_top, gate_sum = (R2[:, 8848 + i:8849 + i] for i in range(4))
        prob, top1, top1_f, eq_a, eq_b, comb1 = (R2[:, 8856 + 8 * i:8864 + 8 * i] for i in range(6))
        top1_i = R2[:, 8904:8912].bitcast(u32)
        gates = R2[:, 8912:8914]
        comb1_s = R2[0:8, 9000:9000 + P]
        comb = sb("comb", [P, B, 8])
        HB = sb("HB", [P, D])
        RW = sb("RW", [P, 2, 8])
        RW1 = sb("RW1", [P, 2, P])
        RW2 = sb("RW2", [P, E1])
        brow = sb("brow", [8, 2 * D])
        srow = sb("srow", [1, D + 8])
        PS = ctx.enter_context(nc.psum_tensor("PS", [P, 8, 512], f32))
        PB = [PS[:, i, :] for i in range(8)]
        scanp = [PS[:, i:i + 2, :].rearrange("p a n -> p (a n)")[:, 0:T] for i in (3, 6)]
        aggp = PS[:, 6:8, :]
        tail = (T * P - E) * ROW // 48
        zero_rows = R3[0:48, 4900:4900 + tail // U]

        phase_done = sem("phase_done")
        phases = {}

        def phase_end(e):
            k = phases[id(e)] = phases.get(id(e), 0) + 1
            e.drain().then_inc(phase_done, 1)
            e.wait_ge(phase_done, 5 * k)

        class Chain:

            def __init__(self, e, s):
                self.e, self.s, self.base, self.n = e, s, 0, 0

            def link(self, ins):
                ins.then_inc(self.s, 1)
                self.n += 1
                self.e.wait_ge(self.s, self.base + self.n)

            def pause(self):
                self.e.sem_inc(pauses, 1)

            def loop(self, i, per):
                self.start, self.per = self.base + self.n, per
                self.base, self.n = self.start + i * per, 0

            def loop_end(self, count):
                assert self.n == self.per, (self.n, self.per)
                self.base, self.n = self.start + count * self.per, 0

        pauses, loads_begun = sem("pauses"), sem("loads_begun")
        dve_step, act_step, pool_step = sem("dve_step"), sem("act_step"), sem("pool_step")

        def block_row(e, which, b):
            row = e.value_load(tab[0:1, ds(b + BK * which, 1)], min_val=0, max_val=2 ** 31 - 1)
            why = "the fields of a table's entry"
            return (nc.s_assert_within(e.snap(row & 1023), 0, T - 1, skip_runtime_bounds_check_because=why),
                    nc.s_assert_within(e.snap((row >> ROUNDS_AT) & 255), 1, T, skip_runtime_bounds_check_because=why),
                    nc.s_assert_within(e.snap(row >> BEFORE_AT), 0, B * T, skip_runtime_bounds_check_because=why))

        def this_round(e, which, lo, before, j):
            why = "rounds are cut so that a block's last one begins at its last tile or before"
            return (nc.s_assert_within(e.snap(lo + j * PER_ROUND[which]), 0, T - PER_ROUND[which],
                                       skip_runtime_bounds_check_because=why),
                    e.snap((before + j) * PER_ROUND[which]), e.snap((before + j) * 16))

        def all_rounds(e, which):
            row = e.value_load(tab[0:1, BK * which + B:BK * which + B + 1], min_val=0, max_val=2 ** 31 - 1)
            return nc.s_assert_within(e.snap(row >> BEFORE_AT), B, B * T,
                                      skip_runtime_bounds_check_because="a round per block or more")

        in_const, in_edge, in_dst, in_rows = sem("in_const"), sem("in_edge"), sem("in_dst"), sem("in_rows")
        in_x, in_gw, brow_clear = sem("in_x"), sem("in_gw"), sem("brow_clear")
        low_made, low_used = sem("low_made"), sem("low_used")
        high_made = sems("high_made", 2)
        keys_ready, bucket_rows, bucket_tot, totals_ready, bases_ready = (
            sem("keys_ready"), sem("bucket_rows"), sem("bucket_tot"), sem("totals_ready"), sem("bases_ready"))
        deg_ready, ext_ready, ext_t, ext2_ready, ext2_t = (
            sem("deg_ready"), sem("ext_ready"), sem("ext_t"), sem("ext2_ready"), sem("ext2_t"))
        root_in, root_out, scales_ready = sem("root_in"), sem("root_out"), sem("scales_ready")
        dst_in, oht_made, exp_done = sems("dst_in", 2), sem("oht_made"), sem("exp_done")
        msg_made, idx_made, scattered = sem("msg_made"), sem("idx_made"), sems("scattered", U)
        row_in, oh_made, row_used, cleared = sems("row_in", UW // UG), sem("oh_made"), sem("row_used"), sem("cleared")
        rows_written, sends_begun, gathers_begun = sem("rows_written"), sem("sends_begun"), sem("gathers_begun")
        in_w0, in_w1, in_small = sem("in_w0"), sem("in_w1"), sem("in_small")
        agg_made, head_mm, head_moved, head_y, head_added = (
            sem("agg_made"), sem("head_mm"), sem("head_moved"), sem("head_y"), sem("head_added"))
        norm_made, slot_read, turned, turn_moved, slot_moved = (
            sem("norm_made"), sem("slot_read"), sem("turned"), sem("turn_moved"), sem("slot_moved"))
        exp_in, exp_out, comb_ready = sem("exp_in"), sem("exp_out"), sem("comb_ready")
        comb_t, comb_moved, bias_mm, bias_added = sem("comb_t"), sem("comb_moved"), sem("bias_mm"), sem("bias_added")
        hid_mm, hid_moved, y_mm, y_added = sem("hid_mm"), sem("hid_moved"), sem("y_mm"), sem("y_added")
        hid1_mm, hid1_moved, y1_mm, y1_added = sem("hid1_mm"), sem("hid1_moved"), sem("y1_mm"), sem("y1_added")
        pair_mm, pair_act, pair_dve, loop_mm, loop_added = (
            sem("pair_mm"), sem("pair_act"), sem("pair_dve"), sem("loop_mm"), sem("loop_added"))
        hx_out, hx_freed = sem("hx_out"), sem("hx_freed")
        gidx_made, got, oh2_made, row2_used = sem("gidx_made"), sems("got", UW), sem("oh2_made"), sem("row2_used")
        agg_added, agg2_added = sem("agg_added"), sem("agg2_added")
        var1_made, dev1_made = sem("var1_made"), sem("dev1_made")
        scales1, norm1_made, turned1, turned1_moved = sem("scales1"), sem("norm1_made"), sem("turned1"), sem("turned1_moved")
        rh_mm, rh_moved, logits1, max_made, probs_made, tops_made, gates_made = (
            sem("rh_mm"), sem("rh_moved"), sem("logits1"), sem("max_made"), sem("probs_made"), sem("tops_made"), sem("gates_made"))
        comb1_ready, comb1_t, comb1_moved, bias1_mm, bias1_added = (
            sem("comb1_ready"), sem("comb1_t"), sem("comb1_moved"), sem("bias1_mm"), sem("bias1_added"))
        out_done = sem("out_done")

        def turn_bank(s):
            return PB[s % 2][:, 0:D].rearrange("p (k n) -> p k n", k=2)

        HIDDEN1 = [(0, 0)] + [x for e in range(E1) for x in ([(0, e + 1)] if e + 1 < E1 else []) + [(1, e)]]
        PE_TURN, PE_HIDDEN, PE_LOGITS = 3, 5, 6
        ACT_NORM, ACT_TURNED, ACT_HIDDEN, ACT_PROBS, ACT_GATES = 2, 4, 6, 8, 10

        dst_line = dst_rows.rearrange("(o t) e -> o (t e)", o=1)

        block = ctx.enter_context(nc.Block())

        @block.sync
        def _(sp):
            for to, of in ((C[:, :], consts), (blk_shift[:, :], shifted), (KC[:, :], bias_cols)):
                sp.dma_start(to, of).then_inc(in_const, 16)
            sp.dma_start(src_i, src_t).then_inc(in_edge, 16)
            sp.dma_start(wts, weight_t).then_inc(in_edge, 16)
            sp.dma_start(drow_i.rearrange("p (g e) -> p g e", g=TG),
                         dst_rows.rearrange("(g p) e -> p g e", p=P)).then_inc(in_rows, 16)
            sp.dma_start(dst_i, dst_t).then_inc(in_dst, 16)
            sp.dma_start(typ_i, type_t).then_inc(in_dst, 16)
            for c in range(NC):
                sp.dma_start(X[:, c * CB:(c + 1) * CB, :],
                             x[c * CN:(c + 1) * CN, :].rearrange("(b p) d -> p b d", p=P)).then_inc(in_x, 16)
            sp.dma_start(RW[:, :, :], f0_router.rearrange("(k p) e -> p k e", p=P)).then_inc(in_small, 16)
            sp.dma_start(RW1[:, :, :], f1_rw1.rearrange("(k p) e -> p k e", p=P)).then_inc(in_small, 16)
            sp.dma_start(RW2[:, :], f1_rw2).then_inc(in_small, 16)
            sp.dma_start(brow[:, 0:D], f0_b2).then_inc(in_small, 16)
            sp.wait_ge(brow_clear, 1)
            sp.dma_start(brow[0:E1, D:2 * D], f1_b3).then_inc(in_small, 16)
            sp.dma_start(srow[:, 0:D], gnn_b2).then_inc(in_small, 16)
            sp.dma_start(srow[:, D:D + E1], f1_rb2).then_inc(in_small, 16)
            sp.dma_start(HB[:, :], h_bias.broadcast_to([P, D])).then_inc(in_small, 16)
            for i, w in enumerate((gnn_w, gnn_w1, gnn_w2, loop_w)):
                sp.dma_start(GW[:, 512 * i:512 * (i + 1)].rearrange("p (k o) -> p k o", k=2),
                             w.rearrange("(k p) o -> p k o", p=P)).then_inc(in_gw, 16)
            phase_end(sp)
            with sp.Fori(0, B) as b:
                lo, rounds, before = block_row(sp, DST, b)
                with sp.Fori(0, rounds) as j:
                    t0, n, dmas = this_round(sp, DST, lo, before, j)
                    for h in range(2):
                        edge = sp.snap((t0 + UH * h) * P)
                        sp.wait_ge(oht_made, n + UH * (h + 1))
                        sp.sem_inc(loads_begun, 1)
                        sp.dma_start(R3[:, UH * P * h:UH * P * (h + 1)].bitcast(i32),
                                     dst_line[:, ds(edge, UH * P)].broadcast_to([P, UH * P])
                                     ).then_inc(dst_in[h], 16)
            phase_end(sp)
            sp.wait_ge(rows_written, 1)
            with sp.Fori(0, B) as b:
                lo, rounds, before = block_row(sp, SRC, b)
                with sp.Fori(0, rounds) as j:
                    t0, n, dmas = this_round(sp, SRC, lo, before, j)
                    for k in range(UW // UG):
                        row = sp.snap((t0 + UG * k) * P)
                        sp.wait_ge(row_used, n + UG * (k + 1))
                        sp.sem_inc(loads_begun, 1)
                        sp.dma_start(back[:, UG * k:UG * (k + 1), :],
                                     msgs[ds(row, UG * P), :].rearrange("(s p) c -> p s c", p=P)
                                     ).then_inc(row_in[k], 16)
            phase_end(sp)
            phase_end(sp)
            for e in range(R0):
                for m, w in enumerate((f0_w1, f0_w2)):
                    sp.dma_start(W0[:, e, m, :, :], w[e, :, :].rearrange("(k p) o -> p k o", p=P)).then_inc(in_w0, 16)
            for rel in range(REL):
                sp.dma_start(WR[:, :, rel * D:(rel + 1) * D],
                             rel_w[rel, :, :].rearrange("(k p) o -> p k o", p=P)).then_inc(in_w0, 16)
            phase_end(sp)
            phase_end(sp)
            with sp.Fori(0, NC) as c:
                for s in range(CB):
                    sp.wait_ge(pair_act, c * (2 * CB) + 2 * s + 4)
                    sp.wait_ge(pair_dve, c * (2 * CB) + 2 * s + 4)
                    sp.dma_start(hx[ds((c * CB + s) * (P * REL), P * REL), :].rearrange("(p r) d -> p (r d)", r=REL),
                                 hxs[:, s % 2, :]).then_inc(hx_out, 16)
                    sp.wait_ge(hx_out, c * (16 * CB) + 16 * s + 16)
                    sp.sem_inc(hx_freed, 1)
            phase_end(sp)
            for e in range(E1):
                for m, w in enumerate((f1_w1, f1_w2, f1_w3)):
                    sp.dma_start(W1[:, e, m, :, :], w[e, :, :].rearrange("(k p) o -> p k o", p=P)).then_inc(in_w1, 16)
            full = N // P
            with sp.Fori(0, full) as b:
                sp.wait_ge(y1_added, b * E1 + (2 + E1))
                sp.dma_start(out[ds(b * P, P), :], X[:, ds(b, 1), :]).then_inc(out_done, 16)
            sp.wait_ge(y1_added, B * E1 + 2)
            sp.dma_start(out[full * P:N, :], X[0:N - full * P, full, :]).then_inc(out_done, 16)
            sp.wait_ge(out_done, 16 * (full + 1))

        @block.gpsimd
        def _(pool):
            nc.gpsimd.memset(brow[:, D:2 * D], 0.0).then_inc(brow_clear, 1)
            nc.gpsimd.memset(zero_rows, 0.0).then_inc(pool_step, 1)
            pool.wait_ge(pool_step, 1)
            rest = msgs[E:T * P, :].rearrange("(p r) c -> p (r c)", p=48)
            for u in range(U):
                pool.dma_start(rest[:, tail // U * u:tail // U * (u + 1)], zero_rows).then_inc(scattered[u], 16)
            phase_end(pool)
            last_row = pool.to_reg(T * P - 1)
            with pool.Fori(0, B) as b:
                lo, rounds, before = block_row(pool, DST, b)
                with pool.Fori(0, rounds) as j:
                    t0, n, dmas = this_round(pool, DST, lo, before, j)
                    for u in range(U):
                        pool.wait_ge(msg_made, n + U + u + 1)
                        pool.wait_ge(idx_made, n + u + 1)
                        pool.sem_inc(sends_begun, 1)
                        pool.indirect_dma_start(
                            msgs, bass.IndirectOffsetOnAxis(ap=idx[:, u:u + 1], axis=0), msg[:, u, :], None,
                            bounds_check=last_row, oob_is_err=False).then_inc(scattered[u], 16)
            rounds = all_rounds(pool, DST)
            for u in range(U):
                pool.wait_ge(scattered[u], rounds * 16 + 16)
            pool.sem_inc(rows_written, 1)
            phase_end(pool)
            for c in range(NC):
                nc.gpsimd.memset(AG[:, c * CB:(c + 1) * CB, :], 0.0).then_inc(cleared, CB)
            phase_end(pool)
            phase_end(pool)
            phase_end(pool)
            phase_end(pool)
            phase_end(pool)
            with pool.Fori(0, B) as b:
                lo, rounds, before = block_row(pool, DST_W, b)
                with pool.Fori(0, rounds) as j:
                    t0, n, dmas = this_round(pool, DST_W, lo, before, j)
                    made = pool.snap((before + j) * (UW // UG))
                    for u in range(UW):
                        if u % UG == 0:
                            pool.wait_ge(row2_used, n + u + UG)
                            nc.gpsimd.tensor_copy(idx[:, u:u + UG], gidx[:, ds(t0 + u, UG)]).then_inc(gidx_made, 1)
                            pool.wait_ge(gidx_made, made + u // UG + 1)
                            pool.sem_inc(gathers_begun, 1)
                        pool.indirect_dma_start(
                            rows_in[:, u, :], None, hx, bass.IndirectOffsetOnAxis(ap=idx[:, u:u + 1], axis=0),
                            ).then_inc(got[u], 16)

        @block.scalar
        def _(act):
            for b in range(BK):
                act.wait_ge(bucket_rows, b + 1)
                if b:
                    act.wait_ge(bucket_tot, b)
                nc.scalar.activation(junk, OHB[:, b, :], ACT.Identity,
                                     accum_out=tot[:, b:b + 1]).then_inc(bucket_tot, 1)
            act.wait_ge(root_in, 1)
            nc.scalar.activation(sc1[:, :], sc1[:, :], ACT.Sqrt)
            nc.scalar.activation(rstd[:, :], rstd[:, :], ACT.Sqrt).then_inc(root_out, 1)
            act.wait_ge(scales_ready, 1)
            phase_end(act)
            with act.Fori(0, B) as b:
                lo, rounds, before = block_row(act, DST, b)
                with act.Fori(0, rounds) as j:
                    t0, n, dmas = this_round(act, DST, lo, before, j)
                    for u in range(U):
                        act.wait_ge(scattered[u], dmas + 16)
                        nc.scalar.activation(msg[:, u, D:D + 1], srcf[:, ds(t0 + u, 1)], ACT.Copy)
                        act.wait_ge(exp_done, n + U + u + 1)
                        nc.scalar.activation(msg[:, u, 0:D], PB[u][:, 0:D], ACT.Copy,
                                             scale=wts[:, ds(t0 + u, 1)]).then_inc(msg_made, 1)
            phase_end(act)
            phase_end(act)
            with act.Fori(0, NC) as c:
                for i in range(CB):
                    act.wait_ge(head_mm, c * 15 + i + 1)
                    nc.scalar.activation(TC[0][:, :, i * P:(i + 1) * P],
                                         PB[i % 4][:, 0:D].rearrange("p (k n) -> p k n", k=2),
                                         ACT.Copy).then_inc(head_moved, 1)
                for layer, (func, k0) in enumerate(((ACT.Identity, K_B), (ACT.Relu, K_B1))):
                    for q in range(4):
                        half, m = divmod(q, 2)
                        act.wait_ge(head_mm, c * 15 + CB + 4 * layer + q + 1)
                        nc.scalar.activation(TC[layer + 1][:, m, half * HN:(half + 1) * HN],
                                             PB[4 - 4 * layer + q][:, 0:HN], func,
                                             bias=KC[:, k0 + m:k0 + m + 1]).then_inc(head_moved, 1)
            phase_end(act)

            def roots(k):
                act.wait_ge(root_in, k + 1)
                nc.scalar.activation(rstd[:, :], rstd[:, :], ACT.Sqrt).then_inc(root_out, 1)

            def normalise(k, xt):
                act.wait_ge(scales_ready, k + 1)

                def to_xt(c, s):
                    act.wait_ge(slot_moved, c * CB + (k - 1) * B + s + 4)
                    nc.scalar.activation(XT[:, :, ds((c * CB + s) * P, P)], xts[:, s, :, :],
                                         ACT.Copy).then_inc(turn_moved, 1)

                with act.Fori(0, NC) as c:
                    for s in range(CB):
                        act.wait_ge(slot_moved, c * CB + (k - 1) * B + s + 1)
                        nc.scalar.activation(xn[:, s % 4, :], X[:, ds(c * CB + s, 1), :], ACT.Identity,
                                             bias=nmr[:, ds(c * CB + s, 1)],
                                             scale=rstd[:, ds(c * CB + s, 1)]).then_inc(norm_made, 1)
                        if xt and s:
                            to_xt(c, s - 1)
                        if k == 2:
                            if s:
                                pairs(c, s - 1)
                    if xt:
                        to_xt(c, CB - 1)
                    if k == 2:
                        pairs(c, CB - 1)

            def pairs(c, s):
                act.wait_ge(hx_freed, c * CB + s + (2 if s == 0 else 1))
                for q in (0, 2):
                    act.wait_ge(pair_mm, c * (4 * CB) + 4 * s + q + 1)
                    nc.scalar.activation(hxs[:, s % 2, q * 512:(q + 1) * 512], PB[2 + q][:, :],
                                         ACT.Copy).then_inc(pair_act, 1)

            roots(1)
            normalise(1, True)
            act.wait_ge(exp_in, 1)
            nc.scalar.activation(pr, pr, ACT.Exp).then_inc(exp_out, 1)
            phase_end(act)
            with act.Fori(0, NC) as c:
                for e in range(R0):
                    for q in range(4):
                        half, m = divmod(q, 2)
                        act.wait_ge(hid_mm, c * (4 * R0) + 4 * e + q + 1)
                        nc.scalar.activation(HT[e % 2][:, m, half * HN:(half + 1) * HN], PB[q][:, 0:HN], ACT.Gelu,
                                             bias=KC[:, K_F0 + 2 * e + m:K_F0 + 2 * e + m + 1]).then_inc(hid_moved, 1)
            phase_end(act)
            roots(2)
            normalise(2, False)
            phase_end(act)
            def norm1(b):
                act.wait_ge(var1_made, b + 1)
                nc.scalar.activation(rstd1, rstd1, ACT.Sqrt).then_inc(dev1_made, 1)
                act.wait_ge(scales1, b + 1)
                nc.scalar.activation(x_norm, X[:, ds(b, 1), :], ACT.Identity, bias=nmr1,
                                     scale=rstd1).then_inc(norm1_made, 1)

            def turned1_out(b):
                act.wait_ge(turned1, b + 1)
                nc.scalar.activation(x_turned[:, ds(b % 2 * D, D)], PB[1][:, 0:D], ACT.Copy).then_inc(turned1_moved, 1)

            def router_hidden(b):
                act.wait_ge(rh_mm, b + 1)
                nc.scalar.activation(router_h, PB[2][:, 0:P], ACT.Relu,
                                     bias=KC[:, K_R1:K_R1 + 1]).then_inc(rh_moved, 1)

            def probs(b):
                act.wait_ge(max_made, b + 1)
                nc.scalar.activation(prob[:, 0:E1], PB[1][:, 0:E1], ACT.Exp, bias=neg_max,
                                     accum_out=prob_sum).then_inc(probs_made, 1)

            def gate_exps(b):
                act.wait_ge(tops_made, b + 1)
                nc.scalar.activation(gates, top1[:, 0:2], ACT.Exp, bias=neg_top,
                                     accum_out=gate_sum).then_inc(gates_made, 1)

            stages = {ACT_NORM: norm1, ACT_TURNED: turned1_out, ACT_HIDDEN: router_hidden, ACT_PROBS: probs,
                      ACT_GATES: gate_exps}

            def hidden1(before, b):
                for at, (layer, e) in enumerate(HIDDEN1):
                    for m in range(2):
                        k0 = (K_X1, K_X2)[layer] + 2 * e + m
                        i = 2 * at + m
                        act.wait_ge(hid1_mm, before * (4 * E1) + i + 1)
                        nc.scalar.activation((H1, H2)[layer][:, e % 2, m, :], PB[3 + i % 3][:, 0:P], ACT.Relu,
                                             bias=KC[:, k0:k0 + 1]).then_inc(hid1_moved, 1)
                    if b is not None and at in stages:
                        stages[at](b)

            for at in sorted(stages):
                stages[at](0)
            with act.Fori(0, B - 1) as b:
                hidden1(b, b + 1)
            hidden1(B - 1, None)

        @block.vector
        def _(dve):
            ch = Chain(dve, dve_step)
            for s, n in ((low_used, 8), (oht_made, U), (exp_done, U), (msg_made, U), (row_used, UW),
                         (row2_used, UW), (agg_added, 1), (agg2_added, 1), (head_added, 1), (slot_moved, 3), (hid_moved, 4),
                         (hid1_moved, 3), (y_added, 4), (y1_added, 2), (hx_freed, 2), (loop_added, 1),
                         (comb_moved, 2), (bias_added, 2), (bias1_added, 1), (turn_moved, CB), (slot_read, CB),
                         (pair_act, 2), (pair_dve, 2)):
                dve.sem_inc(s, n)
            dve.wait_ge(in_edge, 32)
            nc.vector.tensor_copy(srcf, src_i)
            ch.link(nc.vector.tensor_scalar(tmp_i, src_i, 7, None, ALU.arith_shift_right))
            ch.link(nc.vector.tensor_copy(blkS, tmp_i))
            ch.link(nc.vector.tensor_scalar(tmp_i, src_i, 127, None, ALU.bitwise_and))
            nc.vector.tensor_copy(loS, tmp_i).then_inc(keys_ready, 1)
            dve.wait_ge(keys_ready, 1)
            for b in range(BK):
                nc.vector.tensor_scalar(OHB[:, b, :], blkS, float(b), None, ALU.is_equal).then_inc(bucket_rows, 1)
            dve.wait_ge(in_const, 48)
            with dve.Fori(0, T // 8) as i:
                for s in range(8):
                    dve.wait_ge(low_used, i * 8 + s + 1)
                    if s % UD == 0:
                        dve.wait_ge(low_used, i * 8 + s + UD)
                        nc.vector.tensor_tensor(
                            OHHI[:, s // UD, :, :],
                            blkS[:, ds(i * 8 + s, UD)].unsqueeze(2).broadcast_to([P, UD, B]),
                            C[:, C_BLK:C_BLK + B].unsqueeze(1).broadcast_to([P, UD, B]),
                            ALU.is_equal).then_inc(high_made[s // UD], 1)
                    nc.vector.tensor_scalar(WOH[:, s, :], iota, loS[:, ds(i * 8 + s, 1)], wts[:, ds(i * 8 + s, 1)],
                                            ALU.is_equal, ALU.mult).then_inc(low_made, 1)
            dve.wait_ge(bucket_tot, BK)
            ch.link(nc.vector.tensor_tensor_scan(cum, tot, tot, 0.0, ALU.add, ALU.max))
            nc.vector.tensor_tensor(exc, cum, tot, ALU.subtract).then_inc(totals_ready, 1)
            for c in range(NC):
                dve.wait_ge(in_x, 16 * NC)
                for b in range(c * CB, (c + 1) * CB):
                    nc.vector.bn_stats(stat6[:, b, :], X[:, b, :]).then_inc(dve_step, 1)
                    ch.n += 1
            dve.wait_ge(dve_step, ch.base + ch.n)
            for b in range(B):
                nc.vector.bn_aggr(mv[:, b, :], stat6[:, b, :]).then_inc(dve_step, 1)
                ch.n += 1
            dve.wait_ge(bases_ready, 1)
            ch.link(nc.vector.tensor_copy(base, PB[1][:, 0:BK]))
            for b in range(BK + 1):
                if b < BK:
                    nc.vector.tensor_tensor_scan(scanp[b % 2], OHB[:, b, :], OHB[:, b, :], base[:, b:b + 1],
                                                 ALU.add, ALU.max).then_inc(dve_step, 1)
                    ch.n += 1
                if b:
                    dve.wait_ge(dve_step, ch.base + ch.n - (1 if b < BK else 0))
                    ch.link(nc.vector.copy_predicated(pos1, OHB[:, b - 1, :], scanp[(b - 1) % 2]))
            nc.vector.tensor_scalar(pos_i, pos1, -1.0, None, ALU.add)
            dve.wait_ge(in_dst, 32)
            nc.vector.tensor_copy(dstf[:, :], dst_i)
            nc.vector.tensor_scalar(blkD[:, :], dst_i, 7, 20, ALU.arith_shift_right, ALU.arith_shift_left)
            ch.link(nc.vector.tensor_scalar(tmp_f, src_i, float(NP - 1), float(REL), ALU.min, ALU.mult))
            nc.vector.tensor_tensor(gidx[:, :], tmp_f, typ_i, ALU.add)
            dve.wait_ge(in_rows, 16)
            rows3 = drow_i.rearrange("p (g e) -> p g e", g=TG)
            ch.link(nc.vector.tensor_reduce(tmn, rows3, AX, ALU.min))
            ch.link(nc.vector.tensor_reduce(tmx, rows3, AX, ALU.max))
            ch.link(nc.vector.tensor_copy(tmn_i, tmn))
            ch.link(nc.vector.tensor_copy(tmx_i, tmx))
            ch.link(nc.vector.tensor_scalar(tmn_i, tmn_i, 7, None, ALU.arith_shift_right))
            ch.link(nc.vector.tensor_scalar(tmx_i, tmx_i, 7, None, ALU.arith_shift_right))
            ch.link(nc.vector.tensor_copy(tmn, tmn_i))
            ch.link(nc.vector.tensor_copy(tmx, tmx_i))
            blks = C[:, C_BLK:C_BLK + B].unsqueeze(2).broadcast_to([P, B, TG])
            ch.link(nc.vector.tensor_tensor(ge, blks, tmn.unsqueeze(1).broadcast_to([P, B, TG]), ALU.is_ge))
            ch.link(nc.vector.tensor_tensor(le, blks, tmx.unsqueeze(1).broadcast_to([P, B, TG]), ALU.is_le))
            ch.link(nc.vector.tensor_tensor(inb, ge, le, ALU.mult))
            ch.link(nc.vector.tensor_tensor(ge, inb, C[:, C_REV:C_REV + TG].unsqueeze(1).broadcast_to([P, B, TG]), ALU.mult))
            ch.link(nc.vector.tensor_tensor(le, inb, C[:, C_NEXT:C_NEXT + TG].unsqueeze(1).broadcast_to([P, B, TG]), ALU.mult))
            ch.link(nc.vector.tensor_reduce(two[:, 0, :], ge, AX, ALU.max))
            nc.vector.tensor_reduce(two[:, 1, :], le, AX, ALU.max).then_inc(ext_ready, 1)
            dve.wait_ge(ext_t, 1)
            ch.link(nc.vector.tensor_reduce(ext[:, 0:1], PB[5][0:B, 0:P], AX, ALU.max))
            nc.vector.tensor_reduce(ext[:, 1:2], PB[5][0:B, P:2 * P], AX, ALU.max).then_inc(ext2_ready, 1)
            dve.wait_ge(ext2_t, 1)
            ch.link(nc.vector.tensor_scalar(rowf[:, 0, 0:B], PB[5][0:1, 256:256 + B], -1.0, float(BIG), ALU.mult, ALU.add))
            ch.link(nc.vector.tensor_scalar(rowf[:, 0, 0:B], rowf[:, 0, 0:B], float(E // P), None, ALU.min))
            ch.link(nc.vector.tensor_tensor(rowf[:, 1, 0:B], PB[5][0:1, 384:384 + B], rowf[:, 0, 0:B], ALU.subtract))
            ch.link(nc.vector.tensor_copy(rowi[:, 0, :], PB[2][0:1, 0:BK]))
            ch.link(nc.vector.tensor_scalar(rowf[:, 4, 0:B], PB[2][0:1, 1:BK], -1.0, 0.0, ALU.add, ALU.max))
            ch.link(nc.vector.tensor_copy(rowi[:, 1, 0:B], rowf[:, 4, 0:B]))
            ch.link(nc.vector.tensor_scalar(rowi[:, 2, 0:B], rowi[:, 0, 0:B], 7, None, ALU.arith_shift_right))
            ch.link(nc.vector.tensor_scalar(rowi[:, 3, 0:B], rowi[:, 1, 0:B], 7, None, ALU.arith_shift_right))
            ch.link(nc.vector.tensor_copy(rowf[:, 2, 0:B], rowi[:, 2, 0:B]))
            ch.link(nc.vector.tensor_tensor(rowf[:, 3, 0:B], rowi[:, 3, 0:B], rowi[:, 2, 0:B], ALU.subtract))
            ch.link(nc.vector.tensor_scalar(rowf[:, 3, 0:B], rowf[:, 3, 0:B], 1.0, None, ALU.add))
            for which, at in ((DST, 0), (SRC, 2), (DST_W, 0)):
                per = PER_ROUND[which]
                first, tiles = rowf[:, at, 0:B], rowf[:, 7, 0:B]
                ch.link(nc.vector.tensor_scalar(tiles, rowf[:, at + 1, 0:B], 1.0, float(per - 1), ALU.max, ALU.add))
                ch.link(nc.vector.tensor_scalar(tiles, tiles, float(-(-65536 // per)), None, ALU.mult))
                ch.link(nc.vector.tensor_copy(rowi[:, 4, 0:B], tiles))
                ch.link(nc.vector.tensor_scalar(rowi[:, 4, 0:B], rowi[:, 4, 0:B], 16, None, ALU.arith_shift_right))
                ch.link(nc.vector.tensor_copy(rowf[:, 5, 0:B], rowi[:, 4, 0:B]))
                ch.link(nc.vector.tensor_tensor_scan(rowf[:, 6, 1:BK], rowf[:, 5, 0:B], rowf[:, 5, 0:B], 0.0,
                                                     ALU.add, ALU.max))
                nc.vector.memset(rowf[:, 6, 0:1], 0.0)
                ch.link(nc.vector.tensor_copy(rowi[:, 5, 0:B], first))
                entry = tab[0:1, BK * which:BK * (which + 1)]
                ch.link(nc.vector.tensor_copy(entry, rowf[:, 6, :]))
                ch.link(nc.vector.tensor_scalar(entry, entry, BEFORE_AT, None, ALU.arith_shift_left))
                ch.link(nc.vector.tensor_scalar(rowi[:, 4, 0:B], rowi[:, 4, 0:B], ROUNDS_AT, None,
                                                ALU.arith_shift_left))
                ch.link(nc.vector.tensor_tensor(entry[:, 0:B], entry[:, 0:B], rowi[:, 4, 0:B], ALU.bitwise_or))
                ch.link(nc.vector.tensor_tensor(entry[:, 0:B], entry[:, 0:B], rowi[:, 5, 0:B], ALU.bitwise_or))
            dve.wait_ge(deg_ready, 1)
            ch.link(nc.vector.tensor_scalar(sc2[:, :], PB[0][:, 0:B], 1.0, None, ALU.add))
            ch.link(nc.vector.tensor_scalar(sc1[:, :], sc2[:, :], 1e-30, None, ALU.max))
            nc.vector.tensor_scalar(rstd[:, :], mv[:, :, 1], EPS, None, ALU.add).then_inc(root_in, 1)
            ch.link(nc.vector.tensor_scalar(sc2[:, :], sc2[:, :], 0.0, None, ALU.is_gt))
            dve.wait_ge(root_out, 1)
            ch.link(nc.vector.reciprocal(sc1[:, :], sc1[:, :]))
            ch.link(nc.vector.tensor_tensor(dinv[:, :], sc1[:, :], sc2[:, :], ALU.mult))
            ch.link(nc.vector.reciprocal(rstd[:, :], rstd[:, :]))
            ch.link(nc.vector.tensor_tensor(sc1[:, :], rstd[:, :], dinv[:, :], ALU.mult))
            ch.link(nc.vector.scalar_tensor_tensor(sc2[:, :], mv[:, :, 0], -1.0, sc1[:, :], ALU.mult, ALU.mult))
            for b in range(B):
                nc.vector.tensor_scalar(XS[:, b, :], X[:, b, :], sc1[:, b:b + 1], sc2[:, b:b + 1], ALU.mult, ALU.add)
            nc.vector.memset(junk[:, 0:1], 0.0).then_inc(scales_ready, 1)
            phase_end(dve)
            nc.vector.memset(msg[:, :, D + 1:ROW], 0.0)
            with dve.Fori(0, B) as b:
                lo, rounds, before = block_row(dve, DST, b)
                with dve.Fori(0, rounds) as j:
                    t0, n, dmas = this_round(dve, DST, lo, before, j)
                    for u in range(U):
                        dve.wait_ge(dst_in[u // UH], dmas + 16)
                        dve.wait_ge(exp_done, n + u + 1)
                        nc.vector.tensor_scalar(oneh[:, u, :], dst_bc[:, u, :], C[:, ds(b + C_NODE, 1)], None,
                                                ALU.is_equal).then_inc(oht_made, 1)
                        dve.wait_ge(scattered[u], dmas + 16)
                        nc.vector.scalar_tensor_tensor(
                            idx[:, u:u + 1].bitcast(i32), blkD[:, ds(t0 + u, 1)], blk_shift[:, ds(b, 1)],
                            pos_i[:, ds(t0 + u, 1)], ALU.bitwise_xor, ALU.bitwise_or).then_inc(idx_made, 1)
            phase_end(dve)
            with dve.Fori(0, B) as b:
                lo, rounds, before = block_row(dve, SRC, b)
                with dve.Fori(0, rounds) as j:
                    t0, n, dmas = this_round(dve, SRC, lo, before, j)
                    for u in range(UW):
                        if u % UG == 0:
                            dve.wait_ge(row_in[u // UG], dmas + 16)
                        dve.wait_ge(row_used, n + u + 1)
                        nc.vector.tensor_scalar(oneh_w[:, u, :], iota, back[:, u, D:D + 1], C[:, ds(b + C_NEG, 1)],
                                                ALU.subtract, ALU.is_equal).then_inc(oh_made, 1)
                    dve.wait_ge(row_used, n + 2 * UW)
                    dve.wait_ge(cleared, b + 1)
                    dve.wait_ge(agg_added, before + j + 1)
                    nc.vector.scalar_tensor_tensor(
                        AG[:, ds(b, 1), :], PB[6][:, 0:D], dinv[:, ds(b, 1)], AG[:, ds(b, 1), :],
                        ALU.mult, ALU.add).then_inc(agg_added, 1)
            phase_end(dve)
            with dve.Fori(0, NC) as c:
                for i in range(CB):
                    nc.vector.scalar_tensor_tensor(
                        head_in[:, i, :], XS[:, ds(c * CB + i, 1), :], dinv[:, ds(c * CB + i, 1)],
                        AG[:, ds(c * CB + i, 1), :], ALU.mult, ALU.add).then_inc(agg_made, 1)
                for i in range(CB):
                    dve.wait_ge(head_y, c * CB + i + 1)
                    nc.vector.tensor_tensor(X[:, ds(c * CB + i, 1), :], X[:, ds(c * CB + i, 1), :],
                                            PB[4 + i % 4][:, 0:D], ALU.add).then_inc(head_added, 1)
            phase_end(dve)

            def statistics(k):
                for b in range(B):
                    nc.vector.bn_stats(stat6[:, b, :], X[:, b, :]).then_inc(dve_step, 1)
                    ch.n += 1
                dve.wait_ge(dve_step, ch.base + ch.n)
                for b in range(B):
                    nc.vector.bn_aggr(mv[:, b, :], stat6[:, b, :]).then_inc(dve_step, 1)
                    ch.n += 1
                dve.wait_ge(dve_step, ch.base + ch.n)
                nc.vector.tensor_scalar(rstd[:, :], mv[:, :, 1], EPS, None, ALU.add).then_inc(root_in, 1)
                dve.wait_ge(root_out, k + 1)
                ch.link(nc.vector.reciprocal(rstd[:, :], rstd[:, :]))
                nc.vector.scalar_tensor_tensor(nmr[:, :], mv[:, :, 0], -1.0, rstd[:, :], ALU.mult,
                                               ALU.mult).then_inc(scales_ready, 1)

            def move_blocks(k, add):
                with dve.Fori(0, NC) as c:
                    for s in range(CB):
                        n = c * CB + (k - 1) * B + s
                        if add:
                            dve.wait_ge(norm_made, n + 1)
                            nc.vector.tensor_tensor(X[:, ds(c * CB + s, 1), :], X[:, ds(c * CB + s, 1), :],
                                                    xn[:, s % 4, :], ALU.add)
                        dve.wait_ge(turned, n + 1)
                        if k == 1:
                            dve.wait_ge(slot_read, n + 1)
                        if k != 2:
                            dve.wait_ge(turn_moved, c * CB + (B if k == 3 else 0) + s + 1)
                        nc.vector.tensor_copy(xts[:, s, :, :], turn_bank(s)).then_inc(slot_moved, 1)
                        if k == 2 and s:
                            pairs(c, s - 1)
                    if k == 2:
                        pairs(c, CB - 1)

            def pairs(c, s):
                dve.wait_ge(hx_freed, c * CB + s + (2 if s == 0 else 1))
                for q in (1, 3):
                    dve.wait_ge(pair_mm, c * (4 * CB) + 4 * s + q + 1)
                    nc.vector.tensor_copy(hxs[:, s % 2, q * 512:(q + 1) * 512], PB[2 + q][:, :]).then_inc(pair_dve, 1)
                dve.wait_ge(loop_mm, c * CB + s + 1)
                nc.vector.scalar_tensor_tensor(X[:, ds(c * CB + s, 1), :], PB[6 + s % 2][:, 0:D], SQH,
                                               X[:, ds(c * CB + s, 1), :], ALU.mult, ALU.add).then_inc(loop_added, 1)

            def softmax_top2(layer, n):
                dve.wait_ge((slot_read, logits1)[layer], (CB, 0)[layer] + B)
                ch.link(nc.vector.tensor_copy(
                    lg[:, :, 0:n], PB[7][:, 0:B * 8].rearrange("p (b e) -> p b e", e=8)[:, :, 0:n]))
                ch.link(nc.vector.tensor_reduce(rmax, lg[:, :, 0:n], AX, ALU.max))
                nc.vector.tensor_tensor(pr[:, :, 0:n], lg[:, :, 0:n], rmax.unsqueeze(2).broadcast_to([P, B, n]),
                                        ALU.subtract).then_inc(exp_in, 1)
                dve.wait_ge(exp_out, layer + 1)
                ch.link(nc.vector.tensor_reduce(rsum, pr[:, :, 0:n], AX, ALU.add))
                ch.link(nc.vector.reciprocal(rsum, rsum))
                ch.link(nc.vector.tensor_tensor(pr[:, :, 0:n], pr[:, :, 0:n],
                                                rsum.unsqueeze(2).broadcast_to([P, B, n]), ALU.mult))
                if n < 8:
                    ch.link(nc.vector.memset(pr[:, :, n:8], -1.0))
                for b in range(B):
                    nc.vector.max(top[:, b, :], pr[:, b, :]).then_inc(dve_step, 1)
                    ch.n += 1
                dve.wait_ge(dve_step, ch.base + ch.n)
                for b in range(B):
                    nc.vector.max_index(top_i[:, b, :], top[:, b, :], pr[:, b, :]).then_inc(dve_step, 1)
                    ch.n += 1
                dve.wait_ge(dve_step, ch.base + ch.n)
                ch.link(nc.vector.tensor_copy(top_f, top_i))

            def combine():
                eights = C[:, C_I8:C_I8 + 8].unsqueeze(1).broadcast_to([P, B, 8])
                for i, eq in enumerate((eq1, eq2)):
                    ch.link(nc.vector.tensor_tensor(eq, eights, top_f[:, :, i:i + 1].broadcast_to([P, B, 8]),
                                                    ALU.is_equal))
                    ch.link(nc.vector.tensor_tensor(eq, eq, g12[:, i, :].unsqueeze(2).broadcast_to([P, B, 8]),
                                                    ALU.mult))
                nc.vector.tensor_tensor(comb[:, :, :], eq1, eq2, ALU.add).then_inc(comb_ready, 1)

            def output_bias(layer):
                def add(b):
                    dve.wait_ge(bias_mm, layer * B + b + 1)
                    nc.vector.tensor_tensor(X[:, b, :], X[:, b, :], PB[2 + b % 2][:, 0:D],
                                            ALU.add).then_inc(bias_added, 1)

                for b in range(B):
                    dve.wait_ge(comb_t, layer * B + b + 1)
                    nc.vector.tensor_copy(comb_s[:, b % 4, :], PB[b % 2][0:8, 0:P]).then_inc(comb_moved, 1)
                    if b:
                        add(b - 1)
                add(B - 1)

            def add_experts(n, made, added):
                with dve.Fori(0, NC) as c:
                    for e in range(n):
                        for i in range(CB):
                            m = c * (n * CB) + e * CB + i
                            dve.wait_ge(made, m + 1)
                            if e:
                                dve.wait_ge(added, m - CB + 1 + 4)
                            nc.vector.scalar_tensor_tensor(
                                X[:, ds(c * CB + i, 1), :], PB[4 + (e * CB + i) % 4][:, 0:D],
                                comb[:, ds(c * CB + i, 1), e:e + 1], X[:, ds(c * CB + i, 1), :],
                                ALU.mult, ALU.add).then_inc(added, 1)

            statistics(1)
            move_blocks(1, True)
            softmax_top2(0, R0)
            ch.link(nc.vector.tensor_tensor(rsum, top[:, :, 0], top[:, :, 1], ALU.add))
            ch.link(nc.vector.tensor_scalar(rsum, rsum, 1e-12, None, ALU.max))
            ch.link(nc.vector.reciprocal(rsum, rsum))
            for i in range(2):
                ch.link(nc.vector.tensor_tensor(g12[:, i, :], top[:, :, i], rsum, ALU.mult))
            combine()
            output_bias(0)
            phase_end(dve)
            add_experts(R0, y_mm, y_added)
            phase_end(dve)
            statistics(2)
            move_blocks(2, False)
            dve.wait_ge(in_small, 128)
            dve.wait_ge(loop_added, B + 1)
            nc.vector.tensor_tensor(X[:, :, :], X[:, :, :], HB[:, :].unsqueeze(1).broadcast_to([P, B, D]), ALU.add)
            phase_end(dve)
            nc.vector.memset(prob, -1.0)
            e8 = C[:, C_I8:C_I8 + 8]

            def edges(b):
                lo, rounds, before = block_row(dve, DST_W, b)
                with dve.Fori(0, rounds) as j:
                    t0, n, dmas = this_round(dve, DST_W, lo, before, j)
                    for u in range(UW):
                        dve.wait_ge(row2_used, n + u + 1)
                        nc.vector.tensor_scalar(oneh_l[:, u, :], iota, dstf[:, ds(t0 + u, 1)],
                                                C[:, ds(b + C_NEG, 1)], ALU.subtract,
                                                ALU.is_equal).then_inc(oh2_made, 1)
                    dve.wait_ge(row2_used, n + 2 * UW)
                    nc.vector.scalar_tensor_tensor(
                        X[:, ds(b, 1), :], PB[0][:, 0:D], SQH, X[:, ds(b, 1), :],
                        ALU.mult, ALU.add).then_inc(agg2_added, 1)
                    dve.wait_ge(agg2_added, before + j + 2)

            def scales(b):
                ch.link(nc.vector.bn_stats(stat1, X[:, ds(b, 1), :]))
                ch.pause()
                ch.link(nc.vector.bn_aggr(mv1, stat1))
                nc.vector.tensor_scalar(rstd1, mv1[:, 1:2], EPS, None, ALU.add).then_inc(var1_made, 1)
                dve.wait_ge(dev1_made, b + 1)
                ch.link(nc.vector.reciprocal(rstd1, rstd1))
                nc.vector.scalar_tensor_tensor(nmr1, mv1[:, 0:1], -1.0, rstd1, ALU.mult,
                                               ALU.mult).then_inc(scales1, 1)

            def route_max(b):
                dve.wait_ge(logits1, b + 1)
                ch.link(nc.vector.tensor_reduce(neg_max, PB[1][:, 0:E1], AX, ALU.max))
                nc.vector.tensor_scalar(neg_max, neg_max, -1.0, None, ALU.mult).then_inc(max_made, 1)

            def route_top(b):
                dve.wait_ge(probs_made, b + 1)
                ch.link(nc.vector.reciprocal(prob_sum, prob_sum))
                ch.link(nc.vector.tensor_scalar(prob[:, 0:E1], prob[:, 0:E1], prob_sum, None, ALU.mult))
                ch.pause()
                ch.link(nc.vector.max(top1, prob))
                nc.vector.tensor_scalar(neg_top, top1[:, 0:1], -1.0, None, ALU.mult).then_inc(tops_made, 1)
                ch.link(nc.vector.max_index(top1_i, top1, prob))
                ch.link(nc.vector.tensor_copy(top1_f, top1_i))

            def route_gates(b):
                dve.wait_ge(gates_made, b + 1)
                ch.link(nc.vector.reciprocal(gate_sum, gate_sum))
                ch.link(nc.vector.tensor_scalar(gates, gates, gate_sum, None, ALU.mult))
                ch.link(nc.vector.tensor_scalar(eq_a, e8, top1_f[:, 0:1], gates[:, 0:1], ALU.is_equal, ALU.mult))
                ch.link(nc.vector.tensor_scalar(eq_b, e8, top1_f[:, 1:2], gates[:, 1:2], ALU.is_equal, ALU.mult))
                nc.vector.tensor_tensor(comb1, eq_a, eq_b, ALU.add).then_inc(comb1_ready, 1)
                ch.link(nc.vector.tensor_tensor(comb[:, ds(b, 1), :], eq_a.unsqueeze(1), eq_b.unsqueeze(1), ALU.add))

            def route_turned(b):
                dve.wait_ge(comb1_t, b + 1)
                nc.vector.tensor_copy(comb1_s, PB[2][0:8, 0:P]).then_inc(comb1_moved, 1)

            def route_bias(b):
                dve.wait_ge(bias1_mm, b + 1)
                nc.vector.tensor_tensor(X[:, ds(b, 1), :], X[:, ds(b, 1), :], PB[1][:, 0:D],
                                        ALU.add).then_inc(bias1_added, 1)

            def add_expert(b, e):
                dve.wait_ge(y1_mm, b * E1 + e + 1)
                if e:
                    dve.wait_ge(y1_added, b * E1 + e + 2)
                else:
                    dve.wait_ge(bias1_added, b + 2)
                nc.vector.scalar_tensor_tensor(
                    X[:, ds(b, 1), :], PB[6 + e % 2][:, 0:D], comb[:, ds(b, 1), e:e + 1],
                    X[:, ds(b, 1), :], ALU.mult, ALU.add).then_inc(y1_added, 1)

            ORDER = (scales, 0, 1, route_max, 2, route_top, 3, route_gates, 4, route_turned, 5, route_bias)

            def layer1(before, b):
                for part in ORDER:
                    if isinstance(part, int):
                        if before is not None:
                            add_expert(before, part)
                    elif b is not None:
                        part(b)

            edges(0)
            layer1(None, 0)
            links = 14
            with dve.Fori(0, B - 1) as i:
                ch.loop(i, links)
                b = dve.snap(i + 1)
                edges(b)
                layer1(i, b)
            ch.loop_end(B - 1)
            layer1(B - 1, None)

        @block.tensor
        def _(pe):
            pe.wait_ge(in_const, 48)
            pe.matmul(PB[0][:, 0:B], zeros[:, 0:P], zeros[:, 0:B], start=True, stop=False, skip_group_check=True)
            with pe.Fori(0, T // 8) as i:
                for s in range(8):
                    if s % UD == 0:
                        pe.wait_ge(high_made[s // UD], i + 1)
                    pe.wait_ge(low_made, i * 8 + s + 1)
                    pe.matmul(PB[0][:, 0:B], WOH[:, s, :], OHHI[:, s // UD, s % UD, :], start=False, stop=False,
                              skip_group_check=True).then_inc(low_used, 1)
            pe.matmul(PB[0][:, 0:B], zeros[:, 0:P], zeros[:, 0:B], start=False, stop=True,
                      skip_group_check=True).then_inc(deg_ready, 1)
            pe.wait_ge(totals_ready, 1)
            pe.matmul(PB[2][:, 0:BK], ones, exc, start=True, stop=True)
            pe.matmul(PB[1][:, 0:BK], ones, exc, start=True, stop=False)
            pe.matmul(PB[1][:, 0:BK], tri, tot, start=False, stop=True).then_inc(bases_ready, 1)
            pe.wait_ge(ext_ready, 1)
            pe.transpose(PB[5][0:B, 0:P], two[:, 0, :], ident)
            pe.transpose(PB[5][0:B, P:2 * P], two[:, 1, :], ident).then_inc(ext_t, 1)
            pe.wait_ge(ext2_ready, 1)
            pe.transpose(PB[5][0:1, 256:256 + B], ext[:, 0:1], ident[0:B, 0:B])
            pe.transpose(PB[5][0:1, 384:384 + B], ext[:, 1:2], ident[0:B, 0:B]).then_inc(ext2_t, 1)
            phase_end(pe)
            with pe.Fori(0, B) as b:
                lo, rounds, before = block_row(pe, DST, b)
                with pe.Fori(0, rounds) as j:
                    t0, n, dmas = this_round(pe, DST, lo, before, j)
                    for u in range(U):
                        pe.wait_ge(oht_made, n + U + u + 1)
                        pe.wait_ge(msg_made, n + u + 1)
                        pe.matmul(PB[u][:, 0:D], oneh[:, u, :], XS[:, ds(b, 1), :], start=True,
                                  stop=True).then_inc(exp_done, 1)
            phase_end(pe)
            with pe.Fori(0, B) as b:
                lo, rounds, before = block_row(pe, SRC, b)
                with pe.Fori(0, rounds) as j:
                    t0, n, dmas = this_round(pe, SRC, lo, before, j)
                    pe.wait_ge(agg_added, before + j + 1)
                    for u in range(UW):
                        pe.wait_ge(oh_made, n + u + 1)
                        pe.matmul(PB[6][:, 0:D], oneh_w[:, u, :], back[:, u, 0:D], start=(u == 0),
                                  stop=(u == UW - 1)).then_inc(row_used, 1)
            phase_end(pe)

            def layer(weight, m, of, at, n, to, signal):
                for k in range(2):
                    moving = of[:, k, at:at + n] if isinstance(at, int) else of[:, k, ds(at, n)]
                    mm = pe.matmul(to[:, 0:n], weight[:, k, m * P:(m + 1) * P], moving,
                                   start=(k == 0), stop=(k == 1))
                mm.then_inc(signal, 1)

            pe.wait_ge(in_gw, 64)
            pe.wait_ge(in_small, 128)
            gw = [GW[:, 512 * i:512 * (i + 1)].rearrange("p (k o) -> p k o", k=2) for i in range(4)]
            with pe.Fori(0, NC) as c:
                for i in range(CB):
                    pe.wait_ge(agg_made, c * CB + i + 1)
                    if i >= 4:
                        pe.wait_ge(head_moved, c * 15 + i - 3)
                    for k in range(2):
                        mm = pe.transpose(PB[i % 4][:, k * P:(k + 1) * P],
                                          head_in[:, i, k * P:(k + 1) * P], ident)
                    mm.then_inc(head_mm, 1)
                pe.wait_ge(head_added, c * CB + 1)
                pe.wait_ge(head_moved, c * 15 + 7)
                for q in range(4):
                    layer(gw[0], q % 2, TC[0], q // 2 * HN, HN, PB[4 + q], head_mm)
                pe.wait_ge(head_moved, c * 15 + 11)
                for q in range(4):
                    layer(gw[1], q % 2, TC[1], q // 2 * HN, HN, PB[q], head_mm)
                pe.wait_ge(head_moved, c * 15 + 15)
                for i in range(CB):
                    if i >= 4:
                        pe.wait_ge(head_added, c * CB + i - 2)
                    for k in range(2):
                        pe.matmul(PB[4 + i % 4][:, 0:D], TC[2][:, k, i * P:(i + 1) * P], gw[2][:, k, :],
                                  start=(k == 0), stop=False)
                    pe.matmul(PB[4 + i % 4][:, 0:D], ones[0:1, :], srow[:, 0:D], start=False,
                              stop=True).then_inc(head_y, 1)
            phase_end(pe)

            def turn(k, after=None):
                with pe.Fori(0, NC) as c:
                    for s in range(CB):
                        n = c * CB + (k - 1) * B + s
                        pe.wait_ge(norm_made, n + 1)
                        last = 3 if s == 0 else 2
                        pe.wait_ge(slot_moved, n + last)
                        for h in range(2):
                            mm = pe.transpose(turn_bank(s)[:, h, :], xn[:, s % 4, h * P:(h + 1) * P], ident)
                        mm.then_inc(turned, 1)
                        if after and s:
                            after(c, s - 1)
                    if after:
                        after(c, CB - 1)

            def logits0(c, s):
                pe.wait_ge(slot_moved, c * CB + s + 4)
                for k in range(2):
                    mm = pe.matmul(PB[7][:, ds((c * CB + s) * 8, 8)], xts[:, s, k, :], RW[:, k, :],
                                   start=(k == 0), stop=(k == 1))
                mm.then_inc(slot_read, 1)

            def relations(c, s):
                pe.wait_ge(slot_moved, c * CB + B + s + 4)
                for q in range(4):
                    pe.wait_ge((pair_act, pair_dve)[q % 2], c * (2 * CB) + 2 * s + q // 2 + 1)
                    for k in range(2):
                        mm = pe.matmul(PB[2 + q][:, :], xts[:, s, k, :], WR[:, k, 512 * q:512 * (q + 1)],
                                       start=(k == 0), stop=(k == 1))
                    mm.then_inc(pair_mm, 1)
                pe.wait_ge(loop_added, c * CB + s + 1)
                for k in range(2):
                    mm = pe.matmul(PB[6 + s % 2][:, 0:D], xts[:, s, k, :], gw[3][:, k, :],
                                   start=(k == 0), stop=(k == 1))
                mm.then_inc(loop_mm, 1)

            def bias_products(layer_no):
                pe.wait_ge(comb_ready, layer_no + 1)

                def product(b):
                    n = layer_no * B + b
                    pe.wait_ge(comb_moved, n + 3)
                    pe.wait_ge(bias_added, n + 1)
                    pe.matmul(PB[2 + b % 2][:, 0:D], comb_s[:, b % 4, :], brow[:, layer_no * D:(layer_no + 1) * D],
                              start=True, stop=True).then_inc(bias_mm, 1)

                for b in range(B):
                    pe.wait_ge(comb_moved, layer_no * B + b + 1)
                    pe.transpose(PB[b % 2][0:8, 0:P], comb[:, b, :], ident).then_inc(comb_t, 1)
                    if b:
                        product(b - 1)
                product(B - 1)

            turn(1, logits0)
            bias_products(0)
            phase_end(pe)
            pe.wait_ge(in_w0, 16 * (2 * R0 + REL))
            with pe.Fori(0, NC) as c:
                def hidden(e):
                    for q in range(4):
                        pe.wait_ge(hid_moved, c * (4 * R0) + 4 * e + q + 1)
                        layer(W0[:, e, 0, :, :], q % 2, XT, c * CN + q // 2 * HN, HN, PB[q], hid_mm)

                hidden(0)
                for e in range(R0):
                    if e + 1 < R0:
                        hidden(e + 1)
                    pe.wait_ge(hid_moved, c * (4 * R0) + 4 * e + 8)
                    for i in range(CB):
                        pe.wait_ge(y_added, c * (R0 * CB) + e * CB + i + 1)
                        for k in range(2):
                            mm = pe.matmul(PB[4 + (e * CB + i) % 4][:, 0:D], HT[e % 2][:, k, i * P:(i + 1) * P],
                                           W0[:, e, 1, k, :], start=(k == 0), stop=(k == 1))
                        mm.then_inc(y_mm, 1)
            phase_end(pe)
            turn(2, relations)
            phase_end(pe)
            def edge_sums(b):
                lo, rounds, before = block_row(pe, DST_W, b)
                with pe.Fori(0, rounds) as j:
                    t0, n, dmas = this_round(pe, DST_W, lo, before, j)
                    pe.wait_ge(agg2_added, before + j + 1)
                    for u in range(UW):
                        pe.wait_ge(oh2_made, n + u + 1)
                        pe.wait_ge(got[u], dmas + 16)
                        pe.matmul(PB[0][:, 0:D], oneh_l[:, u, :], rows_in[:, u, :], start=(u == 0),
                                  stop=(u == UW - 1)).then_inc(row2_used, 1)

            def turned_half(b, k):
                return x_turned[:, ds(b % 2 * D + k * P, P)]

            def turn1(b):
                pe.wait_ge(norm1_made, b + 1)
                pe.wait_ge(bias1_added, b + 1)
                for k in range(2):
                    mm = pe.transpose(PB[1][:, k * P:(k + 1) * P], x_norm[:, k * P:(k + 1) * P], ident)
                mm.then_inc(turned1, 1)

            def router1(b):
                pe.wait_ge(turned1_moved, b + 1)
                for k in range(2):
                    mm = pe.matmul(PB[2][:, 0:P], RW1[:, k, :], turned_half(b, k), start=(k == 0), stop=(k == 1))
                mm.then_inc(rh_mm, 1)

            def router2(b):
                pe.wait_ge(rh_moved, b + 1)
                pe.matmul(PB[1][:, 0:E1], router_h, RW2[:, :], start=True, stop=False)
                pe.matmul(PB[1][:, 0:E1], ones[0:1, :], srow[:, D:D + E1], start=False, stop=True).then_inc(logits1, 1)

            def comb_turn(b):
                pe.wait_ge(comb1_ready, b + 1)
                pe.transpose(PB[2][0:8, 0:P], comb1, ident).then_inc(comb1_t, 1)

            def bias1(b):
                pe.wait_ge(comb1_moved, b + 1)
                pe.matmul(PB[1][:, 0:D], comb1_s, brow[:, D:2 * D], start=True, stop=True).then_inc(bias1_mm, 1)

            def output1(b, e):
                pe.wait_ge(hid1_moved, b * (4 * E1) + 2 * HIDDEN1.index((1, e)) + 5)
                pe.wait_ge(y1_added, b * E1 + e + 1)
                for k in range(2):
                    mm = pe.matmul(PB[6 + e % 2][:, 0:D], H2[:, e % 2, k, :], W1[:, e, 2, k, :],
                                   start=(k == 0), stop=(k == 1))
                mm.then_inc(y1_mm, 1)

            def experts1(before, b):
                for at, (part, e) in enumerate(HIDDEN1):
                    if part == 1:
                        pe.wait_ge(hid1_moved, before * (4 * E1) + 2 * HIDDEN1.index((0, e)) + 5)
                    for m in range(2):
                        i = 2 * at + m
                        pe.wait_ge(hid1_moved, before * (4 * E1) + i + 1)
                        for k in range(2):
                            mm = pe.matmul(PB[3 + i % 3][:, 0:P], W1[:, e, part, k, m * P:(m + 1) * P],
                                           H1[:, e % 2, k, :] if part else turned_half(before, k),
                                           start=(k == 0), stop=(k == 1))
                        mm.then_inc(hid1_mm, 1)
                    if part == 1 and e:
                        output1(before, e - 1)
                    if b is not None:
                        for where, stage in ((PE_TURN, turn1), (PE_HIDDEN, router1), (PE_LOGITS, router2)):
                            if at == where:
                                stage(b)
                if b is not None:
                    comb_turn(b)
                output1(before, E1 - 1)
                if b is not None:
                    bias1(b)

            edge_sums(0)
            for stage in (turn1, router1, router2, comb_turn, bias1):
                stage(0)
            pe.wait_ge(in_w1, 16 * 3 * E1)
            with pe.Fori(0, B - 1) as i:
                b = pe.snap(i + 1)
                edge_sums(b)
                experts1(i, b)
            experts1(B - 1, None)


_OUT = (N, D)


def _lay_out(a):
    import numpy as np

    def tiles(v, pad):
        v = np.concatenate([v, np.full(T * P - E, pad, v.dtype)])
        return np.ascontiguousarray(v.reshape(T, P).T)

    def cols(*vs):
        return np.concatenate([v.reshape(-1, P).T for v in vs], axis=1)

    a = {k: np.asarray(v) for k, v in a.items()}
    consts = np.zeros((P, C_N), np.float32)
    p = np.arange(P)
    consts[:, C_IOTA:C_IOTA + P] = p[None]
    consts[:, C_ID:C_ID + P] = np.eye(P)
    consts[:, C_TRI:C_TRI + P] = p[:, None] < p[None]
    consts[:, C_ONE:C_ONE + P] = 1
    consts[:, C_NODE:C_NODE + B] = p[:, None] + P * np.arange(B)[None]
    consts[:, C_NEG:C_NEG + BK] = -P * np.arange(BK)[None]
    consts[:, C_BLK:C_BLK + BK] = np.arange(BK)[None]
    consts[:, C_I8:C_I8 + 8] = np.arange(8)[None]
    tile = p[:, None] + P * np.arange(TG)[None]
    consts[:, C_REV:C_REV + TG] = BIG - tile
    consts[:, C_NEXT:C_NEXT + TG] = tile + 1
    dst, src = a["dst"].astype(np.int32, copy=False), a["src"].astype(np.int32, copy=False)
    return {
        "x": np.concatenate([a["x"], np.zeros((NP - N, D), np.float32)]),
        "src_t": tiles(src, NP),
        "dst_t": tiles(dst, NP),
        "type_t": tiles(a["edge_type_8"], 0),
        "weight_t": tiles(a["edge_weight"], 0),
        "dst_rows": np.concatenate([dst, np.full(TG * P * P - E, NP, dst.dtype)]).reshape(TG * P, P),
        "consts": consts,
        "shifted": np.broadcast_to(np.arange(BK, dtype=np.int32) << 20, (P, BK)).copy(),
        "bias_cols": np.ascontiguousarray(cols(
            a["L0_gnn_b"], a["L0_gnn_b1"], a["L0_ffn_b1"], a["L1_ffn_router_b1"], a["L1_ffn_expert_b1"],
            a["L1_ffn_expert_b2"])),
        "gnn_w": a["L0_gnn_W"], "gnn_w1": a["L0_gnn_W1"], "gnn_w2": a["L0_gnn_W2"],
        "gnn_b2": a["L0_gnn_b2"].reshape(1, D),
        "f0_router": np.ascontiguousarray(a["L0_ffn_router_w"].T), "f0_w1": a["L0_ffn_w1"],
        "f0_w2": a["L0_ffn_w2"], "f0_b2": a["L0_ffn_b2"],
        "rel_w": a["L1_gnn_weight"], "loop_w": a["L1_gnn_loop_weight"],
        "h_bias": a["L1_gnn_h_bias"].reshape(1, D),
        "f1_rw1": a["L1_ffn_router_w1"], "f1_rw2": a["L1_ffn_router_w2"],
        "f1_rb2": a["L1_ffn_router_b2"].reshape(1, E1), "f1_w1": a["L1_ffn_expert_w1"],
        "f1_w2": a["L1_ffn_expert_w2"], "f1_w3": a["L1_ffn_expert_w3"], "f1_b3": a["L1_ffn_expert_b3"],
    }


def kernel(**inputs):
    import concourse.bacc as bacc
    from concourse.bass_utils import run_bass_kernel_spmd

    nc = bacc.Bacc("TRN2", target_bir_lowering=False, num_devices=1)
    arrays = {f"in_{k}": v for k, v in _lay_out(inputs).items()}
    args = {k[3:]: nc.dram_tensor(k, v.shape, mybir.dt.from_np(v.dtype), kind="ExternalInput").ap()
            for k, v in arrays.items()}
    out = nc.dram_tensor("out", _OUT, f32, kind="ExternalOutput").ap()
    build(nc, out=out, **args)
    r = run_bass_kernel_spmd(nc, [arrays], core_ids=[0])
    return r.results[0]["out"]
```

```python
import concourse.bass as bass
from concourse import mybir
from contextlib import ExitStack

f32 = mybir.dt.float32
bf16 = mybir.dt.bfloat16
i32 = mybir.dt.int32
u32 = mybir.dt.uint32
u8 = mybir.dt.uint8
ALU = mybir.AluOpType
ACT = mybir.ActivationFunctionType
AX = mybir.AxisListType.X
ds = bass.ds

N, D, E, P = 6250, 256, 100000, 128
B = -(-N // P)
NP = B * P
U = 6
UH = U // 2
UW = 18
UG = 6
UD = 8
UD_DVE, UD_ACT = range(0, 5), range(5, 8)
T = 800
TG = 7
ROW = 264
BK = B + 1
R0, REL = 8, 8
E1 = 6
CB = 7
CN = CB * P
HN = CN // 2
NC = B // CB
BIG = 1024
EPS = 1e-5
DST, SRC, DST_W = 0, 1, 2
PER_ROUND = (U, UW, UW)
HALVES = ((0, (B + 1) // 2), ((B + 1) // 2, B))
ROUNDS_AT, BEFORE_AT = 10, 18
C_IOTA, C_ID, C_TRI, C_ONE, C_ZERO = 0, 128, 256, 384, 512
C_NODE, C_NEG, C_BLK, C_I8, C_REV, C_NEXT, C_N = 768, 817, 867, 917, 925, 932, 939
K_B, K_B1, K_F0, K_R1, K_X1, K_X2, K_N = 0, 2, 4, 20, 21, 33, 45
SQH = 0.5 ** 0.5


def build(nc, x, src_t, dst_t, type_t, weight_t, dst_rows, consts, shifted, bias_cols,
          gnn_w, gnn_w1, gnn_w2, gnn_b2, f0_router, f0_w1, f0_w2, f0_b2,
          rel_w, loop_w, h_bias, f1_rw1, f1_rw2, f1_rb2, f1_w1, f1_w2, f1_w3, f1_b3, out):
    ctx = ExitStack()
    with ctx:
        def sb(name, shape, dt=f32):
            return ctx.enter_context(nc.sbuf_tensor(name, shape, dt))

        def sem(name):
            return ctx.enter_context(nc.semaphore(name))

        def sems(name, n):
            return [sem(f"{name}{i}") for i in range(n)]

        msgs = nc.dram_tensor("msgs_sorted", [T * P, ROW], f32, kind="Internal").ap()
        hx = nc.dram_tensor("hx_rows", [NP * REL, D], f32, kind="Internal").ap()

        X = sb("X", [P, B, D])
        R1 = sb("R1", [P, B * D])
        R2 = sb("R2", [P, B * D])
        R3 = sb("R3", [P, 7168])
        C = sb("C", [P, C_N])
        GW = sb("GW", [P, 4 * 512])
        KC = sb("KC", [P, K_N])
        blk_shift = sb("blk_shift", [P, BK], i32)
        dstf = sb("dstf", [P, T])
        gidx = sb("gidx", [P, T], u32)
        blkD = sb("blkD", [P, T], i32)
        tab = sb("tab", [1, 3 * BK], i32)
        stat6 = sb("stat6", [P, B, 6])
        mv = sb("mv", [P, B, 2])
        rstd = sb("rstd", [P, B])
        nmr = sb("nmr", [P, B])
        dinv = sb("dinv", [P, B])
        sc1 = sb("sc1", [P, B])
        sc2 = sb("sc2", [P, B])
        idx = sb("idx", [P, UW], u32)
        iota, ident, tri = C[:, C_IOTA:C_IOTA + P], C[:, C_ID:C_ID + P], C[:, C_TRI:C_TRI + P]
        ones, zeros = C[:, C_ONE:C_ONE + P], C[:, C_ZERO:C_ZERO + D]

        XS = R1[:, :].rearrange("p (b d) -> p b d", d=D)
        XT = R2[:, :].rearrange("p (k n) -> p k n", k=2)
        src_i = R1[:, 0:T].bitcast(i32)
        dst_i = R1[:, T:2 * T].bitcast(i32)
        typ_i = R1[:, 2 * T:3 * T].bitcast(i32)
        tmp_i = R1[:, 3 * T:4 * T].bitcast(i32)
        blkS = R1[:, 4 * T:5 * T]
        loS = R1[:, 5 * T:6 * T]
        pos1 = R1[:, 6 * T:7 * T]
        tmp_f = R1[:, 7 * T:8 * T]
        drow_i = R1[:, 8 * T:8 * T + TG * P].bitcast(i32)
        OHB = R2[:, 0:BK * T // 4].bitcast(u8).rearrange("p (b t) -> p b t", b=BK)
        o = BK * T // 4
        wts, srcf, pos_i = R2[:, o:o + T], R2[:, o + T:o + 2 * T], R2[:, o + 2 * T:o + 3 * T].bitcast(i32)
        blk_eq = R1[:, 7300:7300 + UD * B].bitcast(bf16).rearrange("p (h s n) -> p h s n", h=2, s=UD)
        wt_blk = R1[:, 7700:7700 + 3 * UD * B].bitcast(bf16).rearrange("p (h s a n) -> p h s a n", h=2, s=UD, a=3)
        lo_eq = R1[:, 8900:8900 + UD * P].bitcast(bf16).rearrange("p (h s n) -> p h s n", h=2, s=UD)
        wt_part = [R1[:, 10000 + T // 2 * i:10000 + T // 2 * (i + 1)].bitcast(bf16) for i in range(3)]
        lo_now = R1[:, 11200:11200 + UD]
        minus_lo = R1[:, 11208:11208 + 2 * UD].rearrange("p (h s) -> p h s", h=2)
        distance = R1[:, 11232:11232 + 2 * len(UD_ACT) * P].rearrange("p (h s n) -> p h s n", h=2, s=len(UD_ACT))
        wt_rest, wt_rest2 = R1[:, 6 * T:7 * T], R1[:, 7 * T:8 * T]
        junk = R3[:, 1500:1500 + T]
        tot = R3[:, 2400:2400 + BK]
        cum = R3[:, 2450:2450 + BK]
        exc = R3[:, 2500:2500 + BK]
        base = R3[:, 2550:2550 + BK]
        tmn = R3[:, 2600:2600 + TG]
        tmx = R3[:, 2607:2607 + TG]
        tmn_i = R3[:, 2614:2614 + TG].bitcast(i32)
        tmx_i = R3[:, 2621:2621 + TG].bitcast(i32)
        ge = R3[:, 2640:2640 + B * TG].rearrange("p (b g) -> p b g", g=TG)
        le = R3[:, 3000:3000 + B * TG].rearrange("p (b g) -> p b g", g=TG)
        inb = R3[:, 3400:3400 + B * TG].rearrange("p (b g) -> p b g", g=TG)
        two = R3[:, 3800:3800 + 2 * B].rearrange("p (a b) -> p a b", a=2)
        ext = R3[0:B, 3900:3902]
        rowf = R3[0:1, 4000:4000 + 8 * BK].rearrange("p (a b) -> p a b", a=8)
        rowi = R3[0:1, 4500:4500 + 8 * BK].bitcast(i32).rearrange("p (a b) -> p a b", a=8)
        dst_bc = R3[:, 0:U * P].bitcast(i32).rearrange("p (s n) -> p s n", s=U)
        oneh = R3[:, 1024:1024 + U * P].rearrange("p (s n) -> p s n", s=U)
        msg = R3[:, 2304:2304 + 2 * U * ROW].rearrange("p (h s n) -> p h s n", h=2, s=U)
        oneh_w = R3[:, 0:UW * P].rearrange("p (s n) -> p s n", s=UW)
        back = R3[:, UW * P:UW * (P + ROW)].rearrange("p (s n) -> p s n", s=UW)
        agg_in = R1[:, 8192:8192 + D]
        agg_t, mid_t, hid_t = (R1[:, 8448 + D * i:8448 + D * (i + 1)].rearrange("p (k n) -> p k n", k=2) for i in range(3))
        x_norm0 = R1[:, 9216:9216 + D]
        xt0 = R1[:, 9472:9472 + D].rearrange("p (k n) -> p k n", k=2)
        comb0_s = R1[0:8, 9728:9728 + P]
        stat0, mv0, rstd0 = R1[:, 9856:9862], R1[:, 9864:9866], R1[:, 9868:9869]
        neg_max0, prob_sum0, gate_sum0, var0, power0 = (R1[:, 9872 + i:9873 + i] for i in range(5))
        prob0, top0, top0_f, eq0_a, eq0_b, comb0 = (R1[:, 9880 + 8 * i:9888 + 8 * i] for i in range(6))
        top0_i = R1[:, 9928:9936].bitcast(u32)
        gates0 = R1[:, 9936:9938]
        xn = R3[:, 0:4 * D].rearrange("p (s d) -> p s d", s=4)
        xts = R3[:, 1024:1024 + CB * D].rearrange("p (s k n) -> p s k n", s=CB, k=2)
        hxs = R3[:, 2816:2816 + 2 * REL * D].rearrange("p (s n) -> p s n", s=2)
        HT = [R3[:, 2 * CN * i:2 * CN * (i + 1)].rearrange("p (k n) -> p k n", k=2) for i in range(4)]
        W0 = R1[:, 0:R0 * 1024].rearrange("p (e m k o) -> p e m k o", e=R0, m=2, k=2)
        WR = R1[:, R0 * 1024:R0 * 1024 + 2 * REL * D].rearrange("p (k n) -> p k n", k=2)
        W1 = R1[:, 0:E1 * 1536].rearrange("p (e m k o) -> p e m k o", e=E1, m=3, k=2)
        rows_in = R2[:, 0:UW * D].rearrange("p (s d) -> p s d", s=UW)
        oneh_l = R2[:, 4608:4608 + UW * P].rearrange("p (s n) -> p s n", s=UW)
        x_norm = R2[:, 6912:6912 + D]
        x_turned = R2[:, 7168:7168 + 2 * D]
        H1 = R2[:, 7680:7680 + 2 * D].rearrange("p (s k n) -> p s k n", s=2, k=2)
        H2 = R2[:, 8192:8192 + 2 * D].rearrange("p (s k n) -> p s k n", s=2, k=2)
        router_h = R2[:, 8704:8704 + P]
        stat1, mv1 = R2[:, 8832:8838], R2[:, 8840:8842]
        rstd1, nmr1 = R2[:, 8844:8845], R2[:, 8845:8846]
        var1, minus_half, newton, half_bits = (R2[:, 8914 + i:8915 + i] for i in range(4))
        neg_max, prob_sum, neg_top, gate_sum = (R2[:, 8848 + i:8849 + i] for i in range(4))
        prob, top1, top1_f, eq_a, eq_b, comb1 = (R2[:, 8856 + 8 * i:8864 + 8 * i] for i in range(6))
        top1_i = R2[:, 8904:8912].bitcast(u32)
        gates = R2[:, 8912:8914]
        comb1_s = R2[0:8, 9000:9000 + P]
        comb = sb("comb", [P, B, 8])
        HB = sb("HB", [P, D])
        RW = sb("RW", [P, 2, 8])
        RW1 = sb("RW1", [P, 2, P])
        RW2 = sb("RW2", [P, E1])
        brow = sb("brow", [8, 2 * D])
        srow = sb("srow", [1, D + 8])
        PS = ctx.enter_context(nc.psum_tensor("PS", [P, 8, 512], f32))
        PB = [PS[:, i, :] for i in range(8)]
        scanp = [PS[:, i:i + 2, :].rearrange("p a n -> p (a n)")[:, 0:T] for i in (3, 6)]
        tail = (T * P - E) * ROW // 48
        zero_rows = R3[0:48, 5500:5500 + tail // (2 * U)]

        phase_done = sem("phase_done")
        phases = {}

        def phase_end(e):
            k = phases[id(e)] = phases.get(id(e), 0) + 1
            e.drain().then_inc(phase_done, 1)
            e.wait_ge(phase_done, 5 * k)

        class Chain:

            def __init__(self, e, s):
                self.e, self.s, self.base, self.n = e, s, 0, 0

            def link(self, ins):
                ins.then_inc(self.s, 1)
                self.n += 1
                self.e.wait_ge(self.s, self.base + self.n)

            def pause(self):
                self.e.sem_inc(pauses, 1)

            def loop(self, i, per):
                self.start, self.per = self.base + self.n, per
                self.base, self.n = self.start + i * per, 0

            def loop_end(self, count):
                assert self.n == self.per, (self.n, self.per)
                self.base, self.n = self.start + count * self.per, 0

        pauses, loads_begun = sem("pauses"), sem("loads_begun")
        dve_step, pool_step = sem("dve_step"), sem("pool_step")

        def block_row(e, which, b):
            row = e.value_load(tab[0:1, ds(b + BK * which, 1)], min_val=0, max_val=2 ** 31 - 1)
            why = "the fields of a table's entry"
            return (nc.s_assert_within(e.snap(row & 1023), 0, T - 1, skip_runtime_bounds_check_because=why),
                    nc.s_assert_within(e.snap((row >> ROUNDS_AT) & 255), 1, T, skip_runtime_bounds_check_because=why),
                    nc.s_assert_within(e.snap(row >> BEFORE_AT), 0, B * T, skip_runtime_bounds_check_because=why))

        def rounds_before(e, which, b):
            if b == 0:
                return 0
            row = e.value_load(tab[0:1, BK * which + b:BK * which + b + 1], min_val=0, max_val=2 ** 31 - 1)
            return nc.s_assert_within(e.snap(row >> BEFORE_AT), b, B * T,
                                      skip_runtime_bounds_check_because="a round per block or more")

        def slot_idx(half, u):
            return idx[:, half * U + u:half * U + u + 1]

        def since(at, start):
            return at if isinstance(start, int) else (at - start) & ((1 << (31 - BEFORE_AT)) - 1)

        def this_round(e, which, lo, before, j, start=0):
            why = "rounds are cut so that a block's last one begins at its last tile or before"
            return (nc.s_assert_within(e.snap(lo + j * PER_ROUND[which]), 0, T - PER_ROUND[which],
                                       skip_runtime_bounds_check_because=why),
                    e.snap((before + j) * PER_ROUND[which]),
                    e.snap(since(before + j, start) * 16))

        in_const, in_edge, in_dst, in_rows = sem("in_const"), sem("in_edge"), sem("in_dst"), sem("in_rows")
        in_x, in_gw, brow_clear = sem("in_x"), sem("in_gw"), sem("brow_clear")
        lo_made, lo_made_act, high_made, low_made, used, now_made, blk_made = (
            sem("lo_made"), sem("lo_made_act"), sem("high_made"), sem("low_made"), sem("used"), sem("now_made"),
            sem("blk_made"))
        dist_made = sem("dist_made")
        keys_ready, bucket_rows, bucket_tot, totals_ready, bases_ready = (
            sem("keys_ready"), sem("bucket_rows"), sem("bucket_tot"), sem("totals_ready"), sem("bases_ready"))
        deg_ready, ext_ready, ext_t, ext2_ready, ext2_t = (
            sem("deg_ready"), sem("ext_ready"), sem("ext_t"), sem("ext2_ready"), sem("ext2_t"))
        root_in, root_out, scales_ready, xs_begun = sem("root_in"), sem("root_out"), sem("scales_ready"), sem("xs_begun")
        dst_in, oht_made, exp_done = [sems(f"dst_in{h}_", 2) for h in range(2)], sem("oht_made"), sem("exp_done")
        msg_made, idx_made, scattered = sem("msg_made"), sem("idx_made"), [sems(f"scattered{h}_", U) for h in range(2)]
        row_in, oh_made, row_used = sems("row_in", UW // UG), sem("oh_made"), sem("row_used")
        rows_written, sends_begun, gathers_begun = sem("rows_written"), sem("sends_begun"), sem("gathers_begun")
        in_w0, in_wr, in_w1, in_small = sem("in_w0"), sem("in_wr"), sem("in_w1"), sem("in_small")
        agg_begun, agg_ready, agg_turned, agg_t_made, mid_mm, mid_made, hid0_mm, hid0_made, head_y, head_added = (
            sem("agg_begun"), sem("agg_ready"), sem("agg_turned"), sem("agg_t_made"), sem("mid_mm"), sem("mid_made"),
            sem("hid0_mm"), sem("hid0_made"), sem("head_y"), sem("head_added"))
        var0_made, rstd0_made, norm0_made, norm0_added, turned0, xt0_made, xt0_saved = (
            sem("var0_made"), sem("rstd0_made"), sem("norm0_made"), sem("norm0_added"), sem("turned0"),
            sem("xt0_made"), sem("xt0_saved"))
        logits0, max0_made, probs0_made, comb0_ready, comb0_t, comb0_moved, bias0_mm, bias0_added = (
            sem("logits0"), sem("max0_made"), sem("probs0_made"), sem("comb0_ready"), sem("comb0_t"),
            sem("comb0_moved"), sem("bias0_mm"), sem("bias0_added"))
        norm_made, turned, slot_moved = (
            sem("norm_made"), sem("turned"), sem("slot_moved"))
        hid_mm, hid_moved, y_mm, y_added = sem("hid_mm"), sem("hid_moved"), sem("y_mm"), sem("y_added")
        hid1_mm, hid1_moved, y1_mm, y1_added = sem("hid1_mm"), sem("hid1_moved"), sem("y1_mm"), sem("y1_added")
        pair_mm, pair_act, pair_dve, loop_mm, loop_added = (
            sem("pair_mm"), sem("pair_act"), sem("pair_dve"), sem("loop_mm"), sem("loop_added"))
        hx_out, hx_freed = sem("hx_out"), sem("hx_freed")
        gidx_made, got, oh2_made, row2_used = sem("gidx_made"), sems("got", UW), sem("oh2_made"), sem("row2_used")
        agg_added, agg2_added = sem("agg_added"), sem("agg2_added")
        scales1, norm1_made, turned1, turned1_moved = sem("scales1"), sem("norm1_made"), sem("turned1"), sem("turned1_moved")
        rh_mm, rh_moved, logits1, max_made, probs_made, tops_made, gates_made = (
            sem("rh_mm"), sem("rh_moved"), sem("logits1"), sem("max_made"), sem("probs_made"), sem("tops_made"), sem("gates_made"))
        comb1_ready, comb1_t, comb1_moved, bias1_mm, bias1_added = (
            sem("comb1_ready"), sem("comb1_t"), sem("comb1_moved"), sem("bias1_mm"), sem("bias1_added"))
        out_done = sem("out_done")

        def turn_bank(s):
            return PB[s % 2][:, 0:D].rearrange("p (k n) -> p k n", k=2)

        HIDDEN1 = [(0, 0)] + [x for e in range(E1) for x in ([(0, e + 1)] if e + 1 < E1 else []) + [(1, e)]]
        PE_BIAS, PE_TURN, PE_HIDDEN, PE_LOGITS = 4, 5, 7, 8
        ACT_NORM, ACT_TURNED, ACT_HIDDEN, ACT_PROBS, ACT_GATES = 4, 6, 8, 10, 11

        dst_line = dst_rows.rearrange("(o t) e -> o (t e)", o=1)

        block = ctx.enter_context(nc.Block())

        @block.sync
        def _(sp):
            for to, of in ((C[:, :], consts), (blk_shift[:, :], shifted), (KC[:, :], bias_cols)):
                sp.dma_start(to, of).then_inc(in_const, 16)
            sp.dma_start(src_i, src_t).then_inc(in_edge, 16)
            sp.dma_start(wts, weight_t).then_inc(in_edge, 16)
            sp.dma_start(drow_i.rearrange("p (g e) -> p g e", g=TG),
                         dst_rows.rearrange("(g p) e -> p g e", p=P)).then_inc(in_rows, 16)
            sp.dma_start(dst_i, dst_t).then_inc(in_dst, 16)
            sp.dma_start(typ_i, type_t).then_inc(in_dst, 16)
            for c in range(NC):
                sp.dma_start(X[:, c * CB:(c + 1) * CB, :],
                             x[c * CN:(c + 1) * CN, :].rearrange("(b p) d -> p b d", p=P)).then_inc(in_x, 16)
            sp.dma_start(RW[:, :, :], f0_router.rearrange("(k p) e -> p k e", p=P)).then_inc(in_small, 16)
            sp.dma_start(RW1[:, :, :], f1_rw1.rearrange("(k p) e -> p k e", p=P)).then_inc(in_small, 16)
            sp.dma_start(RW2[:, :], f1_rw2).then_inc(in_small, 16)
            sp.dma_start(brow[:, 0:D], f0_b2).then_inc(in_small, 16)
            sp.wait_ge(brow_clear, 1)
            sp.dma_start(brow[0:E1, D:2 * D], f1_b3).then_inc(in_small, 16)
            sp.dma_start(srow[:, 0:D], gnn_b2).then_inc(in_small, 16)
            sp.dma_start(srow[:, D:D + E1], f1_rb2).then_inc(in_small, 16)
            sp.dma_start(HB[:, :], h_bias.broadcast_to([P, D])).then_inc(in_small, 16)
            for i, w in enumerate((gnn_w, gnn_w1, gnn_w2, loop_w)):
                sp.dma_start(GW[:, 512 * i:512 * (i + 1)].rearrange("p (k o) -> p k o", k=2),
                             w.rearrange("(k p) o -> p k o", p=P)).then_inc(in_gw, 16)
            phase_end(sp)
            for half, (first_b, end_b) in enumerate(HALVES):
                with sp.Fori(first_b, end_b) as b:
                    lo, rounds, before = block_row(sp, DST, b)
                    with sp.Fori(0, rounds) as j:
                        t0, n, _ = this_round(sp, DST, lo, before, j)
                        for h in range(2):
                            edge = sp.snap((t0 + UH * h) * P)
                            sp.wait_ge(oht_made, n + UH * (h + 1))
                            sp.sem_inc(loads_begun, 1)
                            sp.dma_start(R3[:, UH * P * h:UH * P * (h + 1)].bitcast(i32),
                                         dst_line[:, ds(edge, UH * P)].broadcast_to([P, UH * P])
                                         ).then_inc(dst_in[half][h], 16)
            phase_end(sp)
            sp.wait_ge(rows_written, 1)
            with sp.Fori(0, B) as b:
                lo, rounds, before = block_row(sp, SRC, b)
                with sp.Fori(0, rounds) as j:
                    t0, n, dmas = this_round(sp, SRC, lo, before, j)
                    for k in range(UW // UG):
                        row = sp.snap((t0 + UG * k) * P)
                        sp.wait_ge(row_used, n + UG * (k + 1))
                        sp.sem_inc(loads_begun, 1)
                        sp.dma_start(back[:, UG * k:UG * (k + 1), :],
                                     msgs[ds(row, UG * P), :].rearrange("(s p) c -> p s c", p=P)
                                     ).then_inc(row_in[k], 16)
            phase_end(sp)
            for rel in range(REL):
                sp.dma_start(WR[:, :, rel * D:(rel + 1) * D],
                             rel_w[rel, :, :].rearrange("(k p) o -> p k o", p=P)).then_inc(in_wr, 16)
            phase_end(sp)
            with sp.Fori(0, NC) as c:
                for s in range(CB):
                    sp.wait_ge(pair_act, c * (2 * CB) + 2 * s + 4)
                    sp.wait_ge(pair_dve, c * (2 * CB) + 2 * s + 4)
                    sp.dma_start(hx[ds((c * CB + s) * (P * REL), P * REL), :].rearrange("(p r) d -> p (r d)", r=REL),
                                 hxs[:, s % 2, :]).then_inc(hx_out, 16)
                    sp.wait_ge(hx_out, c * (16 * CB) + 16 * s + 16)
                    sp.sem_inc(hx_freed, 1)
            phase_end(sp)
            for e in range(E1):
                for m, w in enumerate((f1_w1, f1_w2, f1_w3)):
                    sp.dma_start(W1[:, e, m, :, :], w[e, :, :].rearrange("(k p) o -> p k o", p=P)).then_inc(in_w1, 16)
            full = N // P
            with sp.Fori(0, full) as b:
                sp.wait_ge(y1_added, b * E1 + (2 + E1))
                sp.dma_start(out[ds(b * P, P), :], X[:, ds(b, 1), :]).then_inc(out_done, 16)
            sp.wait_ge(y1_added, B * E1 + 2)
            sp.dma_start(out[full * P:N, :], X[0:N - full * P, full, :]).then_inc(out_done, 16)
            sp.wait_ge(out_done, 16 * (full + 1))

        @block.gpsimd
        def _(pool):
            nc.gpsimd.memset(brow[:, D:2 * D], 0.0).then_inc(brow_clear, 1)
            nc.gpsimd.memset(zero_rows, 0.0).then_inc(pool_step, 1)
            pool.wait_ge(pool_step, 1)
            rest = msgs[E:T * P, :].rearrange("(p r) c -> p (r c)", p=48)
            part = tail // (2 * U)
            for u in range(2 * U):
                pool.dma_start(rest[:, part * u:part * (u + 1)], zero_rows).then_inc(scattered[u // U][u % U], 16)
            with pool.Fori(0, T // (2 * UD)) as i:
                for h in range(2):
                    at = pool.snap(i * (2 * UD) + h * UD)
                    pool.wait_ge(blk_made, i * 2 + h + 1)
                    for a in (1, 2):
                        ins = nc.gpsimd.tensor_tensor(wt_blk[:, h, :, a, :], blk_eq[:, h, :, :],
                                                      wt_part[a][:, ds(at, UD)].unsqueeze(2).broadcast_to([P, UD, B]),
                                                      ALU.mult)
                    ins.then_inc(low_made, 1)
            phase_end(pool)
            last_row = pool.to_reg(T * P - 1)
            for half, (first_b, end_b) in enumerate(HALVES):
                with pool.Fori(first_b, end_b) as b:
                    lo, rounds, before = block_row(pool, DST, b)
                    with pool.Fori(0, rounds) as j:
                        t0, n, _ = this_round(pool, DST, lo, before, j)
                        for u in range(U):
                            pool.wait_ge(msg_made, n + U + u + 1)
                            pool.wait_ge(idx_made, n + u + 1)
                            pool.sem_inc(sends_begun, 1)
                            pool.indirect_dma_start(
                                msgs, bass.IndirectOffsetOnAxis(ap=slot_idx(half, u), axis=0), msg[:, half, u, :], None,
                                bounds_check=last_row, oob_is_err=False).then_inc(scattered[half][u], 16)
            halfway, end = rounds_before(pool, DST, HALVES[1][0]), rounds_before(pool, DST, B)
            rest = pool.snap(since(end, halfway))
            for u in range(U):
                pool.wait_ge(scattered[0][u], halfway * 16 + 16)
                pool.wait_ge(scattered[1][u], rest * 16 + 16)
            pool.sem_inc(rows_written, 1)
            phase_end(pool)
            for e in range(R0):
                for m, w in enumerate((f0_w1, f0_w2)):
                    pool.dma_start(W0[:, e, m, :, :], w[e, :, :].rearrange("(k p) o -> p k o", p=P)).then_inc(in_w0, 16)

            def scale0(b):
                pool.wait_ge(var0_made, b + 1)
                nc.gpsimd.tensor_tensor(rstd0, var0, power0, ALU.pow).then_inc(rstd0_made, 1)

            def save0(b):
                pool.wait_ge(norm0_made, b + 1)
                nc.gpsimd.tensor_tensor(X[:, ds(b, 1), :], X[:, ds(b, 1), :], x_norm0.unsqueeze(1),
                                        ALU.add).then_inc(norm0_added, 1)
                pool.wait_ge(xt0_made, b + 1)
                nc.gpsimd.tensor_copy(XT[:, :, ds(b * P, P)], xt0).then_inc(xt0_saved, 1)

            scale0(0)
            with pool.Fori(0, B - 1) as b:
                save0(b)
                scale0(b + 1)
            save0(B - 1)
            phase_end(pool)
            phase_end(pool)
            phase_end(pool)
            with pool.Fori(0, B) as b:
                lo, rounds, before = block_row(pool, DST_W, b)
                with pool.Fori(0, rounds) as j:
                    t0, n, dmas = this_round(pool, DST_W, lo, before, j)
                    made = pool.snap((before + j) * (UW // UG))
                    for u in range(UW):
                        if u % UG == 0:
                            pool.wait_ge(row2_used, n + u + UG)
                            nc.gpsimd.tensor_copy(idx[:, u:u + UG], gidx[:, ds(t0 + u, UG)]).then_inc(gidx_made, 1)
                            pool.wait_ge(gidx_made, made + u // UG + 1)
                            pool.sem_inc(gathers_begun, 1)
                        pool.indirect_dma_start(
                            rows_in[:, u, :], None, hx, bass.IndirectOffsetOnAxis(ap=idx[:, u:u + 1], axis=0),
                            ).then_inc(got[u], 16)

        @block.scalar
        def _(act):
            for b in range(BK):
                act.wait_ge(bucket_rows, b + 1)
                if b:
                    act.wait_ge(bucket_tot, b)
                nc.scalar.activation(junk, OHB[:, b, :], ACT.Identity,
                                     accum_out=tot[:, b:b + 1]).then_inc(bucket_tot, 1)
            with act.Fori(0, T // (2 * UD)) as i:
                for h in range(2):
                    act.wait_ge(now_made, i * 2 + h + 1)
                    for k, s in enumerate(UD_ACT):
                        ins = nc.scalar.activation(distance[:, h, k, :], iota, ACT.Abs, bias=minus_lo[:, h, s:s + 1])
                    ins.then_inc(dist_made, 1)
                    act.wait_ge(dist_made, i * 2 + h + 1)
                    for k, s in enumerate(UD_ACT):
                        ins = nc.scalar.activation(lo_eq[:, h, s, :], distance[:, h, k, :], ACT.Relu,
                                                   bias=ones[:, 0:1], scale=-1.0)
                    ins.then_inc(lo_made_act, 1)
            act.wait_ge(root_in, 1)
            nc.scalar.activation(sc1[:, :], sc1[:, :], ACT.Sqrt)
            nc.scalar.activation(rstd[:, :], rstd[:, :], ACT.Sqrt).then_inc(root_out, 1)
            act.wait_ge(xs_begun, 1)
            for b in range(B // 2, B):
                nc.scalar.activation(XS[:, b, :], X[:, b, :], ACT.Identity, bias=sc2[:, b:b + 1], scale=sc1[:, b:b + 1])
            act.wait_ge(scales_ready, 1)
            phase_end(act)
            for half, (first_b, end_b) in enumerate(HALVES):
                start = rounds_before(act, DST, first_b)
                with act.Fori(first_b, end_b) as b:
                    lo, rounds, before = block_row(act, DST, b)
                    with act.Fori(0, rounds) as j:
                        t0, n, dmas = this_round(act, DST, lo, before, j, start)
                        for u in range(U):
                            act.wait_ge(scattered[half][u], dmas + 16)
                            nc.scalar.activation(msg[:, half, u, D:D + 1], srcf[:, ds(t0 + u, 1)], ACT.Copy)
                            act.wait_ge(exp_done, n + U + u + 1)
                            nc.scalar.activation(msg[:, half, u, 0:D], PB[u][:, 0:D], ACT.Copy,
                                                 scale=wts[:, ds(t0 + u, 1)]).then_inc(msg_made, 1)
            phase_end(act)
            def begin_sums(b):
                act.wait_ge(agg_turned, b + 1)
                nc.scalar.activation(agg_in, X[:, ds(b, 1), :], ACT.Identity, bias=nmr[:, ds(b, 1)],
                                     scale=rstd[:, ds(b, 1)]).then_inc(agg_begun, 1)

            def head_turned(b):
                act.wait_ge(agg_turned, b + 2)
                nc.scalar.activation(agg_t, PB[2][:, 0:D].rearrange("p (k n) -> p k n", k=2),
                                     ACT.Copy).then_inc(agg_t_made, 1)

            def head_layer(b, made, to, bank, func, k0, signal):
                act.wait_ge(made, b + 1)
                for m in range(2):
                    ins = nc.scalar.activation(to[:, m, :], PB[bank][:, m * P:(m + 1) * P], func,
                                               bias=KC[:, k0 + m:k0 + m + 1])
                ins.then_inc(signal, 1)

            def route_xt(b):
                act.wait_ge(turned0, b + 1)
                act.wait_ge(xt0_saved, b + 1)
                nc.scalar.activation(xt0, PB[4][:, 0:D].rearrange("p (k n) -> p k n", k=2),
                                     ACT.Copy).then_inc(xt0_made, 1)

            def route_probs(b):
                act.wait_ge(max0_made, b + 1)
                nc.scalar.activation(prob0, PB[5][:, 0:8], ACT.Exp, bias=neg_max0,
                                     accum_out=prob_sum0).then_inc(probs0_made, 1)

            def step(b, head, route):
                if head is not None:
                    head_turned(head)
                if b is not None:
                    begin_sums(b)
                if route is not None:
                    route_xt(route)
                if head is not None:
                    head_layer(head, mid_mm, mid_t, 3, ACT.Identity, K_B, mid_made)
                if route is not None:
                    route_probs(route)
                if head is not None:
                    head_layer(head, hid0_mm, hid_t, 2, ACT.Relu, K_B1, hid0_made)

            step(0, None, None)
            step(1, 0, None)
            with act.Fori(0, B - 2) as i:
                step(act.snap(i + 2), act.snap(i + 1), i)
            step(None, B - 1, B - 2)
            step(None, None, B - 1)
            phase_end(act)

            def roots(k):
                act.wait_ge(root_in, k + 1)
                nc.scalar.activation(rstd[:, :], rstd[:, :], ACT.Sqrt).then_inc(root_out, 1)

            def normalise():
                act.wait_ge(scales_ready, 2)
                with act.Fori(0, NC) as c:
                    for s in range(CB):
                        act.wait_ge(slot_moved, c * CB + s + 1)
                        nc.scalar.activation(xn[:, s % 4, :], X[:, ds(c * CB + s, 1), :], ACT.Identity,
                                             bias=nmr[:, ds(c * CB + s, 1)],
                                             scale=rstd[:, ds(c * CB + s, 1)]).then_inc(norm_made, 1)
                        if s:
                            pairs(c, s - 1)
                    pairs(c, CB - 1)

            def pairs(c, s):
                act.wait_ge(hx_freed, c * CB + s + (2 if s == 0 else 1))
                for q in (0, 2):
                    act.wait_ge(pair_mm, c * (4 * CB) + 4 * s + q + 1)
                    nc.scalar.activation(hxs[:, s % 2, q * 512:(q + 1) * 512], PB[2 + q][:, :],
                                         ACT.Copy).then_inc(pair_act, 1)

            with act.Fori(0, NC) as c:
                for e in range(R0):
                    for q in range(4):
                        half, m = divmod(q, 2)
                        act.wait_ge(hid_mm, c * (4 * R0) + 4 * e + q + 1)
                        nc.scalar.activation(HT[e % 2][:, m, half * HN:(half + 1) * HN], PB[q][:, 0:HN], ACT.Gelu,
                                             bias=KC[:, K_F0 + 2 * e + m:K_F0 + 2 * e + m + 1]).then_inc(hid_moved, 1)
            phase_end(act)
            roots(1)
            normalise()
            phase_end(act)
            def norm1(b):
                act.wait_ge(scales1, b + 1)
                nc.scalar.activation(x_norm, X[:, ds(b, 1), :], ACT.Identity, bias=nmr1,
                                     scale=rstd1).then_inc(norm1_made, 1)

            def turned1_out(b):
                act.wait_ge(turned1, b + 1)
                nc.scalar.activation(x_turned[:, ds(b % 2 * D, D)], PB[1][:, 0:D], ACT.Copy).then_inc(turned1_moved, 1)

            def router_hidden(b):
                act.wait_ge(rh_mm, b + 1)
                nc.scalar.activation(router_h, PB[2][:, 0:P], ACT.Relu,
                                     bias=KC[:, K_R1:K_R1 + 1]).then_inc(rh_moved, 1)

            def probs(b):
                act.wait_ge(max_made, b + 1)
                nc.scalar.activation(prob[:, 0:E1], PB[1][:, 0:E1], ACT.Exp, bias=neg_max,
                                     accum_out=prob_sum).then_inc(probs_made, 1)

            def gate_exps(b):
                act.wait_ge(tops_made, b + 1)
                nc.scalar.activation(gates, top1[:, 0:2], ACT.Exp, bias=neg_top,
                                     accum_out=gate_sum).then_inc(gates_made, 1)

            stages = {ACT_NORM: norm1, ACT_TURNED: turned1_out, ACT_HIDDEN: router_hidden, ACT_PROBS: probs,
                      ACT_GATES: gate_exps}

            def hidden1(before, b):
                for at, (layer, e) in enumerate(HIDDEN1):
                    for m in range(2):
                        k0 = (K_X1, K_X2)[layer] + 2 * e + m
                        i = 2 * at + m
                        act.wait_ge(hid1_mm, before * (4 * E1) + i + 1)
                        nc.scalar.activation((H1, H2)[layer][:, e % 2, m, :], PB[3 + i % 3][:, 0:P], ACT.Relu,
                                             bias=KC[:, k0:k0 + 1]).then_inc(hid1_moved, 1)
                    if b is not None and at in stages:
                        stages[at](b)

            for at in sorted(stages):
                stages[at](0)
            with act.Fori(0, B - 1) as b:
                hidden1(b, b + 1)
            hidden1(B - 1, None)

        @block.vector
        def _(dve):
            ch = Chain(dve, dve_step)
            for s, n in ((used, 2), (lo_made, 1), (oht_made, U), (exp_done, U), (msg_made, U), (row_used, UW),
                         (row2_used, UW), (agg_added, 1), (agg_ready, 2), (agg_turned, 1), (xt0_saved, 1),
                         (bias0_added, 1), (agg2_added, 1), (head_added, 1), (slot_moved, 3), (hid_moved, 4),
                         (hid1_moved, 3), (y_added, 4), (y1_added, 2), (hx_freed, 2), (loop_added, 1), (bias1_added, 1),
                         (pair_act, 2), (pair_dve, 2)):
                dve.sem_inc(s, n)
            dve.wait_ge(in_edge, 32)
            nc.vector.tensor_copy(srcf, src_i)
            ch.link(nc.vector.tensor_scalar(tmp_i, src_i, 7, None, ALU.arith_shift_right))
            ch.link(nc.vector.tensor_copy(blkS, tmp_i))
            ch.link(nc.vector.tensor_scalar(tmp_i, src_i, 127, None, ALU.bitwise_and))
            nc.vector.tensor_copy(loS, tmp_i).then_inc(keys_ready, 1)
            dve.wait_ge(keys_ready, 1)
            for b in range(BK):
                nc.vector.tensor_scalar(OHB[:, b, :], blkS, float(b), None, ALU.is_equal).then_inc(bucket_rows, 1)
            dve.wait_ge(in_const, 48)
            ch.link(nc.vector.tensor_copy(wt_part[0], wts))
            ch.link(nc.vector.tensor_tensor(wt_rest, wts, wt_part[0], ALU.subtract))
            ch.link(nc.vector.tensor_copy(wt_part[1], wt_rest))
            ch.link(nc.vector.tensor_tensor(wt_rest2, wt_rest, wt_part[1], ALU.subtract))
            nc.vector.tensor_copy(wt_part[2], wt_rest2)
            with dve.Fori(0, T // (2 * UD)) as i:
                for h in range(2):
                    at = dve.snap(i * (2 * UD) + h * UD)
                    dve.wait_ge(used, i * 2 + h + 1)
                    dve.wait_ge(lo_made, i * 2 + h + 1)
                    nc.vector.tensor_scalar(minus_lo[:, h, :], loS[:, ds(at, UD)], -1.0, None,
                                            ALU.mult).then_inc(now_made, 1)
                    nc.vector.tensor_copy(lo_now, loS[:, ds(at, UD)])
                    nc.vector.tensor_tensor(
                        blk_eq[:, h, :, :], blkS[:, ds(at, UD)].unsqueeze(2).broadcast_to([P, UD, B]),
                        C[:, C_BLK:C_BLK + B].unsqueeze(1).broadcast_to([P, UD, B]),
                        ALU.is_equal).then_inc(blk_made, 1)
                    dve.wait_ge(blk_made, i * 2 + h + 1)
                    for s in UD_DVE:
                        ins = nc.vector.tensor_scalar(lo_eq[:, h, s, :], iota, lo_now[:, s:s + 1], None,
                                                      ALU.is_equal)
                    ins.then_inc(lo_made, 1)
                    nc.vector.tensor_tensor(wt_blk[:, h, :, 0, :], blk_eq[:, h, :, :],
                                            wt_part[0][:, ds(at, UD)].unsqueeze(2).broadcast_to([P, UD, B]),
                                            ALU.mult).then_inc(high_made, 1)
            dve.wait_ge(bucket_tot, BK)
            ch.link(nc.vector.tensor_tensor_scan(cum, tot, tot, 0.0, ALU.add, ALU.max))
            nc.vector.tensor_tensor(exc, cum, tot, ALU.subtract).then_inc(totals_ready, 1)
            for c in range(NC):
                dve.wait_ge(in_x, 16 * NC)
                for b in range(c * CB, (c + 1) * CB):
                    nc.vector.bn_stats(stat6[:, b, :], X[:, b, :]).then_inc(dve_step, 1)
                    ch.n += 1
            dve.wait_ge(dve_step, ch.base + ch.n)
            for b in range(B):
                nc.vector.bn_aggr(mv[:, b, :], stat6[:, b, :]).then_inc(dve_step, 1)
                ch.n += 1
            dve.wait_ge(bases_ready, 1)
            ch.link(nc.vector.tensor_copy(base, PB[1][:, 0:BK]))
            for b in range(BK + 1):
                if b < BK:
                    nc.vector.tensor_tensor_scan(scanp[b % 2], OHB[:, b, :], OHB[:, b, :], base[:, b:b + 1],
                                                 ALU.add, ALU.max).then_inc(dve_step, 1)
                    ch.n += 1
                if b:
                    dve.wait_ge(dve_step, ch.base + ch.n - (1 if b < BK else 0))
                    ch.link(nc.vector.copy_predicated(pos1, OHB[:, b - 1, :], scanp[(b - 1) % 2]))
            nc.vector.tensor_scalar(pos_i, pos1, -1.0, None, ALU.add)
            dve.wait_ge(in_dst, 32)
            nc.vector.tensor_copy(dstf[:, :], dst_i)
            nc.vector.tensor_scalar(blkD[:, :], dst_i, 7, 20, ALU.arith_shift_right, ALU.arith_shift_left)
            ch.link(nc.vector.tensor_scalar(tmp_f, src_i, float(NP - 1), float(REL), ALU.min, ALU.mult))
            nc.vector.tensor_tensor(gidx[:, :], tmp_f, typ_i, ALU.add)
            dve.wait_ge(in_rows, 16)
            rows3 = drow_i.rearrange("p (g e) -> p g e", g=TG)
            ch.link(nc.vector.tensor_reduce(tmn, rows3, AX, ALU.min))
            ch.link(nc.vector.tensor_reduce(tmx, rows3, AX, ALU.max))
            ch.link(nc.vector.tensor_copy(tmn_i, tmn))
            ch.link(nc.vector.tensor_copy(tmx_i, tmx))
            ch.link(nc.vector.tensor_scalar(tmn_i, tmn_i, 7, None, ALU.arith_shift_right))
            ch.link(nc.vector.tensor_scalar(tmx_i, tmx_i, 7, None, ALU.arith_shift_right))
            ch.link(nc.vector.tensor_copy(tmn, tmn_i))
            ch.link(nc.vector.tensor_copy(tmx, tmx_i))
            blks = C[:, C_BLK:C_BLK + B].unsqueeze(2).broadcast_to([P, B, TG])
            ch.link(nc.vector.tensor_tensor(ge, blks, tmn.unsqueeze(1).broadcast_to([P, B, TG]), ALU.is_ge))
            ch.link(nc.vector.tensor_tensor(le, blks, tmx.unsqueeze(1).broadcast_to([P, B, TG]), ALU.is_le))
            ch.link(nc.vector.tensor_tensor(inb, ge, le, ALU.mult))
            ch.link(nc.vector.tensor_tensor(ge, inb, C[:, C_REV:C_REV + TG].unsqueeze(1).broadcast_to([P, B, TG]), ALU.mult))
            ch.link(nc.vector.tensor_tensor(le, inb, C[:, C_NEXT:C_NEXT + TG].unsqueeze(1).broadcast_to([P, B, TG]), ALU.mult))
            ch.link(nc.vector.tensor_reduce(two[:, 0, :], ge, AX, ALU.max))
            nc.vector.tensor_reduce(two[:, 1, :], le, AX, ALU.max).then_inc(ext_ready, 1)
            dve.wait_ge(ext_t, 1)
            ch.link(nc.vector.tensor_reduce(ext[:, 0:1], PB[5][0:B, 0:P], AX, ALU.max))
            nc.vector.tensor_reduce(ext[:, 1:2], PB[5][0:B, P:2 * P], AX, ALU.max).then_inc(ext2_ready, 1)
            dve.wait_ge(ext2_t, 1)
            ch.link(nc.vector.tensor_scalar(rowf[:, 0, 0:B], PB[5][0:1, 256:256 + B], -1.0, float(BIG), ALU.mult, ALU.add))
            ch.link(nc.vector.tensor_scalar(rowf[:, 0, 0:B], rowf[:, 0, 0:B], float(E // P), None, ALU.min))
            ch.link(nc.vector.tensor_tensor(rowf[:, 1, 0:B], PB[5][0:1, 384:384 + B], rowf[:, 0, 0:B], ALU.subtract))
            ch.link(nc.vector.tensor_copy(rowi[:, 0, :], PB[2][0:1, 0:BK]))
            ch.link(nc.vector.tensor_scalar(rowf[:, 4, 0:B], PB[2][0:1, 1:BK], -1.0, 0.0, ALU.add, ALU.max))
            ch.link(nc.vector.tensor_copy(rowi[:, 1, 0:B], rowf[:, 4, 0:B]))
            ch.link(nc.vector.tensor_scalar(rowi[:, 2, 0:B], rowi[:, 0, 0:B], 7, None, ALU.arith_shift_right))
            ch.link(nc.vector.tensor_scalar(rowi[:, 3, 0:B], rowi[:, 1, 0:B], 7, None, ALU.arith_shift_right))
            ch.link(nc.vector.tensor_copy(rowf[:, 2, 0:B], rowi[:, 2, 0:B]))
            ch.link(nc.vector.tensor_tensor(rowf[:, 3, 0:B], rowi[:, 3, 0:B], rowi[:, 2, 0:B], ALU.subtract))
            ch.link(nc.vector.tensor_scalar(rowf[:, 3, 0:B], rowf[:, 3, 0:B], 1.0, None, ALU.add))
            for which, at in ((DST, 0), (SRC, 2), (DST_W, 0)):
                per = PER_ROUND[which]
                first, tiles = rowf[:, at, 0:B], rowf[:, 7, 0:B]
                ch.link(nc.vector.tensor_scalar(tiles, rowf[:, at + 1, 0:B], 1.0, float(per - 1), ALU.max, ALU.add))
                ch.link(nc.vector.tensor_scalar(tiles, tiles, float(-(-65536 // per)), None, ALU.mult))
                ch.link(nc.vector.tensor_copy(rowi[:, 4, 0:B], tiles))
                ch.link(nc.vector.tensor_scalar(rowi[:, 4, 0:B], rowi[:, 4, 0:B], 16, None, ALU.arith_shift_right))
                ch.link(nc.vector.tensor_copy(rowf[:, 5, 0:B], rowi[:, 4, 0:B]))
                ch.link(nc.vector.tensor_tensor_scan(rowf[:, 6, 1:BK], rowf[:, 5, 0:B], rowf[:, 5, 0:B], 0.0,
                                                     ALU.add, ALU.max))
                nc.vector.memset(rowf[:, 6, 0:1], 0.0)
                ch.link(nc.vector.tensor_copy(rowi[:, 5, 0:B], first))
                entry = tab[0:1, BK * which:BK * (which + 1)]
                ch.link(nc.vector.tensor_copy(entry, rowf[:, 6, :]))
                ch.link(nc.vector.tensor_scalar(entry, entry, BEFORE_AT, None, ALU.arith_shift_left))
                ch.link(nc.vector.tensor_scalar(rowi[:, 4, 0:B], rowi[:, 4, 0:B], ROUNDS_AT, None,
                                                ALU.arith_shift_left))
                ch.link(nc.vector.tensor_tensor(entry[:, 0:B], entry[:, 0:B], rowi[:, 4, 0:B], ALU.bitwise_or))
                ch.link(nc.vector.tensor_tensor(entry[:, 0:B], entry[:, 0:B], rowi[:, 5, 0:B], ALU.bitwise_or))
            dve.wait_ge(deg_ready, 1)
            ch.link(nc.vector.tensor_scalar(sc2[:, :], PB[0][:, 0:B], 1.0, None, ALU.add))
            for a in (1, 2):
                ch.link(nc.vector.tensor_tensor(sc2[:, :], sc2[:, :], PB[0][:, a * B:(a + 1) * B], ALU.add))
            ch.link(nc.vector.tensor_scalar(sc1[:, :], sc2[:, :], 1e-30, None, ALU.max))
            nc.vector.tensor_scalar(rstd[:, :], mv[:, :, 1], EPS, None, ALU.add).then_inc(root_in, 1)
            ch.link(nc.vector.tensor_scalar(sc2[:, :], sc2[:, :], 0.0, None, ALU.is_gt))
            dve.wait_ge(root_out, 1)
            ch.link(nc.vector.reciprocal(sc1[:, :], sc1[:, :]))
            ch.link(nc.vector.tensor_tensor(dinv[:, :], sc1[:, :], sc2[:, :], ALU.mult))
            ch.link(nc.vector.reciprocal(rstd[:, :], rstd[:, :]))
            ch.link(nc.vector.tensor_tensor(sc1[:, :], rstd[:, :], dinv[:, :], ALU.mult))
            ch.link(nc.vector.scalar_tensor_tensor(sc2[:, :], mv[:, :, 0], -1.0, sc1[:, :], ALU.mult, ALU.mult))
            dve.sem_inc(xs_begun, 1)
            for b in range(B // 2):
                nc.vector.tensor_scalar(XS[:, b, :], X[:, b, :], sc1[:, b:b + 1], sc2[:, b:b + 1], ALU.mult, ALU.add)
            nc.vector.tensor_tensor(rstd[:, :], sc1[:, :], dinv[:, :], ALU.mult)
            nc.vector.tensor_tensor(nmr[:, :], sc2[:, :], dinv[:, :], ALU.mult)
            nc.vector.memset(junk[:, 0:1], 0.0).then_inc(scales_ready, 1)
            phase_end(dve)
            nc.vector.memset(msg[:, :, :, D + 1:ROW], 0.0)
            for half, (first_b, end_b) in enumerate(HALVES):
                start = rounds_before(dve, DST, first_b)
                with dve.Fori(first_b, end_b) as b:
                    lo, rounds, before = block_row(dve, DST, b)
                    with dve.Fori(0, rounds) as j:
                        t0, n, dmas = this_round(dve, DST, lo, before, j, start)
                        for u in range(U):
                            dve.wait_ge(dst_in[half][u // UH], dmas + 16)
                            dve.wait_ge(exp_done, n + u + 1)
                            nc.vector.tensor_scalar(oneh[:, u, :], dst_bc[:, u, :], C[:, ds(b + C_NODE, 1)], None,
                                                    ALU.is_equal).then_inc(oht_made, 1)
                            dve.wait_ge(scattered[half][u], dmas + 16)
                            nc.vector.scalar_tensor_tensor(
                                slot_idx(half, u).bitcast(i32), blkD[:, ds(t0 + u, 1)], blk_shift[:, ds(b, 1)],
                                pos_i[:, ds(t0 + u, 1)], ALU.bitwise_xor, ALU.bitwise_or).then_inc(idx_made, 1)
            phase_end(dve)
            def one_hots0(b, n, dmas, k):
                dve.wait_ge(row_in[k], dmas + 16)
                for u in range(UG * k, UG * (k + 1)):
                    dve.wait_ge(row_used, n + u + 1)
                    nc.vector.tensor_scalar(oneh_w[:, u, :], iota, back[:, u, D:D + 1], C[:, ds(b + C_NEG, 1)],
                                            ALU.subtract, ALU.is_equal).then_inc(oh_made, 1)

            def add_sums0(b, rounds_before):
                dve.wait_ge(row_used, rounds_before * UW + 2 * UW)
                dve.wait_ge(agg_begun, b + 1)
                dve.wait_ge(agg_added, rounds_before + 1)
                nc.vector.scalar_tensor_tensor(
                    agg_in.unsqueeze(1), PS[:, ds(b % 2, 1), 0:D], dinv[:, ds(b, 1)], agg_in.unsqueeze(1),
                    ALU.mult, ALU.add).then_inc(agg_added, 1)

            def more_rounds0(b, rounds, before):
                with dve.If(rounds > 1):
                    with dve.Fori(1, rounds) as j:
                        add_sums0(b, before + j - 1)
                        for k in range(UW // UG):
                            one_hots0(b, dve.snap((before + j) * UW), dve.snap((before + j) * 16), k)

            def head_sum(b):
                dve.wait_ge(head_y, b + 1)
                nc.vector.tensor_tensor(X[:, ds(b, 1), :], X[:, ds(b, 1), :], PB[3][:, 0:D],
                                        ALU.add).then_inc(head_added, 1)
                dve.wait_ge(head_added, b + 2)
                ch.pause()
                ch.link(nc.vector.bn_stats(stat0, X[:, ds(b, 1), :]))
                ch.pause()
                ch.link(nc.vector.bn_aggr(mv0, stat0))
                nc.vector.tensor_scalar(var0, mv0[:, 1:2], EPS, None, ALU.add).then_inc(var0_made, 1)

            def head_norm(b):
                dve.wait_ge(rstd0_made, b + 1)
                dve.wait_ge(norm0_added, b)
                nc.vector.tensor_scalar(x_norm0.unsqueeze(1), X[:, ds(b, 1), :], mv0[:, 0:1], rstd0, ALU.subtract,
                                        ALU.mult).then_inc(norm0_made, 1)

            def route0_max(b):
                dve.wait_ge(logits0, b + 1)
                ch.link(nc.vector.tensor_reduce(neg_max0, PB[5][:, 0:8], AX, ALU.max))
                nc.vector.tensor_scalar(neg_max0, neg_max0, -1.0, None, ALU.mult).then_inc(max0_made, 1)

            def route0_gates(b):
                dve.wait_ge(probs0_made, b + 1)
                ch.link(nc.vector.reciprocal(prob_sum0, prob_sum0))
                ch.link(nc.vector.tensor_scalar(prob0, prob0, prob_sum0, None, ALU.mult))
                ch.pause()
                ch.link(nc.vector.max(top0, prob0))
                ch.link(nc.vector.tensor_tensor(gate_sum0, top0[:, 0:1], top0[:, 1:2], ALU.add))
                ch.pause()
                nc.vector.max_index(top0_i, top0, prob0)
                ch.link(nc.vector.tensor_scalar(gate_sum0, gate_sum0, 1e-12, None, ALU.max))
                nc.vector.tensor_copy(top0_f, top0_i)
                ch.link(nc.vector.reciprocal(gate_sum0, gate_sum0))
                ch.link(nc.vector.tensor_scalar(gates0, top0[:, 0:2], gate_sum0, None, ALU.mult))
                nc.vector.tensor_scalar(eq0_a, e8, top0_f[:, 0:1], gates0[:, 0:1], ALU.is_equal, ALU.mult)
                ch.link(nc.vector.tensor_scalar(eq0_b, e8, top0_f[:, 1:2], gates0[:, 1:2], ALU.is_equal, ALU.mult))
                nc.vector.tensor_tensor(comb0, eq0_a, eq0_b, ALU.add).then_inc(comb0_ready, 1)
                nc.vector.tensor_tensor(comb[:, ds(b, 1), :], eq0_a.unsqueeze(1), eq0_b.unsqueeze(1), ALU.add)

            def route0_turned(b):
                dve.wait_ge(comb0_t, b + 1)
                nc.vector.tensor_copy(comb0_s, PB[4][0:8, 0:P]).then_inc(comb0_moved, 1)

            def route0_bias(b):
                dve.wait_ge(norm0_added, b + 1)
                dve.wait_ge(bias0_mm, b + 1)
                nc.vector.tensor_tensor(X[:, ds(b, 1), :], X[:, ds(b, 1), :], PB[5][:, 0:D],
                                        ALU.add).then_inc(bias0_added, 1)

            def step(b, head, route, last=False, row=None, next_b=None):
                loaded = None
                if b is not None:
                    lo, rounds, before = row or block_row(dve, SRC, b)
                    n, dmas = dve.snap(before * UW), dve.snap(before * 16)
                    one_hots0(b, n, dmas, 1)
                if route is not None:
                    route0_max(route)
                if b is not None:
                    one_hots0(b, n, dmas, 2)
                if route is not None:
                    route0_gates(route)
                if head is not None:
                    head_sum(head)
                if route is not None:
                    route0_turned(route)
                if b is not None:
                    more_rounds0(b, rounds, before)
                    if not last:
                        one_hots0(b + 1, dve.snap((before + rounds) * UW), dve.snap((before + rounds) * 16), 0)
                if next_b is not None:
                    loaded = block_row(dve, SRC, next_b)
                if head is not None:
                    head_norm(head)
                if route is not None:
                    route0_bias(route)
                if b is not None:
                    add_sums0(b, before + rounds - 1)
                    dve.wait_ge(agg_added, before + rounds + 1)
                    dve.sem_inc(agg_ready, 1)
                return loaded

            e8 = C[:, C_I8:C_I8 + 8]
            nc.vector.memset(power0, -0.5)
            one_hots0(0, 0, 0, 0)
            step(0, None, None)
            step(1, 0, None)
            with dve.Fori(0, (B - 3) // 2) as pair:
                ch.loop(pair, 22)
                i = dve.snap(pair * 2)
                row = step(dve.snap(i + 2), dve.snap(i + 1), i, next_b=dve.snap(i + 3))
                step(dve.snap(i + 3), dve.snap(i + 2), dve.snap(i + 1), row=row)
            ch.loop_end((B - 3) // 2)
            step(B - 1, B - 2, B - 3, last=True)
            step(None, B - 1, B - 2)
            step(None, None, B - 1)
            phase_end(dve)

            def statistics():
                for b in range(B):
                    nc.vector.bn_aggr(mv[:, b, :], stat6[:, b, :]).then_inc(dve_step, 1)
                    ch.n += 1
                dve.wait_ge(dve_step, ch.base + ch.n)
                nc.vector.tensor_scalar(rstd[:, :], mv[:, :, 1], EPS, None, ALU.add).then_inc(root_in, 1)
                dve.wait_ge(root_out, 2)
                ch.link(nc.vector.reciprocal(rstd[:, :], rstd[:, :]))
                nc.vector.scalar_tensor_tensor(nmr[:, :], mv[:, :, 0], -1.0, rstd[:, :], ALU.mult,
                                               ALU.mult).then_inc(scales_ready, 1)

            def move_blocks():
                with dve.Fori(0, NC) as c:
                    for s in range(CB):
                        dve.wait_ge(turned, c * CB + s + 1)
                        nc.vector.tensor_copy(xts[:, s, :, :], turn_bank(s)).then_inc(slot_moved, 1)
                        if s:
                            pairs(c, s - 1)
                    pairs(c, CB - 1)

            def pairs(c, s):
                dve.wait_ge(hx_freed, c * CB + s + (2 if s == 0 else 1))
                for q in (1, 3):
                    dve.wait_ge(pair_mm, c * (4 * CB) + 4 * s + q + 1)
                    nc.vector.tensor_copy(hxs[:, s % 2, q * 512:(q + 1) * 512], PB[2 + q][:, :]).then_inc(pair_dve, 1)
                dve.wait_ge(loop_mm, c * CB + s + 1)
                nc.vector.scalar_tensor_tensor(X[:, ds(c * CB + s, 1), :], PB[6 + s % 2][:, 0:D], SQH,
                                               X[:, ds(c * CB + s, 1), :], ALU.mult, ALU.add).then_inc(loop_added, 1)

            def add_experts(n, made, added):
                with dve.Fori(0, NC) as c:
                    for e in range(n):
                        for i in range(CB):
                            m = c * (n * CB) + e * CB + i
                            dve.wait_ge(made, m + 1)
                            if e:
                                dve.wait_ge(added, m - CB + 1 + 4)
                            nc.vector.scalar_tensor_tensor(
                                X[:, ds(c * CB + i, 1), :], PB[4 + (e * CB + i) % 4][:, 0:D],
                                comb[:, ds(c * CB + i, 1), e:e + 1], X[:, ds(c * CB + i, 1), :],
                                ALU.mult, ALU.add).then_inc(added, 1)
                    dve.wait_ge(added, c * (n * CB) + (n * CB + 4))
                    ch.pause()
                    for i in range(CB):
                        nc.vector.bn_stats(stat6[:, ds(c * CB + i, 1), :], X[:, ds(c * CB + i, 1), :])

            add_experts(R0, y_mm, y_added)
            phase_end(dve)
            statistics()
            move_blocks()
            dve.wait_ge(in_small, 128)
            dve.wait_ge(loop_added, B + 1)
            nc.vector.tensor_tensor(X[:, :, :], X[:, :, :], HB[:, :].unsqueeze(1).broadcast_to([P, B, D]), ALU.add)
            phase_end(dve)
            nc.vector.memset(prob, -1.0)

            def one_hots(b, t0, n, us):
                for u in us:
                    dve.wait_ge(row2_used, n + u + 1)
                    nc.vector.tensor_scalar(oneh_l[:, u, :], iota, dstf[:, ds(t0 + u, 1)],
                                            C[:, ds(b + C_NEG, 1)], ALU.subtract,
                                            ALU.is_equal).then_inc(oh2_made, 1)

            def add_sums(b, before, n):
                dve.wait_ge(row2_used, n + 2 * UW)
                nc.vector.scalar_tensor_tensor(
                    X[:, ds(b, 1), :], PB[0][:, 0:D], SQH, X[:, ds(b, 1), :],
                    ALU.mult, ALU.add).then_inc(agg2_added, 1)
                dve.wait_ge(agg2_added, before + 2)

            class Edges:

                def __init__(self, b):
                    self.b = b
                    self.lo, self.rounds, self.before = block_row(dve, DST_W, b)
                    self.t0, self.n, _ = this_round(dve, DST_W, self.lo, self.before, 0)

                def part(self, k):
                    one_hots(self.b, self.t0, self.n, range(UG * k, UG * (k + 1)))

                def rest(self):
                    add_sums(self.b, self.before, self.n)
                    with dve.If(self.rounds > 1):
                        with dve.Fori(1, self.rounds) as j:
                            t0, n, _ = this_round(dve, DST_W, self.lo, self.before, j)
                            one_hots(self.b, t0, n, range(UW))
                            add_sums(self.b, self.before + j, n)

            def scales(b):
                ch.link(nc.vector.bn_stats(stat1, X[:, ds(b, 1), :]))
                ch.pause()
                ch.link(nc.vector.bn_aggr(mv1, stat1))
                ch.link(nc.vector.tensor_scalar(var1, mv1[:, 1:2], EPS, None, ALU.add))
                nc.vector.tensor_scalar(minus_half, var1, -0.5, None, ALU.mult)
                ch.link(nc.vector.tensor_scalar(half_bits.bitcast(i32), var1.bitcast(i32), 1, None,
                                                ALU.arith_shift_right))
                ch.link(nc.vector.tensor_scalar(rstd1.bitcast(i32), half_bits.bitcast(i32), -1.0,
                                                float(0x5F3759DF), ALU.mult, ALU.add))
                for _ in range(3):
                    ch.link(nc.vector.scalar_tensor_tensor(newton, rstd1, rstd1, minus_half, ALU.mult, ALU.mult))
                    ch.link(nc.vector.scalar_tensor_tensor(rstd1, newton, 1.5, rstd1, ALU.add, ALU.mult))
                nc.vector.scalar_tensor_tensor(nmr1, mv1[:, 0:1], -1.0, rstd1, ALU.mult,
                                               ALU.mult).then_inc(scales1, 1)

            def route_max(b):
                dve.wait_ge(logits1, b + 1)
                ch.link(nc.vector.tensor_reduce(neg_max, PB[1][:, 0:E1], AX, ALU.max))
                nc.vector.tensor_scalar(neg_max, neg_max, -1.0, None, ALU.mult).then_inc(max_made, 1)

            def route_top(b):
                dve.wait_ge(probs_made, b + 1)
                ch.link(nc.vector.reciprocal(prob_sum, prob_sum))
                ch.link(nc.vector.tensor_scalar(prob[:, 0:E1], prob[:, 0:E1], prob_sum, None, ALU.mult))
                ch.pause()
                ch.link(nc.vector.max(top1, prob))
                nc.vector.tensor_scalar(neg_top, top1[:, 0:1], -1.0, None, ALU.mult).then_inc(tops_made, 1)
                ch.link(nc.vector.max_index(top1_i, top1, prob))
                ch.link(nc.vector.tensor_copy(top1_f, top1_i))

            def route_gates(b):
                dve.wait_ge(gates_made, b + 1)
                ch.link(nc.vector.reciprocal(gate_sum, gate_sum))
                ch.link(nc.vector.tensor_scalar(gates, gates, gate_sum, None, ALU.mult))
                ch.link(nc.vector.tensor_scalar(eq_a, e8, top1_f[:, 0:1], gates[:, 0:1], ALU.is_equal, ALU.mult))
                ch.link(nc.vector.tensor_scalar(eq_b, e8, top1_f[:, 1:2], gates[:, 1:2], ALU.is_equal, ALU.mult))
                nc.vector.tensor_tensor(comb1, eq_a, eq_b, ALU.add).then_inc(comb1_ready, 1)
                ch.link(nc.vector.tensor_tensor(comb[:, ds(b, 1), :], eq_a.unsqueeze(1), eq_b.unsqueeze(1), ALU.add))

            def route_turned(b):
                dve.wait_ge(comb1_t, b + 1)
                nc.vector.tensor_copy(comb1_s, PB[2][0:8, 0:P]).then_inc(comb1_moved, 1)

            def route_bias(b):
                dve.wait_ge(bias1_mm, b + 1)
                nc.vector.tensor_tensor(X[:, ds(b, 1), :], X[:, ds(b, 1), :], PB[1][:, 0:D],
                                        ALU.add).then_inc(bias1_added, 1)

            def add_expert(b, e):
                dve.wait_ge(y1_mm, b * E1 + e + 1)
                if e:
                    dve.wait_ge(y1_added, b * E1 + e + 2)
                else:
                    dve.wait_ge(bias1_added, b + 2)
                nc.vector.scalar_tensor_tensor(
                    X[:, ds(b, 1), :], PB[6 + e % 2][:, 0:D], comb[:, ds(b, 1), e:e + 1],
                    X[:, ds(b, 1), :], ALU.mult, ALU.add).then_inc(y1_added, 1)

            ORDER = (route_turned, scales, route_bias, 0, "0", 1, "1", 2, route_max, 3, "2", route_top, 4, 5,
                     route_gates)

            def layer1(before, b, after):
                edges = None
                for part in ORDER:
                    if isinstance(part, int):
                        if before is not None:
                            add_expert(before, part)
                    elif isinstance(part, str):
                        if after is not None:
                            edges = edges or Edges(after)
                            edges.part(int(part))
                    elif part in (route_turned, route_bias):
                        if before is not None:
                            part(before)
                    elif b is not None:
                        part(b)
                if edges:
                    edges.rest()

            first = Edges(0)
            for k in range(UW // UG):
                first.part(k)
            first.rest()
            layer1(None, 0, 1)
            links = 22
            with dve.Fori(0, B - 2) as i:
                ch.loop(i, links)
                layer1(i, dve.snap(i + 1), dve.snap(i + 2))
            ch.loop_end(B - 2)
            layer1(B - 2, B - 1, None)
            layer1(B - 1, None, None)

        @block.tensor
        def _(pe):
            pe.wait_ge(in_const, 48)
            pe.matmul(PB[0][:, 0:3 * B], zeros[:, 0:P], zeros[:, 0:3 * B], start=True, stop=False, skip_group_check=True)
            with pe.Fori(0, T // (2 * UD)) as i:
                for h in range(2):
                    for made in (lo_made, lo_made_act, high_made, low_made):
                        pe.wait_ge(made, i * 2 + h + (2 if made is lo_made else 1))
                    for s in range(UD):
                        mm = pe.matmul(PB[0][:, 0:3 * B], lo_eq[:, h, s, :],
                                       wt_blk[:, h, s, :, :].rearrange("p a n -> p (a n)"),
                                       start=False, stop=False, skip_group_check=True)
                    mm.then_inc(used, 1)
            pe.matmul(PB[0][:, 0:3 * B], zeros[:, 0:P], zeros[:, 0:3 * B], start=False, stop=True,
                      skip_group_check=True).then_inc(deg_ready, 1)
            pe.wait_ge(totals_ready, 1)
            pe.matmul(PB[2][:, 0:BK], ones, exc, start=True, stop=True)
            pe.matmul(PB[1][:, 0:BK], ones, exc, start=True, stop=False)
            pe.matmul(PB[1][:, 0:BK], tri, tot, start=False, stop=True).then_inc(bases_ready, 1)
            pe.wait_ge(ext_ready, 1)
            pe.transpose(PB[5][0:B, 0:P], two[:, 0, :], ident)
            pe.transpose(PB[5][0:B, P:2 * P], two[:, 1, :], ident).then_inc(ext_t, 1)
            pe.wait_ge(ext2_ready, 1)
            pe.transpose(PB[5][0:1, 256:256 + B], ext[:, 0:1], ident[0:B, 0:B])
            pe.transpose(PB[5][0:1, 384:384 + B], ext[:, 1:2], ident[0:B, 0:B]).then_inc(ext2_t, 1)
            phase_end(pe)
            with pe.Fori(0, B) as b:
                lo, rounds, before = block_row(pe, DST, b)
                with pe.Fori(0, rounds) as j:
                    t0, n, dmas = this_round(pe, DST, lo, before, j)
                    for u in range(U):
                        pe.wait_ge(oht_made, n + U + u + 1)
                        pe.wait_ge(msg_made, n + u + 1)
                        pe.matmul(PB[u][:, 0:D], oneh[:, u, :], XS[:, ds(b, 1), :], start=True,
                                  stop=True).then_inc(exp_done, 1)
            phase_end(pe)
            def layer(weight, m, of, at, n, to, signal):
                for k in range(2):
                    moving = of[:, k, at:at + n] if isinstance(at, int) else of[:, k, ds(at, n)]
                    mm = pe.matmul(to[:, 0:n], weight[:, k, m * P:(m + 1) * P], moving,
                                   start=(k == 0), stop=(k == 1))
                mm.then_inc(signal, 1)

            pe.wait_ge(in_gw, 64)
            pe.wait_ge(in_small, 128)
            gw = [GW[:, 512 * i:512 * (i + 1)].rearrange("p (k o) -> p k o", k=2) for i in range(4)]

            def sum_round(b, n, after):
                for u in range(UW):
                    pe.wait_ge(oh_made, n + u + 1)
                    pe.matmul(PS[:, ds(b % 2, 1), 0:D], oneh_w[:, u, :], back[:, u, 0:D], start=(u == 0),
                              stop=(u == UW - 1)).then_inc(row_used, 1)
                    for stage in after.get(u, ()):
                        stage()

            def head_turn(b):
                pe.wait_ge(agg_ready, b + 3)
                for k in range(2):
                    mm = pe.transpose(PB[2][:, k * P:(k + 1) * P], agg_in[:, k * P:(k + 1) * P], ident)
                mm.then_inc(agg_turned, 1)

            def head_layer(b, ready, w, of, bank, signal):
                pe.wait_ge(ready, b + 1)
                pe.wait_ge(head_added, b + 1)
                for m in range(2):
                    for k in range(2):
                        mm = pe.matmul(PB[bank][:, m * P:(m + 1) * P], w[:, k, m * P:(m + 1) * P], of[:, k, :],
                                       start=(k == 0), stop=(k == 1))
                mm.then_inc(signal, 1)

            def head_out(b):
                pe.wait_ge(hid0_made, b + 1)
                for k in range(2):
                    pe.matmul(PB[3][:, 0:D], hid_t[:, k, :], gw[2][:, k, :], start=(k == 0), stop=False)
                pe.matmul(PB[3][:, 0:D], ones[0:1, :], srow[:, 0:D], start=False, stop=True).then_inc(head_y, 1)

            def route_turn(b):
                pe.wait_ge(norm0_made, b + 1)
                for k in range(2):
                    mm = pe.transpose(PB[4][:, k * P:(k + 1) * P], x_norm0[:, k * P:(k + 1) * P], ident)
                mm.then_inc(turned0, 1)

            def route_logits(b):
                pe.wait_ge(xt0_made, b + 1)
                pe.wait_ge(bias0_added, b + 1)
                for k in range(2):
                    mm = pe.matmul(PB[5][:, 0:8], xt0[:, k, :], RW[:, k, :], start=(k == 0), stop=(k == 1))
                mm.then_inc(logits0, 1)

            def route_comb(b):
                pe.wait_ge(comb0_ready, b + 1)
                pe.transpose(PB[4][0:8, 0:P], comb0, ident).then_inc(comb0_t, 1)

            def route_bias(b):
                pe.wait_ge(comb0_moved, b + 1)
                pe.matmul(PB[5][:, 0:D], comb0_s, brow[:, 0:D], start=True, stop=True).then_inc(bias0_mm, 1)

            def step(b, head, route, row=None, next_b=None):
                after, loaded = {}, []
                if next_b is not None:
                    after[9] = [lambda: loaded.append(block_row(pe, SRC, next_b))]
                if head is not None:
                    after[2] = [lambda: head_turn(head)]
                    after[4] = [lambda: head_layer(head, agg_t_made, gw[0], agg_t, 3, mid_mm)]
                    after[8] = [lambda: head_layer(head, mid_made, gw[1], mid_t, 2, hid0_mm)]
                    after[11] = [lambda: head_out(head)]
                if route is not None:
                    after[3] = [lambda: route_turn(route)]
                    after[5] = [lambda: route_logits(route)]
                    after[13] = [lambda: route_comb(route)]
                    after[16] = [lambda: route_bias(route)]
                if b is None:
                    for u in sorted(after):
                        for stage in after[u]:
                            stage()
                    return
                lo, rounds, before = row or block_row(pe, SRC, b)
                pe.wait_ge(agg_ready, b + 1)
                sum_round(b, pe.snap(before * UW), after)
                with pe.If(rounds > 1):
                    with pe.Fori(1, rounds) as j:
                        pe.wait_ge(agg_added, before + j + 1)
                        sum_round(b, pe.snap((before + j) * UW), {})
                return loaded[0] if loaded else None

            step(0, None, None)
            step(1, 0, None)
            with pe.Fori(0, (B - 3) // 2) as pair:
                i = pe.snap(pair * 2)
                row = step(pe.snap(i + 2), pe.snap(i + 1), i, next_b=pe.snap(i + 3))
                step(pe.snap(i + 3), pe.snap(i + 2), pe.snap(i + 1), row)
            step(B - 1, B - 2, B - 3)
            step(None, B - 1, B - 2)
            step(None, None, B - 1)
            phase_end(pe)

            def turn(after):
                with pe.Fori(0, NC) as c:
                    for s in range(CB):
                        pe.wait_ge(norm_made, c * CB + s + 1)
                        pe.wait_ge(slot_moved, c * CB + s + (3 if s == 0 else 2))
                        for h in range(2):
                            mm = pe.transpose(turn_bank(s)[:, h, :], xn[:, s % 4, h * P:(h + 1) * P], ident)
                        mm.then_inc(turned, 1)
                        if s:
                            after(c, s - 1)
                    after(c, CB - 1)

            def relations(c, s):
                pe.wait_ge(slot_moved, c * CB + s + 4)
                for q in range(4):
                    pe.wait_ge((pair_act, pair_dve)[q % 2], c * (2 * CB) + 2 * s + q // 2 + 1)
                    for k in range(2):
                        mm = pe.matmul(PB[2 + q][:, :], xts[:, s, k, :], WR[:, k, 512 * q:512 * (q + 1)],
                                       start=(k == 0), stop=(k == 1))
                    mm.then_inc(pair_mm, 1)
                pe.wait_ge(loop_added, c * CB + s + 1)
                for k in range(2):
                    mm = pe.matmul(PB[6 + s % 2][:, 0:D], xts[:, s, k, :], gw[3][:, k, :],
                                   start=(k == 0), stop=(k == 1))
                mm.then_inc(loop_mm, 1)

            pe.wait_ge(in_w0, 16 * 2 * R0)
            with pe.Fori(0, NC) as c:
                def hidden(e):
                    for q in range(4):
                        pe.wait_ge(hid_moved, c * (4 * R0) + 4 * e + q + 1)
                        layer(W0[:, e, 0, :, :], q % 2, XT, c * CN + q // 2 * HN, HN, PB[q], hid_mm)

                hidden(0)
                for e in range(R0):
                    if e + 1 < R0:
                        hidden(e + 1)
                    pe.wait_ge(hid_moved, c * (4 * R0) + 4 * e + 8)
                    for i in range(CB):
                        pe.wait_ge(y_added, c * (R0 * CB) + e * CB + i + 1)
                        for k in range(2):
                            mm = pe.matmul(PB[4 + (e * CB + i) % 4][:, 0:D], HT[e % 2][:, k, i * P:(i + 1) * P],
                                           W0[:, e, 1, k, :], start=(k == 0), stop=(k == 1))
                        mm.then_inc(y_mm, 1)
            phase_end(pe)
            pe.wait_ge(in_wr, 16 * REL)
            turn(relations)
            phase_end(pe)
            def row_of(b):
                return (b,) + block_row(pe, DST_W, b) if b is not None else None

            def edge_sums(row):
                b, lo, rounds, before = row

                def one_round(j):
                    t0, n, dmas = this_round(pe, DST_W, lo, before, j)
                    pe.wait_ge(agg2_added, before + j + 1)
                    for u in range(UW):
                        pe.wait_ge(oh2_made, n + u + 1)
                        pe.wait_ge(got[u], dmas + 16)
                        pe.matmul(PB[0][:, 0:D], oneh_l[:, u, :], rows_in[:, u, :], start=(u == 0),
                                  stop=(u == UW - 1)).then_inc(row2_used, 1)

                one_round(0)
                with pe.If(rounds > 1):
                    with pe.Fori(1, rounds) as j:
                        one_round(j)

            def turned_half(b, k):
                return x_turned[:, ds(b % 2 * D + k * P, P)]

            def turn1(b):
                pe.wait_ge(norm1_made, b + 1)
                pe.wait_ge(bias1_added, b + 1)
                for k in range(2):
                    mm = pe.transpose(PB[1][:, k * P:(k + 1) * P], x_norm[:, k * P:(k + 1) * P], ident)
                mm.then_inc(turned1, 1)

            def router1(b):
                pe.wait_ge(turned1_moved, b + 1)
                for k in range(2):
                    mm = pe.matmul(PB[2][:, 0:P], RW1[:, k, :], turned_half(b, k), start=(k == 0), stop=(k == 1))
                mm.then_inc(rh_mm, 1)

            def router2(b):
                pe.wait_ge(rh_moved, b + 1)
                pe.matmul(PB[1][:, 0:E1], router_h, RW2[:, :], start=True, stop=False)
                pe.matmul(PB[1][:, 0:E1], ones[0:1, :], srow[:, D:D + E1], start=False, stop=True).then_inc(logits1, 1)

            def comb_turn(b):
                pe.wait_ge(comb1_ready, b + 1)
                pe.transpose(PB[2][0:8, 0:P], comb1, ident).then_inc(comb1_t, 1)

            def bias1(b):
                pe.wait_ge(comb1_moved, b + 1)
                pe.matmul(PB[1][:, 0:D], comb1_s, brow[:, D:2 * D], start=True, stop=True).then_inc(bias1_mm, 1)

            def output1(b, e):
                pe.wait_ge(hid1_moved, b * (4 * E1) + 2 * HIDDEN1.index((1, e)) + 5)
                pe.wait_ge(y1_added, b * E1 + e + 1)
                for k in range(2):
                    mm = pe.matmul(PB[6 + e % 2][:, 0:D], H2[:, e % 2, k, :], W1[:, e, 2, k, :],
                                   start=(k == 0), stop=(k == 1))
                mm.then_inc(y1_mm, 1)

            def experts1(before, b, after):
                comb_turn(before)
                for at, (part, e) in enumerate(HIDDEN1):
                    if at == PE_BIAS:
                        bias1(before)
                    if part == 1:
                        pe.wait_ge(hid1_moved, before * (4 * E1) + 2 * HIDDEN1.index((0, e)) + 5)
                    for m in range(2):
                        i = 2 * at + m
                        pe.wait_ge(hid1_moved, before * (4 * E1) + i + 1)
                        for k in range(2):
                            mm = pe.matmul(PB[3 + i % 3][:, 0:P], W1[:, e, part, k, m * P:(m + 1) * P],
                                           H1[:, e % 2, k, :] if part else turned_half(before, k),
                                           start=(k == 0), stop=(k == 1))
                        mm.then_inc(hid1_mm, 1)
                    if part == 1 and e:
                        output1(before, e - 1)
                    if b is not None:
                        for where, stage in ((PE_TURN, turn1), (PE_HIDDEN, router1), (PE_LOGITS, router2)):
                            if at == where:
                                stage(b)
                row = row_of(after)
                output1(before, E1 - 1)
                if row:
                    edge_sums(row)

            edge_sums(row_of(0))
            for stage in (turn1, router1, router2):
                stage(0)
            edge_sums(row_of(1))
            pe.wait_ge(in_w1, 16 * 3 * E1)
            with pe.Fori(0, B - 2) as i:
                experts1(i, pe.snap(i + 1), pe.snap(i + 2))
            experts1(B - 2, B - 1, None)
            experts1(B - 1, None, None)


_OUT = (N, D)


def _lay_out(a):
    import numpy as np

    def tiles(v, pad):
        v = np.concatenate([v, np.full(T * P - E, pad, v.dtype)])
        return np.ascontiguousarray(v.reshape(T, P).T)

    def cols(*vs):
        return np.concatenate([v.reshape(-1, P).T for v in vs], axis=1)

    a = {k: np.asarray(v) for k, v in a.items()}
    consts = np.zeros((P, C_N), np.float32)
    p = np.arange(P)
    consts[:, C_IOTA:C_IOTA + P] = p[None]
    consts[:, C_ID:C_ID + P] = np.eye(P)
    consts[:, C_TRI:C_TRI + P] = p[:, None] < p[None]
    consts[:, C_ONE:C_ONE + P] = 1
    consts[:, C_NODE:C_NODE + B] = p[:, None] + P * np.arange(B)[None]
    consts[:, C_NEG:C_NEG + BK] = -P * np.arange(BK)[None]
    consts[:, C_BLK:C_BLK + BK] = np.arange(BK)[None]
    consts[:, C_I8:C_I8 + 8] = np.arange(8)[None]
    tile = p[:, None] + P * np.arange(TG)[None]
    consts[:, C_REV:C_REV + TG] = BIG - tile
    consts[:, C_NEXT:C_NEXT + TG] = tile + 1
    dst, src = a["dst"].astype(np.int32, copy=False), a["src"].astype(np.int32, copy=False)
    return {
        "x": np.concatenate([a["x"], np.zeros((NP - N, D), np.float32)]),
        "src_t": tiles(src, NP),
        "dst_t": tiles(dst, NP),
        "type_t": tiles(a["edge_type_8"], 0),
        "weight_t": tiles(a["edge_weight"], 0),
        "dst_rows": np.concatenate([dst, np.full(TG * P * P - E, NP, dst.dtype)]).reshape(TG * P, P),
        "consts": consts,
        "shifted": np.broadcast_to(np.arange(BK, dtype=np.int32) << 20, (P, BK)).copy(),
        "bias_cols": np.ascontiguousarray(cols(
            a["L0_gnn_b"], a["L0_gnn_b1"], a["L0_ffn_b1"], a["L1_ffn_router_b1"], a["L1_ffn_expert_b1"],
            a["L1_ffn_expert_b2"])),
        "gnn_w": a["L0_gnn_W"], "gnn_w1": a["L0_gnn_W1"], "gnn_w2": a["L0_gnn_W2"],
        "gnn_b2": a["L0_gnn_b2"].reshape(1, D),
        "f0_router": np.ascontiguousarray(a["L0_ffn_router_w"].T), "f0_w1": a["L0_ffn_w1"],
        "f0_w2": a["L0_ffn_w2"], "f0_b2": a["L0_ffn_b2"],
        "rel_w": a["L1_gnn_weight"], "loop_w": a["L1_gnn_loop_weight"],
        "h_bias": a["L1_gnn_h_bias"].reshape(1, D),
        "f1_rw1": a["L1_ffn_router_w1"], "f1_rw2": a["L1_ffn_router_w2"],
        "f1_rb2": a["L1_ffn_router_b2"].reshape(1, E1), "f1_w1": a["L1_ffn_expert_w1"],
        "f1_w2": a["L1_ffn_expert_w2"], "f1_w3": a["L1_ffn_expert_w3"], "f1_b3": a["L1_ffn_expert_b3"],
    }


def kernel(**inputs):
    import concourse.bacc as bacc
    from concourse.bass_utils import run_bass_kernel_spmd

    nc = bacc.Bacc("TRN2", target_bir_lowering=False, num_devices=1)
    arrays = {f"in_{k}": v for k, v in _lay_out(inputs).items()}
    args = {k[3:]: nc.dram_tensor(k, v.shape, mybir.dt.from_np(v.dtype), kind="ExternalInput").ap()
            for k, v in arrays.items()}
    out = nc.dram_tensor("out", _OUT, f32, kind="ExternalOutput").ap()
    build(nc, out=out, **args)
    r = run_bass_kernel_spmd(nc, [arrays], core_ids=[0])
    return r.results[0]["out"]
```
